# Optimizing a Trainium2 kernel written in Bass

```python
import numpy as np
import jax
import jax.numpy as jnp

def _softmax(x, axis=-1):
    return jax.nn.softmax(x, axis=axis)

def _gelu(x):
    return jax.nn.gelu(x, approximate=True)

def _silu(x):
    return jax.nn.silu(x)

def _sigmoid(x):
    return jax.nn.sigmoid(x)

def _layernorm(x, axis=-1, eps=1e-05):
    m = jnp.mean(x, axis=axis, keepdims=True)
    v = jnp.var(x, axis=axis, keepdims=True)
    return (x - m) / jnp.sqrt(v + eps)

def _scatter_add(tgt, idx, src, axis=0):
    return tgt.at[idx].add(src)

def _segment_sum(src, seg, n):
    return jax.ops.segment_sum(src, seg, n)
kernel_name = 'mk_gnn_ffn_d2_gnn_r8_ee1275'

def setup_inputs(seed: int=0):
    np.random.seed(seed)
    _w = jnp.asarray

    def _rec_inputs():
        import jax
        import jax.numpy as jnp
        _gk = jax.random.key(seed)
        x = -0.0003713 + 1 * jax.random.normal(jax.random.fold_in(_gk, 1), (6250, 256), jnp.float32)
        src = jax.random.randint(jax.random.fold_in(_gk, 2), (200000,), 0, 6250, jnp.int32)
        dst = jnp.minimum((6250 * jax.random.uniform(jax.random.fold_in(_gk, 3), (200000,)) ** 2.0).astype(jnp.int32), 49999)
        _o = jnp.argsort(dst, stable=True)
        src = src[_o]
        dst = dst[_o]
        return (x, src, dst)
    x, src, dst = _rec_inputs()

    def _L0_gnn_setup():
        import jax, jax.numpy as jnp
        import numpy as np
        N, E, H, D, P = (6250, 100000, 4, 64, 16)
        IN = 256
        key = jax.random.key(seed)
        ks = jax.random.split(key, 8)
        feat = jax.random.normal(ks[0], (N, IN), jnp.float32)
        src = jax.random.randint(ks[1], (E,), 0, N, dtype=jnp.int32)
        dst = jax.random.randint(ks[2], (E,), 0, N, dtype=jnp.int32)
        C = IN - P
        W = jax.random.normal(ks[3], (C, H * D), jnp.float32) / np.sqrt(C).astype(np.float32)
        attn_src = jax.random.normal(ks[4], (1, H, D), jnp.float32) * 0.1
        attn_dst = jax.random.normal(ks[5], (1, H, D), jnp.float32) * 0.1
        pos_attn_src = jax.random.normal(ks[6], (1, H, P), jnp.float32) * 0.1
        pos_attn_dst = jax.random.normal(ks[7], (1, H, P), jnp.float32) * 0.1
        return dict(feat=feat, src=src, dst=dst, W=W, attn_src=attn_src, attn_dst=attn_dst, pos_attn_src=pos_attn_src, pos_attn_dst=pos_attn_dst)
    _L0_gnn_all = _L0_gnn_setup()
    _L0_gnn_in = {k: v for k, v in _L0_gnn_all.items() if k in ('W', 'attn_src', 'attn_dst', 'pos_attn_src', 'pos_attn_dst')}
    del _L0_gnn_all

    def _L0_ffn_setup():
        import jax, jax.numpy as jnp
        import numpy as np
        B, T, D, H, E = (16, 512, 256, 512, 8)
        key = jax.random.key(seed)
        ks = jax.random.split(key, 5)
        x = jax.random.normal(ks[0], (B, T, D), dtype=jnp.float32)
        gate_w = jax.random.normal(ks[1], (D, E), dtype=jnp.float32) * 0.02
        gate_b = jnp.zeros((E,), dtype=jnp.float32)
        W1 = jax.random.normal(ks[2], (E, D, H), dtype=jnp.float32) * 0.02
        b1 = jnp.zeros((E, H), dtype=jnp.float32)
        W2 = jax.random.normal(ks[3], (E, H, D), dtype=jnp.float32) * 0.02
        b2 = jnp.zeros((E, D), dtype=jnp.float32)
        return {'x': x, 'gate_w': gate_w, 'gate_b': gate_b, 'W1': W1, 'b1': b1, 'W2': W2, 'b2': b2}
    _L0_ffn_all = _L0_ffn_setup()
    _L0_ffn_in = {k: v for k, v in _L0_ffn_all.items() if k in ('gate_w', 'gate_b', 'W1', 'b1', 'W2', 'b2')}
    del _L0_ffn_all

    def _L1_gnn_setup():
        import jax, jax.numpy as jnp
        import numpy as np
        N_NODES = 1250
        N_EDGES = 40000
        D = 256
        key = jax.random.key(seed)
        k_x, k_w, k_m, k_s, k_d = jax.random.split(key, 5)
        x = jax.random.normal(k_x, (N_NODES, D), dtype=jnp.float32)
        W = jax.random.normal(k_w, (D, D), dtype=jnp.float32)
        M = jax.random.normal(k_m, (D, D), dtype=jnp.float32)
        edge_src = jax.random.randint(k_s, (N_EDGES,), 0, N_NODES, dtype=jnp.int64)
        edge_dst = jax.random.randint(k_d, (N_EDGES,), 0, N_NODES, dtype=jnp.int64)
        return {'x': x, 'W': W, 'M': M, 'edge_src': edge_src, 'edge_dst': edge_dst}
    _L1_gnn_all = _L1_gnn_setup()
    _L1_gnn_in = {k: v for k, v in _L1_gnn_all.items() if k in ('W', 'M')}
    del _L1_gnn_all

    def _L1_ffn_setup():
        import jax, jax.numpy as jnp
        import numpy as np
        BN_EPS = 0.001

        def _bn(h, g, b, m, v):
            return g * (h - m) * jax.lax.rsqrt(v + BN_EPS) + b
        key = jax.random.key(seed)
        ks = jax.random.split(key, 8)
        B, F, Df = (256, 64, 256)
        E, H, D = (8, 256, 256)
        s1 = 1.0 / np.sqrt(Df)
        s2 = 1.0 / np.sqrt(H)
        return {'x': jax.random.normal(ks[0], (B, F, Df), jnp.float32), 'Wr': jax.random.normal(ks[1], (Df, E), jnp.float32) * s1, 'br': jnp.zeros((E,), jnp.float32), 'W1': jax.random.normal(ks[2], (E, Df, H), jnp.float32) * s1, 'b1': jnp.zeros((E, H), jnp.float32), 'g1': jnp.ones((E, H), jnp.float32), 'be1': jnp.zeros((E, H), jnp.float32), 'm1': jnp.zeros((E, H), jnp.float32), 'v1': jnp.ones((E, H), jnp.float32), 'W2': jax.random.normal(ks[3], (E, H, H), jnp.float32) * s2, 'b2': jnp.zeros((E, H), jnp.float32), 'g2': jnp.ones((E, H), jnp.float32), 'be2': jnp.zeros((E, H), jnp.float32), 'm2': jnp.zeros((E, H), jnp.float32), 'v2': jnp.ones((E, H), jnp.float32), 'Wo': jax.random.normal(ks[4], (E, H, D), jnp.float32) * s2, 'bo': jnp.zeros((E, D), jnp.float32)}
    _L1_ffn_all = _L1_ffn_setup()
    _L1_ffn_in = {k: v for k, v in _L1_ffn_all.items() if k in ('Wr', 'br', 'W1', 'b1', 'g1', 'be1', 'm1', 'v1', 'W2', 'b2', 'g2', 'be2', 'm2', 'v2', 'Wo', 'bo')}
    del _L1_ffn_all
    return {'x': x, 'src': src, 'dst': dst, 'L0_gnn_W': _L0_gnn_in['W'], 'L0_gnn_attn_src': _L0_gnn_in['attn_src'], 'L0_gnn_attn_dst': _L0_gnn_in['attn_dst'], 'L0_gnn_pos_attn_src': _L0_gnn_in['pos_attn_src'], 'L0_gnn_pos_attn_dst': _L0_gnn_in['pos_attn_dst'], 'L0_ffn_gate_w': _L0_ffn_in['gate_w'], 'L0_ffn_gate_b': _L0_ffn_in['gate_b'], 'L0_ffn_W1': _L0_ffn_in['W1'], 'L0_ffn_b1': _L0_ffn_in['b1'], 'L0_ffn_W2': _L0_ffn_in['W2'], 'L0_ffn_b2': _L0_ffn_in['b2'], 'L1_gnn_W': _L1_gnn_in['W'], 'L1_gnn_M': _L1_gnn_in['M'], 'L1_ffn_Wr': _L1_ffn_in['Wr'], 'L1_ffn_br': _L1_ffn_in['br'], 'L1_ffn_W1': _L1_ffn_in['W1'], 'L1_ffn_b1': _L1_ffn_in['b1'], 'L1_ffn_g1': _L1_ffn_in['g1'], 'L1_ffn_be1': _L1_ffn_in['be1'], 'L1_ffn_m1': _L1_ffn_in['m1'], 'L1_ffn_v1': _L1_ffn_in['v1'], 'L1_ffn_W2': _L1_ffn_in['W2'], 'L1_ffn_b2': _L1_ffn_in['b2'], 'L1_ffn_g2': _L1_ffn_in['g2'], 'L1_ffn_be2': _L1_ffn_in['be2'], 'L1_ffn_m2': _L1_ffn_in['m2'], 'L1_ffn_v2': _L1_ffn_in['v2'], 'L1_ffn_Wo': _L1_ffn_in['Wo'], 'L1_ffn_bo': _L1_ffn_in['bo']}

def reference(x, src, dst, L0_gnn_W, L0_gnn_attn_src, L0_gnn_attn_dst, L0_gnn_pos_attn_src, L0_gnn_pos_attn_dst, L0_ffn_gate_w, L0_ffn_gate_b, L0_ffn_W1, L0_ffn_b1, L0_ffn_W2, L0_ffn_b2, L1_gnn_W, L1_gnn_M, L1_ffn_Wr, L1_ffn_br, L1_ffn_W1, L1_ffn_b1, L1_ffn_g1, L1_ffn_be1, L1_ffn_m1, L1_ffn_v1, L1_ffn_W2, L1_ffn_b2, L1_ffn_g2, L1_ffn_be2, L1_ffn_m2, L1_ffn_v2, L1_ffn_Wo, L1_ffn_bo):
    import jax
    import jax.numpy as jnp

    def _L0_gnn_ref(feat, src, dst, W, attn_src, attn_dst, pos_attn_src, pos_attn_dst):
        import jax, jax.numpy as jnp
        import numpy as np
        N, E, H, D, P = (6250, 100000, 4, 64, 16)
        IN = 256
        content = feat[:, :-P]
        pos = feat[:, -P:]
        ft = (content @ W).reshape(N, H, D)
        s_src = jnp.einsum('nhd,hd->nh', ft, attn_src[0])
        s_dst = jnp.einsum('nhd,hd->nh', ft, attn_dst[0])
        p_src = jnp.einsum('np,hp->nh', pos, pos_attn_src[0])
        p_dst = jnp.einsum('np,hp->nh', pos, pos_attn_dst[0])
        e = (s_src + p_src)[src] + (s_dst + p_dst)[dst]
        e = jax.nn.leaky_relu(e, negative_slope=0.2)
        emax = jax.ops.segment_max(e, dst, num_segments=N)
        ex = jnp.exp(e - emax[dst])
        denom = jax.ops.segment_sum(ex, dst, num_segments=N)
        a = ex / denom[dst]
        msg = ft[src] * a[:, :, None]
        out = jax.ops.segment_sum(msg, dst, num_segments=N)
        h = out.reshape(N, H * D)
        return h + feat

    def _L0_ffn_ref(x, gate_w, gate_b, W1, b1, W2, b2):
        import jax, jax.numpy as jnp
        import numpy as np
        B, T, D, H, E = (16, 512, 256, 512, 8)
        Bb, Tt, Dd = x.shape
        Ee = gate_w.shape[1]
        xf = x.reshape(-1, Dd)
        N = xf.shape[0]
        logits = xf @ gate_w + gate_b
        probs = jax.nn.softmax(logits, axis=-1)
        top2_vals, top2_idx = jax.lax.top_k(probs, 2)
        cw = jnp.zeros((N, Ee), dtype=xf.dtype).at[jnp.arange(N)[:, None], top2_idx].add(top2_vals)

        def step(acc, params):
            w1, bb1, w2, bb2, we = params
            h = jax.nn.gelu(xf @ w1 + bb1, approximate=False)
            y = h @ w2 + bb2
            return (acc + we[:, None] * y, None)
        out, _ = jax.lax.scan(step, jnp.zeros_like(xf), (W1, b1, W2, b2, cw.T))
        return out.reshape(Bb, Tt, Dd)

    def _L1_gnn_ref(x, W, M, edge_src, edge_dst):
        import jax, jax.numpy as jnp
        import numpy as np
        N_NODES = 1250
        N_EDGES = 40000
        D = 256
        self_term = x @ W
        msg = x @ M
        agg = jax.ops.segment_sum(msg[edge_src], edge_dst, num_segments=x.shape[0])
        return jax.nn.relu(self_term + agg)

    def _L1_ffn_ref(x, Wr, br, W1, b1, g1, be1, m1, v1, W2, b2, g2, be2, m2, v2, Wo, bo):
        import jax, jax.numpy as jnp
        import numpy as np
        BN_EPS = 0.001

        def _bn(h, g, b, m, v):
            return g * (h - m) * jax.lax.rsqrt(v + BN_EPS) + b
        feat = jnp.mean(x, axis=0)
        w = jax.nn.softmax(feat @ Wr + br, axis=-1)
        h = jnp.einsum('bfd,edh->bfeh', x, W1) + b1
        h = jax.nn.relu(_bn(h, g1, be1, m1, v1))
        h = jnp.einsum('bfeh,ehk->bfek', h, W2) + b2
        h = jax.nn.relu(_bn(h, g2, be2, m2, v2))
        y = jnp.einsum('bfeh,ehd->bfed', h, Wo) + bo
        return jnp.einsum('bfed,fe->bfd', y, w)
    x = x + _L0_gnn_ref(_layernorm(x, axis=-1), src, dst, L0_gnn_W, L0_gnn_attn_src, L0_gnn_attn_dst, L0_gnn_pos_attn_src, L0_gnn_pos_attn_dst)
    x = x + _L0_ffn_ref(_layernorm(x, axis=-1)[None], L0_ffn_gate_w, L0_ffn_gate_b, L0_ffn_W1, L0_ffn_b1, L0_ffn_W2, L0_ffn_b2)[0]
    x = x + _L1_gnn_ref(_layernorm(x, axis=-1), L1_gnn_W, L1_gnn_M, src, dst)
    x = x + _L1_ffn_ref(_layernorm(x, axis=-1)[None], L1_ffn_Wr, L1_ffn_br, L1_ffn_W1, L1_ffn_b1, L1_ffn_g1, L1_ffn_be1, L1_ffn_m1, L1_ffn_v1, L1_ffn_W2, L1_ffn_b2, L1_ffn_g2, L1_ffn_be2, L1_ffn_m2, L1_ffn_v2, L1_ffn_Wo, L1_ffn_bo)[0]
    return x

_drawn_inputs = setup_inputs


def setup_inputs(seed=0):
    import zlib

    import numpy as np

    out = dict(_drawn_inputs(seed))
    spreads = {'L0_ffn_gate_b': (0.0, 0.267),
     'L0_ffn_b1': (0.0, 0.541),
     'L0_ffn_b2': (0.0, 0.1),
     'L1_ffn_br': (0.0, 0.8),
     'L1_ffn_b1': (0.0, 0.8),
     'L1_ffn_g1': (1.0, 0.6),
     'L1_ffn_be1': (0.0, 0.8),
     'L1_ffn_m1': (0.0, 0.8),
     'L1_ffn_v1': (1.0, 0.6),
     'L1_ffn_b2': (0.0, 2.0),
     'L1_ffn_g2': (1.0, 0.6),
     'L1_ffn_be2': (0.0, 2.0),
     'L1_ffn_m2': (0.0, 2.0),
     'L1_ffn_v2': (1.0, 0.6),
     'L1_ffn_bo': (0.0, 2.0)}
    factors = {'L0_gnn_pos_attn_dst': 4.395,
     'L0_ffn_gate_w': 4.023,
     'L0_ffn_W1': 5.483,
     'L1_ffn_Wr': 8.0,
     'L1_ffn_W1': 8.0,
     'L1_ffn_W2': 8.0,
     'L1_ffn_Wo': 8.0}
    for name, (base, spread) in spreads.items():
        noise = np.random.default_rng([zlib.crc32(name.encode()), seed]).standard_normal(out[name].shape)
        drawn = base * np.exp(spread * noise) if base else spread * noise
        out[name] = jnp.asarray(drawn.astype(out[name].dtype))
    for name, factor in factors.items():
        out[name] = (out[name] * factor).astype(out[name].dtype)
    return out
```

```python
from contextlib import ExitStack

import concourse.bass as bass
from concourse import mybir

F32 = mybir.dt.float32
BF16 = mybir.dt.bfloat16
I32 = mybir.dt.int32
ALU = mybir.AluOpType
ACT = mybir.ActivationFunctionType
AX = mybir.AxisListType
ds = bass.ds

P = 128
LN_EPS = 1e-5
BN_EPS = 0.001
NEG_SLOPE = 0.2
FAR = 1e30


class Shapes:

    def __init__(self, x, src, w0, attn, pos, w1, w2, wr, v1):
        self.N, self.D = x.shape
        self.E = src.shape[0]
        self.C = w0.shape[0]
        self.H, self.HD = attn.shape[1:]
        self.PD = pos.shape[2]
        self.X, _, self.F = w1.shape
        self.X2, self.F2 = v1.shape
        self.T = -(-self.N // P)
        self.G = 7
        self.NG = self.T // self.G
        self.W = self.G * P
        self.HW = self.W // 2
        self.LAST = self.N - (self.T - 1) * P
        self.KC = self.D // P
        self.HC = self.F // P
        self.K = 8
        self.HK = self.K // 2
        self.B = P * self.K
        self.NB = 2 * -(-self.E // (2 * self.B))
        self.A = self.HD + 1
        assert self.T % self.G == 0 and self.D % P == 0 and self.H * self.HD == self.D
        assert self.C + self.PD == self.D and self.HW <= 512 and self.X == self.X2


class Chain:

    def __init__(self, eng, sem, per=0):
        self.eng, self.sem, self.per, self.base, self.n = eng, sem, per, 0, 0

    def begin(self, i):
        self.base, self.n = i * self.per, 0

    def link(self, ins):
        self.n += 1
        ins.then_inc(self.sem, 1)
        self.eng.wait_ge(self.sem, self.base + self.n)

    def end(self):
        assert self.n == self.per, (self.n, self.per)


class Core:

    def __init__(self, nc, z):
        self.nc, self.z, self.phase = nc, z, "all"

    def sb(self, ctx, name, shape, dt=F32):
        return ctx.enter_context(self.nc.sbuf_tensor(f"{self.phase}_{name}", shape, dt))

    def ps(self, ctx, name, shape, dt=F32):
        bank = ctx.enter_context(self.nc.psum_tensor(f"{self.phase}_{name}", [P, 2048 // (2 if dt == BF16 else 4)], dt))
        if len(shape) == 2:
            return bank[:, 0:shape[1]]
        size = 1
        for n in shape[1:]:
            size *= n
        names = "abcd"[:len(shape) - 1]
        sizes = dict(zip(names, shape[1:]))
        return bank[:, 0:size].rearrange(f"p ({' '.join(names)}) -> p {' '.join(names)}", **sizes)

    def sem(self, ctx, name):
        return ctx.enter_context(self.nc.semaphore(f"{self.phase}_{name}"))


def alone(c, eng):
    eng.sem_inc(c.pace, 1)


def spread(ap, shape):
    return ap.broadcast_to(shape)


def prepare(c, x, src, dst, w0, attn_src, attn_dst, pos_src, pos_dst, bn_in, bn_out):
    nc, z = c.nc, c.z
    T, K, NB, B, H, HD, KC, X = z.T, z.K, z.NB, z.B, z.H, z.HD, z.KC, z.X
    NT = -(-NB // P)
    full, rest = z.E // B, z.E % B
    c.phase = "prepare"
    with ExitStack() as ctx:
        s = lambda n: c.sem(ctx, n)
        posw = c.sb(ctx, "posw", [P, KC, 2 * H])
        ablk = c.sb(ctx, "ablk", [P, KC, 2 * H])
        wt = c.sb(ctx, "wt", [P, KC, KC * P])
        edge_i = c.sb(ctx, "edge_i", [P, 2, NT, B], I32)
        edge_f = c.sb(ctx, "edge_f", [P, 2, NT, B])
        span_i = c.sb(ctx, "span_i", [P, NT, 2], I32)
        iota_i = c.sb(ctx, "iota_i", [P, P], I32)
        base_i = c.sb(ctx, "base_i", [P, T], I32)
        bn = c.sb(ctx, "bn", [P, 2, 5, X, z.F2 // P])
        tmp = c.sb(ctx, "bn_tmp", [P, 2, X, z.F2 // P])
        tp = [c.ps(ctx, f"tp{i}", [P, 512]) for i in range(2)]
        wa = c.ps(ctx, "wa", [P, KC, 2 * H])
        x_in, w_in, e_in, bn_ld = s("x_in"), s("w_in"), s("e_in"), s("bn_ld")
        cleared, pool_step, consts, edges_f, dve_step = s("cleared"), s("pool_step"), s("consts"), s("edges_f"), s("dve_step")
        turned, copied, span_out, span_in, wa_ready, sd_ready, bn_ready, bn_st = (
            s("turned"), s("copied"), s("span_out"), s("span_in"), s("wa_ready"), s("sd_ready"), s("bn_ready"), s("bn_st"))
        tmp_out = [[bn[:, n, 1, :, :], bn[:, n, 2, :, :]] for n in range(2)]
        block = ctx.enter_context(nc.Block())

        @block.gpsimd
        def _(pool):
            pool.memset(c.wall[:, :, :], 0.0)
            pool.memset(posw[:, :, :], 0.0)
            pool.memset(ablk[:, :, :], 0.0)
            pool.memset(c.res[:, T - 1, :], 0.0)
            pool.memset(edge_i[:, 0, NT - 1, :], 0)
            pool.memset(edge_i[:, 1, NT - 1, :], T * P + 1).then_inc(cleared, 1)
            pool.memset(c.src_all[:, NB * K:(NB + 1) * K], 0)
            pool.memset(c.ident[:, :], 0.0)
            pool.memset(c.ones[:, :], 1.0)
            pool.memset(c.tri[:, :, :], 0.0)
            pool.memset(c.sel[:, :, :], 0.0)
            pool.memset(c.eps[:, 0:1], LN_EPS)
            pool.memset(c.eps[:, 1:2], BN_EPS)
            pool.iota(iota_i[:, :], pattern=[[1, P]], base=0, channel_multiplier=0)
            pool.iota(base_i[:, :], pattern=[[P, T]], base=0, channel_multiplier=0).then_inc(pool_step, 1)
            pool.wait_ge(pool_step, 1)
            pool.affine_select(out=c.ident[:, :], in_=c.ident[:, :], compare_op=ALU.not_equal, fill=1.0,
                               base=0, pattern=[[-1, P]], channel_multiplier=1)
            pool.affine_select(out=c.tri[:, :, :], in_=c.tri[:, :, :], compare_op=ALU.is_ge, fill=1.0,
                               base=0, pattern=[[-1, X], [1, X]], channel_multiplier=0)
            pool.affine_select(out=c.sel[:, :, :], in_=c.sel[:, :, :], compare_op=ALU.not_equal, fill=1.0,
                               base=0, pattern=[[-1, H], [0, P]], channel_multiplier=1).then_inc(consts, 1)

        @block.sync
        def _(sp):
            sp.wait_ge(cleared, 1)
            for n, e in enumerate((src, dst)):
                for t in range(NT):
                    rows = min(full - t * P, P)
                    sp.dma_start(edge_i[0:rows, n, t, :],
                                 e[t * P * B:(t * P + rows) * B].rearrange("(s e) -> s e", e=B)).then_inc(e_in, 16)
                    if rows < P and rest:
                        sp.dma_start(edge_i[rows:rows + 1, n, t, 0:rest],
                                     e[full * B:z.E].rearrange("(s e) -> s e", s=1)).then_inc(e_in, 16)
            sp.dma_start(c.wall[:, 0, 0:z.D], w0[0:P, :]).then_inc(w_in, 16)
            sp.dma_start(c.wall[0:z.C - P, 1, 0:z.D], w0[P:z.C, :]).then_inc(w_in, 16)
            for n, a in enumerate((attn_src, attn_dst)):
                for h in range(H):
                    at = h * HD
                    sp.dma_start(ablk[at % P:at % P + HD, at // P, n * H + h:n * H + h + 1],
                                 a[0, h, :].rearrange("(d o) -> d o", o=1)).then_inc(w_in, 16)
            for n, a in enumerate((pos_src, pos_dst)):
                sp.dma_start(posw[z.C - P:P, 1, n * H:(n + 1) * H],
                             a[0, :, :].rearrange("h p -> p h"), allow_slow_non_contiguous=True).then_inc(w_in, 16)
            for n, layer in enumerate(bn_in):
                for m, a in enumerate(layer):
                    for e in range(X):
                        sp.dma_start(bn[:, n, m, e, :], a[e, :].rearrange("(k p) -> p k", p=P),
                                     allow_slow_non_contiguous=True).then_inc(bn_ld, 16)
            sp.wait_ge(dve_step, 4)
            for t in range(NT):
                rows = min(NB - t * P, P)
                sp.dma_start(c.span_d[t * P:t * P + rows, :], span_i[0:rows, t, :]).then_inc(span_out, 16)
            sp.wait_ge(span_out, 16 * NT)
            sp.dma_start(c.spans[0:1, :], c.span_d.rearrange("(o s) c -> o (s c)", o=1)).then_inc(span_in, 16)
            sp.wait_ge(bn_ready, 1)
            for n in range(2):
                for m in range(2):
                    sp.dma_start(bn_out[n][m].rearrange("e p k -> p e k"), tmp_out[n][m]).then_inc(bn_st, 16)
            sp.wait_ge(bn_st, 16 * 4)
            sp.wait_ge(span_in, 16)
            sp.wait_ge(x_in, 32)

        @block.scalar
        def _(act):
            act.dma_start(c.res[:, 0:T - 1, :],
                          x[0:(T - 1) * P, :].rearrange("(t p) d -> p t d", p=P)).then_inc(x_in, 16)
            act.wait_ge(cleared, 1)
            act.dma_start(c.res[0:z.LAST, T - 1, :], x[(T - 1) * P:z.N, :]).then_inc(x_in, 16)
            act.wait_ge(consts, 1)
            q = 0
            for n, table in enumerate((c.src_all, c.dst_all)):
                for t in range(NT):
                    rows = min(NB - t * P, P)
                    for k in range(K):
                        act.wait_ge(turned, q + 1)
                        out = table[:, t * P * K:(t * P + rows) * K].rearrange("p (s k) -> p s k", k=K)[:, :, k]
                        act.activation(out, tp[q % 2][:, 0:rows], ACT.Copy).then_inc(copied, 1)
                        q += 1
            for j in range(KC * KC):
                act.wait_ge(turned, q + 1)
                act.activation(wt[:, j // KC, (j % KC) * P:(j % KC + 1) * P], tp[q % 2][:, 0:P], ACT.Copy).then_inc(copied, 1)
                q += 1
            act.wait_ge(bn_ld, 16 * 10 * X)
            for n in range(2):
                last = act.activation(tmp[:, n, :, :], bn[:, n, 4, :, :], ACT.Sqrt, bias=c.eps[:, 1:2])
            last.then_inc(sd_ready, 1)

        @block.tensor
        def _(pe):
            pe.wait_ge(consts, 1)
            pe.wait_ge(edges_f, 1)
            q = 0
            for n in range(2):
                for t in range(NT):
                    rows = min(NB - t * P, P)
                    for k in range(K):
                        if q >= 2:
                            pe.wait_ge(copied, q - 1)
                        pe.transpose(tp[q % 2][:, 0:rows],
                                     edge_f[0:rows, n, t, :].rearrange("s (p k) -> s p k", k=K)[:, :, k],
                                     c.ident[0:rows, 0:rows]).then_inc(turned, 1)
                        q += 1
            pe.wait_ge(w_in, 16 * (4 + 2 * H))
            for jc in range(KC):
                for kc in range(KC):
                    pe.wait_ge(copied, q - 1)
                    pe.transpose(tp[q % 2][:, 0:P], c.wall[:, kc, jc * P:(jc + 1) * P],
                                 c.ident[:, :]).then_inc(turned, 1)
                    q += 1
            pe.wait_ge(copied, q)
            for kc in range(KC):
                for jc in range(KC):
                    last = pe.matmul(wa[:, kc, :], wt[:, jc, kc * P:(kc + 1) * P], ablk[:, jc, :],
                                     start=(jc == 0), stop=(jc == KC - 1))
            last.then_inc(wa_ready, 1)

        @block.vector
        def _(dve):
            ch = Chain(dve, dve_step)
            dve.wait_ge(e_in, 16 * (2 * NT + 2))
            for n in range(2):
                last = dve.tensor_copy(edge_f[:, n, :, :], edge_i[:, n, :, :])
            last.then_inc(edges_f, 1)
            dve.wait_ge(edges_f, 1)
            last = dve.tensor_reduce(span_i[:, :, 0], edge_f[:, 1, :, :], AX.X, ALU.min)
            ch.link(dve.tensor_reduce(span_i[:, :, 1], edge_f[:, 1, :, :], AX.X, ALU.max))
            ch.link(dve.tensor_scalar(span_i[:, :, :], span_i[:, :, :], 7, None, ALU.arith_shift_right))
            ch.link(dve.tensor_scalar(span_i[:, :, 1], span_i[:, :, 1], 1.0, float(T), ALU.add, ALU.min))
            ch.link(dve.tensor_scalar(span_i[:, :, 0], span_i[:, :, 0], float(T - 1), None, ALU.min))
            dve.wait_ge(pool_step, 1)
            dve.tensor_copy(c.iota[:, :], iota_i[:, :])
            dve.tensor_copy(c.base[:, :], base_i[:, :])
            dve.wait_ge(w_in, 16 * (4 + 2 * H))
            dve.wait_ge(wa_ready, 1)
            dve.tensor_tensor(c.wall[:, :, z.D:], wa[:, :, :], posw[:, :, :], ALU.add)
            dve.wait_ge(sd_ready, 1)
            ch.link(dve.reciprocal(tmp[:, :, :, :], tmp[:, :, :, :]))
            ch.link(dve.tensor_tensor(bn[:, :, 1, :, :], bn[:, :, 1, :, :], tmp[:, :, :, :], ALU.mult))
            ch.link(dve.tensor_tensor(bn[:, :, 0, :, :], bn[:, :, 0, :, :], bn[:, :, 3, :, :], ALU.subtract))
            ch.link(dve.tensor_tensor(bn[:, :, 0, :, :], bn[:, :, 0, :, :], bn[:, :, 1, :, :], ALU.mult))
            dve.tensor_tensor(bn[:, :, 2, :, :], bn[:, :, 0, :, :], bn[:, :, 2, :, :], ALU.add).then_inc(bn_ready, 1)


def normalise(c, dve, ch, g, stats, mv, sd, rstd, xn, var_ready, sd_ready, nth):
    z = c.z
    alone(c, dve)
    for j in range(z.G):
        last = dve.bn_stats(stats[:, j, :], c.res[:, ds(g * z.G + j, 1), :].rearrange("p a d -> p (a d)"))
    ch.link(last)
    alone(c, dve)
    for j in range(z.G):
        last = dve.bn_aggr(mv[:, j, :], stats[:, j, :])
    last.then_inc(var_ready, 1)
    dve.wait_ge(sd_ready, nth)
    ch.link(dve.reciprocal(rstd[:, :], sd[:, :]))
    dve.wait_ge(var_ready, nth)
    for j in range(z.G):
        last = dve.tensor_scalar(xn[:, j, :], c.res[:, ds(g * z.G + j, 1), :].rearrange("p a d -> p (a d)"),
                                 mv[:, j, 0:1], rstd[:, j:j + 1], ALU.subtract, ALU.mult)
    return last


def project(c, tab, scores):
    nc, z = c.nc, c.z
    G, KC, H = z.G, z.KC, z.H
    WC = z.D + 2 * H
    c.phase = "project"
    with ExitStack() as ctx:
        s = lambda n: c.sem(ctx, n)
        stats = c.sb(ctx, "stats", [P, G, 6])
        mv = c.sb(ctx, "mv", [P, G, 2])
        sd = c.sb(ctx, "sd", [P, G])
        rstd = c.sb(ctx, "rstd", [P, G])
        xn = c.sb(ctx, "xn", [P, G, z.D])
        xt = c.sb(ctx, "xt", [P, G, KC, P])
        rows = c.sb(ctx, "rows", [P, G, WC])
        tp = [c.ps(ctx, f"tp{i}", [P, KC, P]) for i in range(2)]
        ft = [c.ps(ctx, f"ft{i}", [P, 512]) for i in range(2)]
        dve_step, var_ready, sd_ready, xn_ready, turned, xt_ready, ft_ready, rows_ready, stored = (
            s(n) for n in ("dve_step", "var_ready", "sd_ready", "xn_ready", "turned", "xt_ready", "ft_ready", "rows_ready", "stored"))
        block = ctx.enter_context(nc.Block())

        @block.vector
        def _(dve):
            ch = Chain(dve, dve_step, 2)
            with dve.Fori(0, z.NG) as g:
                ch.begin(g)
                dve.wait_ge(turned, g * G)
                normalise(c, dve, ch, g, stats, mv, sd, rstd, xn, var_ready, sd_ready, g + 1).then_inc(xn_ready, 1)
                ch.end()
                dve.wait_ge(stored, g * 32)
                for j in range(G):
                    dve.wait_ge(ft_ready, g * G + j + 1)
                    dve.tensor_copy(rows[:, j, :], ft[j % 2][:, 0:WC]).then_inc(rows_ready, 1)

        @block.scalar
        def _(act):
            with act.Fori(0, z.NG) as g:
                act.wait_ge(var_ready, g + 1)
                act.activation(sd[:, :], mv[:, :, 1], ACT.Sqrt, bias=c.eps[:, 0:1]).then_inc(sd_ready, 1)
                for j in range(G):
                    act.wait_ge(turned, g * G + j + 1)
                    if j == 0:
                        act.wait_ge(ft_ready, g * G)
                    act.activation(xt[:, j, :, :], tp[j % 2][:, :, :], ACT.Copy).then_inc(xt_ready, 1)

        @block.tensor
        def _(pe):
            with pe.Fori(0, z.NG) as g:
                pe.wait_ge(xn_ready, g + 1)
                for j in range(G):
                    pe.wait_ge(xt_ready, g * G + max(j - 1, 0))
                    for k in range(KC):
                        last = pe.transpose(tp[j % 2][:, k, :], xn[:, j, k * P:(k + 1) * P], c.ident[:, :])
                    last.then_inc(turned, 1)
                for j in range(G):
                    pe.wait_ge(xt_ready, g * G + j + 1)
                    pe.wait_ge(rows_ready, g * G + max(j - 1, 0))
                    for k in range(KC):
                        last = pe.matmul(ft[j % 2][:, 0:WC], xt[:, j, k, :], c.wall[:, k, :],
                                         start=(k == 0), stop=(k == KC - 1))
                    last.then_inc(ft_ready, 1)

        @block.sync
        def _(sp):
            with sp.Fori(0, z.NG) as g:
                sp.wait_ge(rows_ready, g * G + G)
                sp.dma_start(tab[ds(g * z.W, z.W), :].rearrange("(t p) d -> p t d", p=P),
                             rows[:, :, 0:z.D + H]).then_inc(stored, 16)
                sp.dma_start(scores[ds(g * z.W, z.W), :].rearrange("(t p) d -> p t d", p=P),
                             rows[:, :, z.D:]).then_inc(stored, 16)
            sp.wait_ge(stored, z.NG * 32)


def load_span(eng, c, sc):
    lo = eng.value_load(c.spans[0:1, ds(sc * 2, 1)], min_val=0, max_val=c.z.T - 1)
    hi = eng.value_load(c.spans[0:1, ds(sc * 2 + 1, 1)], min_val=1, max_val=c.z.T)
    return lo, hi


def gather_rows(c, pool, tab, idx, rows, idx_ready, rows_free, gathered):
    z = c.z
    with pool.Fori(0, z.NB // 2) as i:
        for u in range(2):
            pool.wait_ge(idx_ready, 2 * i + u + 1)
            pool.wait_ge(rows_free, 2 * i + u + 1)
            alone(c, pool)
            for k in range(z.K):
                pool.indirect_dma_start(rows[u][:, k, :], None, tab,
                                        bass.IndirectOffsetOnAxis(ap=idx[u][:, k:k + 1], axis=0)
                                        ).then_inc(gathered[u][k // z.HK], 16)


def copy_indices(c, act, sc, idx, u):
    return act.activation(idx[u][:, :], c.src_all[:, ds(sc * c.z.K, c.z.K)], ACT.Copy)


def attend(c, tab, scores):
    nc, z = c.nc, c.z
    T, K, HK, H, HD, D, A = z.T, z.K, z.HK, z.H, z.HD, z.D, z.A
    c.phase = "attend"
    with ExitStack() as ctx:
        s = lambda n: c.sem(ctx, n)
        rows = [c.sb(ctx, f"rows{u}", [P, K, D + H]) for u in range(2)]
        idx = [c.sb(ctx, f"idx{u}", [P, K], I32) for u in range(2)]
        ad = c.sb(ctx, "ad", [P, T, 2 * H])
        top = c.sb(ctx, "top", [P, T, H])
        dl = c.sb(ctx, "dl", [P, K])
        oh = [c.sb(ctx, f"oh{h}", [P, HK, P]) for h in range(2)]
        oht = [c.sb(ctx, f"oht{h}", [P, HK * P]) for h in range(2)]
        pen = [c.sb(ctx, f"pen{h}", [P, HK * P]) for h in range(2)]
        ast = [c.sb(ctx, f"ast{h}", [H, HK * P]) for h in range(2)]
        junk = c.sb(ctx, "junk", [P, HK * P])
        run = c.sb(ctx, "run", [P, 3, H])
        adm = c.sb(ctx, "adm", [P, 2, 2 * H])
        fade = c.sb(ctx, "fade", [P, 2, H])
        zz = [c.sb(ctx, f"zz{h}", [P, HK, H]) for h in range(2)]
        msg = [c.sb(ctx, f"msg{h}", [P, HK, H, A]) for h in range(2)]
        tp = [c.ps(ctx, f"tp{h}", [P, HK * P]) for h in range(2)]
        ade = [c.ps(ctx, f"ade{h}", [P, HK, 2 * H]) for h in range(2)]
        bc = [c.ps(ctx, f"bc{h}", [P, HK * P]) for h in range(2)]
        astp = c.ps(ctx, "astp", [P, HK * P])
        accp = c.ps(ctx, "accp", [P, 512])
        gathered = [[s(f"gathered{u}{h}") for h in range(2)] for u in range(2)]
        names = ("idx_ready", "rows_free", "ad_in", "cleared", "dve_step", "onehot_ready",
                 "turned", "oht_ready", "pen_ready", "ast_turned", "ast_ready", "bc_ready", "bc_used",
                 "top_ready", "fade_ready", "fade_z", "ade_ready", "z_ready", "w_ready", "msg_ready", "main_done", "acc_added", "final_step")
        (idx_ready, rows_free, ad_in, cleared, dve_step, onehot_ready,
         turned, oht_ready, pen_ready, ast_turned, ast_ready, bc_ready, bc_used,
         top_ready, fade_ready, fade_z, ade_ready, z_ready, w_ready, msg_ready, main_done, acc_added, final_step) = (s(n) for n in names)
        block = ctx.enter_context(nc.Block())

        @block.sync
        def _(sp):
            sp.dma_start(ad[:, :, :], scores.rearrange("(t p) c -> p t c", p=P)).then_inc(ad_in, 16)
            sp.wait_ge(ad_in, 16)

        @block.gpsimd
        def _(pool):
            gather_rows(c, pool, tab, idx, rows, idx_ready, rows_free, gathered)

        @block.scalar
        def _(act):
            copy_indices(c, act, 0, idx, 0).then_inc(idx_ready, 1)
            r = act.alloc_register(f"{c.phase}_pairs")
            act.reg_mov(r, 0)
            with act.Fori(0, z.NB // 2) as i:
                for u in range(2):
                    sc = 2 * i + u
                    for h in range(2):
                        act.wait_ge(gathered[1 - u][h], (i + u) * 16 * HK)
                    alone(c, act)
                    copy_indices(c, act, sc + 1, idx, 1 - u).then_inc(idx_ready, 1)
                    lo, hi = load_span(act, c, sc)
                    with act.Fori(lo, hi) as b:
                        t = act.snap(r)
                        for h in range(2):
                            act.wait_ge(turned, 2 * t + h + 1)
                            act.activation(oht[h][:, :], tp[h][:, :], ACT.Copy).then_inc(oht_ready, 1)
                            act.activation(pen[h][:, :], tp[h][:, :], ACT.Copy, scale=FAR, bias=-FAR).then_inc(pen_ready, 1)
                            act.wait_ge(ast_turned, 2 * t + h + 1)
                            act.activation(ast[h][:, :], astp[0:H, :], ACT.Copy).then_inc(ast_ready, 1)
                        act.wait_ge(fade_z, t + 1)
                        act.activation(fade[:, 1, :], fade[:, 0, :], ACT.Exp).then_inc(fade_ready, 1)
                        for h in range(2):
                            act.wait_ge(z_ready, 2 * t + h + 1)
                            act.activation(msg[h][:, :, :, HD], zz[h][:, :, :], ACT.Exp).then_inc(w_ready, 1)
                        act.reg_add(r, r, 1)

        @block.tensor
        def _(pe):
            pe.sem_inc(main_done, 2)
            r = pe.alloc_register(f"{c.phase}_pairs")
            pe.reg_mov(r, 0)
            with pe.Fori(0, z.NB // 2) as i:
                for u in range(2):
                    lo, hi = load_span(pe, c, 2 * i + u)
                    with pe.Fori(lo, hi) as b:
                        t = pe.snap(r)
                        for h in range(2):
                            pe.wait_ge(onehot_ready, 2 * t + h + 1)
                            for k in range(HK):
                                last = pe.transpose(tp[h][:, k * P:(k + 1) * P], oh[h][:, k, :], c.ident[:, :])
                            last.then_inc(turned, 1)
                            pe.wait_ge(gathered[u][h], (i + 1) * 16 * HK)
                            pe.wait_ge(ast_ready, 2 * t + h)
                            for k in range(HK):
                                last = pe.transpose(astp[0:H, k * P:(k + 1) * P], rows[u][:, h * HK + k, D:], c.ident[:, :])
                            last.then_inc(ast_turned, 1)
                            pe.wait_ge(ast_ready, 2 * t + h + 1)
                            for n in range(H):
                                pe.wait_ge(bc_used, t * 2 * H + max(h * H + n - 1, 0))
                                pe.matmul(bc[n % 2][:, :], c.sel[0:H, n, :], ast[h][:, :], start=True, stop=True).then_inc(bc_ready, 1)
                        pe.wait_ge(top_ready, t + 1)
                        for h in range(2):
                            pe.wait_ge(oht_ready, 2 * t + h + 1)
                            for k in range(HK):
                                last = pe.matmul(ade[h][:, k, :], oht[h][:, k * P:(k + 1) * P], adm[:, 0, :], start=True, stop=True)
                            last.then_inc(ade_ready, 1)
                        pe.wait_ge(acc_added, t)
                        for h in range(2):
                            pe.wait_ge(msg_ready, 2 * t + h + 1)
                            for k in range(HK):
                                last = pe.matmul(accp[:, 0:H * A], oh[h][:, k, :], msg[h][:, k, :, :].rearrange("p h a -> p (h a)"),
                                                 start=(h == 0 and k == 0), stop=(h == 1 and k == HK - 1))
                            last.then_inc(main_done, 1)
                        pe.reg_add(r, r, 1)

        @block.vector
        def _(dve):
            dve.memset(c.acc[:, :, :], 0.0)
            dve.memset(top[:, :, :], -FAR).then_inc(cleared, 1)
            dve.sem_inc(rows_free, 2)
            dve.wait_ge(ad_in, 16)
            dve.wait_ge(cleared, 1)
            ch = Chain(dve, dve_step, 11)
            r = dve.alloc_register(f"{c.phase}_pairs")
            dve.reg_mov(r, 0)
            with dve.Fori(0, z.NB // 2) as i:
                for u in range(2):
                    sc = 2 * i + u
                    lo, hi = load_span(dve, c, sc)
                    with dve.Fori(lo, hi) as b:
                        t = dve.snap(r)
                        ch.begin(t)
                        ch.link(dve.tensor_scalar(dl[:, :], c.dst_all[:, ds(sc * K, K)], c.base[:, ds(b, 1)], None, ALU.subtract))
                        for h in range(2):
                            dve.wait_ge(main_done, 2 * t + h + 1)
                            dve.tensor_tensor(oh[h][:, :, :], spread(c.iota[:, :].unsqueeze(1), [P, HK, P]),
                                              spread(dl[:, h * HK:(h + 1) * HK].unsqueeze(2), [P, HK, P]),
                                              ALU.is_equal).then_inc(onehot_ready, 1)
                        ch.link(dve.tensor_scalar(run[:, 0, :], top[:, ds(b, 1), :].rearrange("p a h -> p (a h)"), 1.0, None, ALU.mult))
                        for h in range(2):
                            dve.wait_ge(pen_ready, 2 * t + h + 1)
                            for n in range(H):
                                dve.wait_ge(bc_ready, t * 2 * H + h * H + n + 1)
                                alone(c, dve)
                                dve.tensor_tensor_reduce(out=junk[:, :], in0=bc[n % 2][:, :], in1=pen[h][:, :], scale=1.0,
                                                         scalar=run[:, h, n:n + 1], op0=ALU.add, op1=ALU.max,
                                                         accum_out=run[:, h + 1, n:n + 1]).then_inc(bc_used, 1)
                                dve.wait_ge(bc_used, t * 2 * H + h * H + n + 1)
                        ch.link(dve.tensor_scalar(top[:, ds(b, 1), :].rearrange("p a h -> p (a h)"), run[:, 2, :], 1.0, None, ALU.mult))
                        a_b = ad[:, ds(b, 1), H:2 * H].rearrange("p a h -> p (a h)")
                        dve.tensor_scalar(adm[:, 0, 0:H], a_b, 1.0, None, ALU.mult)
                        dve.tensor_tensor(adm[:, 0, H:], run[:, 2, :], a_b, ALU.add)
                        ch.link(dve.tensor_tensor(adm[:, 1, H:], run[:, 0, :], a_b, ALU.add))
                        dve.scalar_tensor_tensor(adm[:, 0, H:], adm[:, 0, H:], NEG_SLOPE, adm[:, 0, H:], ALU.mult, ALU.max).then_inc(top_ready, 1)
                        ch.link(dve.scalar_tensor_tensor(adm[:, 1, H:], adm[:, 1, H:], NEG_SLOPE, adm[:, 1, H:], ALU.mult, ALU.max))
                        dve.tensor_tensor(fade[:, 0, :], adm[:, 1, H:], adm[:, 0, H:], ALU.subtract).then_inc(fade_z, 1)
                        for h in range(2):
                            dve.wait_ge(ade_ready, 2 * t + h + 1)
                            dve.wait_ge(gathered[u][h], (i + 1) * 16 * HK)
                            ch.link(dve.tensor_tensor(zz[h][:, :, :], rows[u][:, h * HK:(h + 1) * HK, D:], ade[h][:, :, 0:H], ALU.add))
                            ch.link(dve.scalar_tensor_tensor(zz[h][:, :, :], zz[h][:, :, :], NEG_SLOPE, zz[h][:, :, :], ALU.mult, ALU.max))
                            ch.link(dve.tensor_tensor(zz[h][:, :, :], zz[h][:, :, :], ade[h][:, :, H:], ALU.subtract))
                            dve.tensor_scalar(zz[h][:, :, :], zz[h][:, :, :], 0.0, None, ALU.min).then_inc(z_ready, 1)
                        for h in range(2):
                            dve.wait_ge(w_ready, 2 * t + h + 1)
                            dve.tensor_tensor(msg[h][:, :, :, 0:HD],
                                              rows[u][:, h * HK:(h + 1) * HK, 0:D].rearrange("p k (h d) -> p k h d", h=H),
                                              spread(msg[h][:, :, :, HD:], [P, HK, H, HD]), ALU.mult).then_inc(msg_ready, 1)
                        dve.wait_ge(main_done, 2 * t + 4)
                        dve.wait_ge(fade_ready, t + 1)
                        for n in range(H):
                            a_n = c.acc[:, ds(b, 1), n * A:(n + 1) * A].rearrange("p a d -> p (a d)")
                            last = dve.scalar_tensor_tensor(a_n, a_n, fade[:, 1, n:n + 1], accp[:, n * A:(n + 1) * A], ALU.mult, ALU.add)
                        last.then_inc(acc_added, 1)
                        ch.end()
                        dve.reg_add(r, r, 1)
                    dve.wait_ge(msg_ready, dve.snap(r) * 2)
                    dve.sem_inc(rows_free, 1)
            dve.wait_ge(acc_added, dve.snap(r))
            parts = c.acc[:, :, :].rearrange("p t (h a) -> p (t h) a", a=A)
            fin = Chain(dve, final_step)
            fin.link(dve.tensor_scalar(parts[:, :, HD:], parts[:, :, HD:], 1e-30, None, ALU.max))
            fin.link(dve.reciprocal(parts[:, :, HD:], parts[:, :, HD:]))
            dve.tensor_tensor(parts[:, :, 0:HD], parts[:, :, 0:HD], spread(parts[:, :, HD:], [P, T * H, HD]), ALU.mult)


def aggregate(c, tab):
    nc, z = c.nc, c.z
    K, HK, D = z.K, z.HK, z.D
    c.phase = "aggregate"
    with ExitStack() as ctx:
        s = lambda n: c.sem(ctx, n)
        rows = [c.sb(ctx, f"rows{u}", [P, K, D]) for u in range(2)]
        idx = [c.sb(ctx, f"idx{u}", [P, K], I32) for u in range(2)]
        dl = c.sb(ctx, "dl", [P, K])
        oh = [c.sb(ctx, f"oh{h}", [P, HK, P]) for h in range(2)]
        accp = c.ps(ctx, "accp", [P, 512])
        gathered = [[s(f"gathered{u}{h}") for h in range(2)] for u in range(2)]
        names = ("idx_ready", "rows_free", "dve_step", "onehot_ready", "main_done", "acc_added", "cleared")
        idx_ready, rows_free, dve_step, onehot_ready, main_done, acc_added, cleared = (s(n) for n in names)
        block = ctx.enter_context(nc.Block())

        @block.gpsimd
        def _(pool):
            gather_rows(c, pool, tab, idx, rows, idx_ready, rows_free, gathered)

        @block.scalar
        def _(act):
            copy_indices(c, act, 0, idx, 0).then_inc(idx_ready, 1)
            with act.Fori(0, z.NB // 2) as i:
                for u in range(2):
                    for h in range(2):
                        act.wait_ge(gathered[1 - u][h], (i + u) * 16 * HK)
                    alone(c, act)
                    copy_indices(c, act, 2 * i + u + 1, idx, 1 - u).then_inc(idx_ready, 1)

        @block.tensor
        def _(pe):
            pe.sem_inc(main_done, 2)
            r = pe.alloc_register(f"{c.phase}_pairs")
            pe.reg_mov(r, 0)
            pe.sem_inc(rows_free, 2)
            with pe.Fori(0, z.NB // 2) as i:
                for u in range(2):
                    lo, hi = load_span(pe, c, 2 * i + u)
                    with pe.Fori(lo, hi) as b:
                        t = pe.snap(r)
                        pe.wait_ge(acc_added, t)
                        for h in range(2):
                            pe.wait_ge(onehot_ready, 2 * t + h + 1)
                            pe.wait_ge(gathered[u][h], (i + 1) * 16 * HK)
                            for k in range(HK):
                                last = pe.matmul(accp[:, 0:D], oh[h][:, k, :], rows[u][:, h * HK + k, :],
                                                 start=(h == 0 and k == 0), stop=(h == 1 and k == HK - 1))
                            last.then_inc(main_done, 1)
                        pe.reg_add(r, r, 1)
                    pe.wait_ge(main_done, pe.snap(r) * 2 + 2)
                    pe.sem_inc(rows_free, 1)

        @block.vector
        def _(dve):
            dve.memset(c.acc[:, :, :], 0.0).then_inc(cleared, 1)
            dve.wait_ge(cleared, 1)
            ch = Chain(dve, dve_step, 1)
            r = dve.alloc_register(f"{c.phase}_pairs")
            dve.reg_mov(r, 0)
            with dve.Fori(0, z.NB // 2) as i:
                for u in range(2):
                    sc = 2 * i + u
                    lo, hi = load_span(dve, c, sc)
                    with dve.Fori(lo, hi) as b:
                        t = dve.snap(r)
                        ch.begin(t)
                        ch.link(dve.tensor_scalar(dl[:, :], c.dst_all[:, ds(sc * K, K)], c.base[:, ds(b, 1)], None, ALU.subtract))
                        for h in range(2):
                            dve.wait_ge(main_done, 2 * t + h + 1)
                            dve.tensor_tensor(oh[h][:, :, :], spread(c.iota[:, :].unsqueeze(1), [P, HK, P]),
                                              spread(dl[:, h * HK:(h + 1) * HK].unsqueeze(2), [P, HK, P]),
                                              ALU.is_equal).then_inc(onehot_ready, 1)
                        ch.end()
                        dve.wait_ge(main_done, 2 * t + 4)
                        a_b = c.acc[:, ds(b, 1), 0:D].rearrange("p a d -> p (a d)")
                        dve.tensor_tensor(a_b, a_b, accp[:, 0:D], ALU.add).then_inc(acc_added, 1)
                        dve.reg_add(r, r, 1)


def combine(c, xt_all, gate, gate_b, conv=None):
    nc, z = c.nc, c.z
    G, KC, D, X, H, HD, A, W = z.G, z.KC, z.D, z.X, z.H, z.HD, z.A, z.W
    NTP = 3 if conv else 1
    c.phase = "combine_sums" if conv else "combine_attention"
    with ExitStack() as ctx:
        s = lambda n: c.sem(ctx, n)
        stats = c.sb(ctx, "stats", [P, G, 6])
        mv = c.sb(ctx, "mv", [P, G, 2])
        sd = c.sb(ctx, "sd", [P, G])
        rstd = c.sb(ctx, "rstd", [P, G])
        xn = c.sb(ctx, "xn", [P, G, D])
        xt = c.sb(ctx, "xt", [P, G, KC, P])
        lg = c.sb(ctx, "lg", [P, G, X])
        red = c.sb(ctx, "red", [P, G])
        gt = c.sb(ctx, "gt", [P, G, X, X])
        eq = c.sb(ctx, "eq", [P, G, X, X])
        gw = c.sb(ctx, "gw", [P, KC, X])
        gb = c.sb(ctx, "gb", [1, X])
        if conv:
            cw = c.sb(ctx, "conv_w", [P, 2, KC, D])
            sums = c.sb(ctx, "sums", [P, G, D])
            st = c.sb(ctx, "st", [P, G, KC, P])
        tp = [c.ps(ctx, f"tp{i}", [P, KC, P]) for i in range(2)]
        cv = [c.ps(ctx, f"cv{i}", [P, 512]) for i in range(2)]
        lgp = c.ps(ctx, "lgp", [P, G, X])
        names = ("dve_step", "var_ready", "sd_ready", "xn_ready", "sums_ready", "turned", "xt_ready", "cv_ready",
                 "res_ready", "lg_ready", "lg_used", "e_ready", "xt_out", "w_in")
        (dve_step, var_ready, sd_ready, xn_ready, sums_ready, turned, xt_ready, cv_ready,
         res_ready, lg_ready, lg_used, e_ready, xt_out, w_in) = (s(n) for n in names)
        block = ctx.enter_context(nc.Block())
        NW = 4 if conv else 2

        @block.sync
        def _(sp):
            sp.dma_start(gw[:, :, :], gate.rearrange("(k p) e -> p k e", p=P)).then_inc(w_in, 16)
            sp.dma_start(gb[:, :], gate_b.rearrange("(o e) -> o e", o=1)).then_inc(w_in, 16)
            for n, w in enumerate(conv or ()):
                sp.dma_start(cw[:, n, :, :], w.rearrange("(k p) d -> p k d", p=P)).then_inc(w_in, 16)
            sp.wait_ge(w_in, 16 * NW)

        rounds = [(xn, xt), (sums, st), (xn, xt)] if conv else [(xn, xt)]

        @block.tensor
        def _(pe):
            pe.wait_ge(w_in, 16 * NW)
            with pe.Fori(0, z.NG) as g:
                for n, (from_, _) in enumerate(rounds):
                    if n == NTP - 1:
                        pe.wait_ge(xn_ready, g * (2 if conv else 1) + (2 if conv else 1))
                    elif n == 0:
                        pe.wait_ge(xn_ready, g * 2 + 1)
                    else:
                        pe.wait_ge(sums_ready, g + 1)
                    for j in range(G):
                        q = n * G + j
                        pe.wait_ge(xt_ready, g * G * NTP + max(q - 1, 0))
                        for k in range(KC):
                            last = pe.transpose(tp[q % 2][:, k, :], from_[:, j, k * P:(k + 1) * P], c.ident[:, :])
                        last.then_inc(turned, 1)
                    if n == 1:
                        for j in range(G):
                            pe.wait_ge(xt_ready, g * G * NTP + G + j + 1)
                            pe.wait_ge(res_ready, g * G + max(j - 1, 0))
                            for m, a in enumerate((xt, st)):
                                for k in range(KC):
                                    last = pe.matmul(cv[j % 2][:, 0:D], a[:, j, k, :], cw[:, m, k, :],
                                                     start=(m == 0 and k == 0), stop=(m == 1 and k == KC - 1))
                            last.then_inc(cv_ready, 1)
                pe.wait_ge(xt_ready, (g + 1) * G * NTP)
                pe.wait_ge(lg_used, g)
                for j in range(G):
                    for k in range(KC):
                        pe.matmul(lgp[:, j, :], xt[:, j, k, :], gw[:, k, :], start=(k == 0), stop=False)
                    last = pe.matmul(lgp[:, j, :], c.ones[0:1, :], gb[:, :], start=False, stop=True)
                last.then_inc(lg_ready, 1)

        @block.scalar
        def _(act):
            with act.Fori(0, z.NG) as g:
                def root(n):
                    act.wait_ge(var_ready, g * 2 + n)
                    act.activation(sd[:, :], mv[:, :, 1], ACT.Sqrt, bias=c.eps[:, 0:1]).then_inc(sd_ready, 1)
                root(1)
                act.wait_ge(lg_ready, g)
                act.wait_ge(xt_out, g)
                for n, (_, to) in enumerate(rounds):
                    if n == NTP - 1:
                        root(2)
                        if conv:
                            act.wait_ge(cv_ready, (g + 1) * G)
                    for j in range(G):
                        q = n * G + j
                        act.wait_ge(turned, g * G * NTP + q + 1)
                        act.activation(to[:, j, :, :], tp[q % 2][:, :, :], ACT.Copy).then_inc(xt_ready, 1)
                act.wait_ge(lg_used, g + 1)
                act.activation(lg[:, :, :], lg[:, :, :], ACT.Exp).then_inc(e_ready, 1)

        @block.gpsimd
        def _(pool):
            with pool.Fori(0, z.NG) as g:
                pool.wait_ge(xt_ready, (g + 1) * G * NTP)
                alone(c, pool)
                for k in range(KC):
                    last = pool.tensor_copy(xt_all[:, k, ds(g * W, W)].rearrange("p (t n) -> p t n", n=P), xt[:, :, k, :])
                last.then_inc(xt_out, 1)

        @block.vector
        def _(dve):
            ch = Chain(dve, dve_step, 8 if conv else 15)
            with dve.Fori(0, z.NG) as g:
                ch.begin(g)
                group = c.res[:, ds(g * G, G), :]
                dve.wait_ge(turned, g * G * NTP)
                last = normalise(c, dve, ch, g, stats, mv, sd, rstd, xn, var_ready, sd_ready, g * 2 + 1)
                if conv:
                    last.then_inc(xn_ready, 1)
                    dve.tensor_scalar(sums[:, :, :], c.acc[:, ds(g * G, G), 0:D], 1.0, None, ALU.mult).then_inc(sums_ready, 1)
                    for j in range(G):
                        row = c.res[:, ds(g * G + j, 1), :].rearrange("p a d -> p (a d)")
                        dve.wait_ge(cv_ready, g * G + j + 1)
                        dve.scalar_tensor_tensor(row, cv[j % 2][:, 0:D], 0.0, row, ALU.max, ALU.add).then_inc(res_ready, 1)
                    dve.wait_ge(res_ready, (g + 1) * G)
                    dve.wait_ge(turned, g * G * NTP + G)
                else:
                    ch.link(last)
                    ch.link(dve.tensor_tensor(group, group, xn[:, :, :], ALU.add))
                    for j in range(G):
                        row = c.res[:, ds(g * G + j, 1), :].rearrange("p a (h d) -> p (a h) d", h=H)
                        att = c.acc[:, ds(g * G + j, 1), :].rearrange("p a (h d) -> p (a h) d", h=H)[:, :, 0:HD]
                        last = dve.tensor_tensor(row, row, att, ALU.add)
                    ch.link(last)
                normalise(c, dve, ch, g, stats, mv, sd, rstd, xn, var_ready, sd_ready, g * 2 + 2).then_inc(xn_ready, 1)
                dve.wait_ge(lg_ready, g + 1)
                ch.link(dve.tensor_reduce(red[:, :], lgp[:, :, :], AX.X, ALU.max))
                dve.tensor_tensor(lg[:, :, :], lgp[:, :, :], spread(red[:, :].unsqueeze(2), [P, G, X]), ALU.subtract).then_inc(lg_used, 1)
                dve.wait_ge(e_ready, g + 1)
                ch.link(dve.tensor_reduce(red[:, :], lg[:, :, :], AX.X, ALU.add))
                ch.link(dve.reciprocal(red[:, :], red[:, :]))
                gates = c.gates[:, ds(g * G, G), :]
                probs = gates if conv else lg[:, :, :]
                ch.link(dve.tensor_tensor(probs, lg[:, :, :], spread(red[:, :].unsqueeze(2), [P, G, X]), ALU.mult))
                if not conv:
                    mine = spread(lg[:, :, :].unsqueeze(3), [P, G, X, X])
                    other = spread(lg[:, :, :].unsqueeze(2), [P, G, X, X])
                    dve.tensor_tensor(gt[:, :, :, :], other, mine, ALU.is_gt)
                    ch.link(dve.tensor_tensor(eq[:, :, :, :], other, mine, ALU.is_equal))
                    tri = spread(c.tri[:, :, :].rearrange("p i j -> p (i j)").unsqueeze(1), [P, G, X * X])
                    ch.link(dve.tensor_tensor(eq[:, :, :, :].rearrange("p t i j -> p t (i j)"),
                                              eq[:, :, :, :].rearrange("p t i j -> p t (i j)"), tri, ALU.mult))
                    ch.link(dve.tensor_tensor(gt[:, :, :, :], gt[:, :, :, :], eq[:, :, :, :], ALU.add))
                    ch.link(dve.tensor_reduce(eq[:, :, :, 0], gt[:, :, :, :], AX.X, ALU.add))
                    dve.scalar_tensor_tensor(gates, eq[:, :, :, 0], 1.5, lg[:, :, :], ALU.is_lt, ALU.mult)
                ch.end()


def experts_gelu(c, xt_all, w1, b1, w2, b2):
    nc, z = c.nc, c.z
    G, KC, HC, D, F, X, W, HW, NG = z.G, z.KC, z.HC, z.D, z.F, z.X, z.W, z.HW, z.NG
    UP = 2 * HC
    c.phase = "experts_gelu"
    with ExitStack() as ctx:
        s = lambda n: c.sem(ctx, n)
        w1s = [c.sb(ctx, f"w1s{u}", [P, KC, F]) for u in range(2)]
        w2s = [c.sb(ctx, f"w2s{u}", [P, HC, D]) for u in range(2)]
        b1s = [c.sb(ctx, f"b1s{u}", [P, HC]) for u in range(2)]
        b2s = [c.sb(ctx, f"b2s{u}", [1, D]) for u in range(2)]
        ht = c.sb(ctx, "ht", [P, HC, W])
        up = [c.ps(ctx, f"up{i}", [P, 512]) for i in range(4)]
        yp = [c.ps(ctx, f"yp{i}", [P, 512]) for i in range(2)]
        w_in = [s(f"w_in{u}") for u in range(2)]
        up_ready, h_ready, y_ready, y_added = (s(n) for n in ("up_ready", "h_ready", "y_ready", "y_added"))
        block = ctx.enter_context(nc.Block())

        @block.sync
        def _(sp):
            def load(e, u):
                sp.dma_start(w1s[u][:, :, :], w1[ds(e, 1), :, :].rearrange("o (k p) f -> p (o k) f", p=P)).then_inc(w_in[u], 16)
                sp.dma_start(w2s[u][:, :, :], w2[ds(e, 1), :, :].rearrange("o (k p) d -> p (o k) d", p=P)).then_inc(w_in[u], 16)
                sp.dma_start(b1s[u][:, :], b1[ds(e, 1), :].rearrange("o (k p) -> p (o k)", p=P),
                             allow_slow_non_contiguous=True).then_inc(w_in[u], 16)
                sp.dma_start(b2s[u][:, :], b2[ds(e, 1), :]).then_inc(w_in[u], 16)

            load(0, 0)
            load(1, 1)
            with sp.Fori(1, X // 2) as o:
                for u in range(2):
                    sp.wait_ge(y_ready, (2 * o + u - 1) * NG * G)
                    load(2 * o + u, u)
            for u in range(2):
                sp.wait_ge(w_in[u], 64 * (X // 2))

        @block.tensor
        def _(pe):
            with pe.Fori(0, X // 2) as o:
                for u in range(2):
                    pe.wait_ge(w_in[u], (o + 1) * 64)
                    alone(c, pe)
                    with pe.Fori(0, NG) as g:
                        n = (2 * o + u) * NG + g
                        for hc in range(HC):
                            for v in range(2):
                                q = 2 * hc + v
                                pe.wait_ge(h_ready, n * UP + max(q - 3, 0))
                                for k in range(KC):
                                    last = pe.matmul(up[q % 4][:, 0:HW], w1s[u][:, k, hc * P:(hc + 1) * P],
                                                     xt_all[:, k, ds(g * W + v * HW, HW)], start=(k == 0), stop=(k == KC - 1))
                                last.then_inc(up_ready, 1)
                        pe.wait_ge(h_ready, (n + 1) * UP)
                        for j in range(G):
                            pe.wait_ge(y_added, n * G + max(j - 1, 0))
                            for hc in range(HC):
                                pe.matmul(yp[j % 2][:, 0:D], ht[:, hc, j * P:(j + 1) * P], w2s[u][:, hc, :], start=(hc == 0), stop=False)
                            pe.matmul(yp[j % 2][:, 0:D], c.ones[0:1, :], b2s[u][:, :], start=False, stop=True).then_inc(y_ready, 1)

        @block.scalar
        def _(act):
            with act.Fori(0, X // 2) as o:
                for u in range(2):
                    act.wait_ge(w_in[u], (o + 1) * 64)
                    with act.Fori(0, NG) as g:
                        n = (2 * o + u) * NG + g
                        act.wait_ge(y_ready, n * G)
                        for q in range(UP):
                            act.wait_ge(up_ready, n * UP + q + 1)
                            act.activation(ht[:, q // 2, (q % 2) * HW:(q % 2 + 1) * HW], up[q % 4][:, 0:HW], ACT.Gelu,
                                           bias=b1s[u][:, q // 2:q // 2 + 1]).then_inc(h_ready, 1)

        @block.vector
        def _(dve):
            with dve.Fori(0, X) as e:
                with dve.Fori(0, NG) as g:
                    n = e * NG + g
                    for j in range(G):
                        row = c.res[:, ds(g * G + j, 1), :].rearrange("p a d -> p (a d)")
                        gate = c.gates[:, ds(g * G + j, 1), ds(e, 1)].rearrange("p a e -> p (a e)")
                        dve.wait_ge(y_ready, n * G + j + 1)
                        if j == 0:
                            dve.wait_ge(y_added, n * G)
                        dve.scalar_tensor_tensor(row, yp[j % 2][:, 0:D], gate, row, ALU.mult, ALU.add).then_inc(y_added, 1)


def store_norms(c, tab):
    nc, z = c.nc, c.z
    G = z.G
    c.phase = "store_norms"
    with ExitStack() as ctx:
        s = lambda n: c.sem(ctx, n)
        stats = c.sb(ctx, "stats", [P, G, 6])
        mv = c.sb(ctx, "mv", [P, G, 2])
        sd = c.sb(ctx, "sd", [P, G])
        rstd = c.sb(ctx, "rstd", [P, G])
        xn = c.sb(ctx, "xn", [P, G, z.D])
        dve_step, var_ready, sd_ready, xn_ready, stored = (s(n) for n in ("dve_step", "var_ready", "sd_ready", "xn_ready", "stored"))
        block = ctx.enter_context(nc.Block())

        @block.vector
        def _(dve):
            ch = Chain(dve, dve_step, 2)
            with dve.Fori(0, z.NG) as g:
                ch.begin(g)
                dve.wait_ge(stored, g * 16)
                normalise(c, dve, ch, g, stats, mv, sd, rstd, xn, var_ready, sd_ready, g + 1).then_inc(xn_ready, 1)
                ch.end()

        @block.scalar
        def _(act):
            with act.Fori(0, z.NG) as g:
                act.wait_ge(var_ready, g + 1)
                act.activation(sd[:, :], mv[:, :, 1], ACT.Sqrt, bias=c.eps[:, 0:1]).then_inc(sd_ready, 1)

        @block.sync
        def _(sp):
            with sp.Fori(0, z.NG) as g:
                sp.wait_ge(xn_ready, g + 1)
                sp.dma_start(tab[ds(g * z.W, z.W), :].rearrange("(t p) d -> p t d", p=P), xn[:, :, :]).then_inc(stored, 16)
            sp.wait_ge(stored, z.NG * 16)


def experts_deep(c, xt_all, w1, w2, wo, bo, bn_out, out):
    nc, z = c.nc, c.z
    G, KC, D, X, W, HW, NG, F2 = z.G, z.KC, z.D, z.X, z.W, z.HW, z.NG, z.F2
    HC = F2 // P
    UP = 2 * HC
    c.phase = "experts_deep"
    with ExitStack() as ctx:
        s = lambda n: c.sem(ctx, n)
        w1s = [c.sb(ctx, f"w1s{u}", [P, KC, F2]) for u in range(2)]
        w2s = [c.sb(ctx, f"w2s{u}", [P, HC, F2]) for u in range(2)]
        wos = [c.sb(ctx, f"wos{u}", [P, HC, D]) for u in range(2)]
        aff = [c.sb(ctx, f"aff{u}", [P, 2, 2, HC]) for u in range(2)]
        bos = [c.sb(ctx, f"bos{u}", [1, D]) for u in range(2)]
        hid = [c.sb(ctx, f"hid{n}", [P, HC, W]) for n in range(2)]
        up = [c.ps(ctx, f"up{i}", [P, 512]) for i in range(4)]
        yp = [c.ps(ctx, f"yp{i}", [P, 512]) for i in range(2)]
        w_in = [s(f"w_in{u}") for u in range(2)]
        up_ready, h_ready, y_ready, y_added, stored = (s(n) for n in ("up_ready", "h_ready", "y_ready", "y_added", "stored"))
        block = ctx.enter_context(nc.Block())
        NL = 8

        @block.sync
        def _(sp):
            def load(e, u):
                for to, w in ((w1s, w1), (w2s, w2), (wos, wo)):
                    sp.dma_start(to[u][:, :, :], w[ds(e, 1), :, :].rearrange("o (k p) f -> p (o k) f", p=P)).then_inc(w_in[u], 16)
                for n in range(2):
                    for m in range(2):
                        sp.dma_start(aff[u][:, n, m, :], bn_out[n][m][ds(e, 1), :, :].rearrange("o p k -> p (o k)")).then_inc(w_in[u], 16)
                sp.dma_start(bos[u][:, :], bo[ds(e, 1), :]).then_inc(w_in[u], 16)

            load(0, 0)
            load(1, 1)
            with sp.Fori(1, X // 2) as o:
                for u in range(2):
                    sp.wait_ge(y_ready, (2 * o + u - 1) * NG * G)
                    load(2 * o + u, u)
            for u in range(2):
                sp.wait_ge(w_in[u], 16 * NL * (X // 2))
            sp.wait_ge(y_added, X * NG * G)
            sp.dma_start(out[0:(z.T - 1) * P, :].rearrange("(t p) d -> p t d", p=P), c.res[:, 0:z.T - 1, :]).then_inc(stored, 16)
            sp.dma_start(out[(z.T - 1) * P:z.N, :], c.res[0:z.LAST, z.T - 1, :]).then_inc(stored, 16)
            sp.wait_ge(stored, 32)

        @block.tensor
        def _(pe):
            with pe.Fori(0, X // 2) as o:
                for u in range(2):
                    pe.wait_ge(w_in[u], (o + 1) * 16 * NL)
                    alone(c, pe)
                    with pe.Fori(0, NG) as g:
                        n = (2 * o + u) * NG + g
                        for layer in range(2):
                            for hc in range(HC):
                                for v in range(2):
                                    q = layer * UP + 2 * hc + v
                                    pe.wait_ge(h_ready, n * 2 * UP + (max(q - 3, 0) if layer == 0 else UP))
                                    for k in range(KC):
                                        moving = xt_all[:, k, ds(g * W + v * HW, HW)] if layer == 0 else hid[0][:, k, v * HW:(v + 1) * HW]
                                        last = pe.matmul(up[q % 4][:, 0:HW], (w1s if layer == 0 else w2s)[u][:, k, hc * P:(hc + 1) * P],
                                                         moving, start=(k == 0), stop=(k == KC - 1))
                                    last.then_inc(up_ready, 1)
                        pe.wait_ge(h_ready, (n + 1) * 2 * UP)
                        for j in range(G):
                            pe.wait_ge(y_added, n * G + max(j - 1, 0))
                            for hc in range(HC):
                                pe.matmul(yp[j % 2][:, 0:D], hid[1][:, hc, j * P:(j + 1) * P], wos[u][:, hc, :], start=(hc == 0), stop=False)
                            pe.matmul(yp[j % 2][:, 0:D], c.ones[0:1, :], bos[u][:, :], start=False, stop=True).then_inc(y_ready, 1)

        @block.scalar
        def _(act):
            with act.Fori(0, X // 2) as o:
                for u in range(2):
                    act.wait_ge(w_in[u], (o + 1) * 16 * NL)
                    with act.Fori(0, NG) as g:
                        n = (2 * o + u) * NG + g
                        act.wait_ge(y_ready, n * G)
                        for q in range(2 * UP):
                            layer, hc, v = q // UP, q % UP // 2, q % 2
                            act.wait_ge(up_ready, n * 2 * UP + q + 1)
                            act.activation(hid[layer][:, hc, v * HW:(v + 1) * HW], up[q % 4][:, 0:HW], ACT.Relu,
                                           scale=aff[u][:, layer, 0, hc:hc + 1], bias=aff[u][:, layer, 1, hc:hc + 1]).then_inc(h_ready, 1)

        @block.vector
        def _(dve):
            with dve.Fori(0, X) as e:
                with dve.Fori(0, NG) as g:
                    n = e * NG + g
                    for j in range(G):
                        row = c.res[:, ds(g * G + j, 1), :].rearrange("p a d -> p (a d)")
                        gate = c.gates[:, ds(g * G + j, 1), ds(e, 1)].rearrange("p a e -> p (a e)")
                        dve.wait_ge(y_ready, n * G + j + 1)
                        if j == 0:
                            dve.wait_ge(y_added, n * G)
                        dve.scalar_tensor_tensor(row, yp[j % 2][:, 0:D], gate, row, ALU.mult, ALU.add).then_inc(y_added, 1)


def gnn_experts(nc, a, out, phases=99):
    z = Shapes(a["x"], a["src"], a["L0_gnn_W"], a["L0_gnn_attn_src"], a["L0_gnn_pos_attn_src"],
               a["L0_ffn_W1"], a["L0_ffn_W2"], a["L1_ffn_Wr"], a["L1_ffn_v1"])
    c = Core(nc, z)
    dram = lambda name, shape, dt=F32: nc.dram_tensor(name, shape, dt, kind="Internal").ap()
    tab0 = dram("rows_attention", (z.T * P, z.D + z.H))
    scores = dram("scores", (z.T * P, 2 * z.H))
    tab1 = dram("rows_sums", (z.T * P, z.D))
    c.span_d = dram("spans_dram", (z.NB, 2), I32)
    bn_out = [[dram(f"bn{n}{m}", (z.X, P, z.F2 // P)) for m in range(2)] for n in range(2)]
    with ExitStack() as ctx:
        c.pace = c.sem(ctx, "pace")
        c.res = c.sb(ctx, "res", [P, z.T, z.D])
        c.gates = c.sb(ctx, "gates", [P, z.T, z.X])
        c.ident = c.sb(ctx, "ident", [P, P])
        c.ones = c.sb(ctx, "ones", [1, P])
        c.eps = c.sb(ctx, "eps", [P, 2])
        c.tri = c.sb(ctx, "tri", [P, z.X, z.X])
        c.sel = c.sb(ctx, "sel", [P, z.H, P])
        c.iota = c.sb(ctx, "iota", [P, P])
        c.base = c.sb(ctx, "base", [P, z.T])
        c.spans = c.sb(ctx, "spans", [1, 2 * z.NB], I32)
        c.src_all = c.sb(ctx, "src_all", [P, (z.NB + 1) * z.K], I32)
        c.dst_all = c.sb(ctx, "dst_all", [P, z.NB * z.K])
        c.wall = c.sb(ctx, "wall", [P, z.KC, z.D + 2 * z.H])
        bn_in = [[a[f"L1_ffn_{n}{i}"] for n in ("b", "g", "be", "m", "v")] for i in (1, 2)]
        prepare(c, a["x"], a["src"], a["dst"], a["L0_gnn_W"], a["L0_gnn_attn_src"], a["L0_gnn_attn_dst"],
                a["L0_gnn_pos_attn_src"], a["L0_gnn_pos_attn_dst"], bn_in, bn_out)
        if phases > 1:
            project(c, tab0, scores)
        for layer in range(2):
            with ExitStack() as inner:
                c.phase = f"layer{layer}"
                c.acc = c.sb(inner, "acc", [P, z.T, z.H * z.A])
                if layer == 0:
                    if phases > 2:
                        attend(c, tab0, scores)
                elif phases > 6:
                    aggregate(c, tab1)
                c.phase = f"layer{layer}"
                c.xt_all = c.sb(inner, "xt_all", [P, z.KC, z.T * P])
                if layer == 0 and phases > 3:
                    combine(c, c.xt_all, a["L0_ffn_gate_w"], a["L0_ffn_gate_b"])
                if layer == 1 and phases > 7:
                    combine(c, c.xt_all, a["L1_ffn_Wr"], a["L1_ffn_br"], (a["L1_gnn_W"], a["L1_gnn_M"]))
                if layer == 0 and phases > 4:
                    experts_gelu(c, c.xt_all, a["L0_ffn_W1"], a["L0_ffn_b1"], a["L0_ffn_W2"], a["L0_ffn_b2"])
                if layer == 0 and phases > 5:
                    store_norms(c, tab1)
                if layer == 1 and phases > 8:
                    experts_deep(c, c.xt_all, a["L1_ffn_W1"], a["L1_ffn_W2"], a["L1_ffn_Wo"], a["L1_ffn_bo"], bn_out, out)


_INS = ["x", "src", "dst", "L0_gnn_W", "L0_gnn_attn_src", "L0_gnn_attn_dst", "L0_gnn_pos_attn_src", "L0_gnn_pos_attn_dst",
        "L0_ffn_gate_w", "L0_ffn_gate_b", "L0_ffn_W1", "L0_ffn_b1", "L0_ffn_W2", "L0_ffn_b2", "L1_gnn_W", "L1_gnn_M",
        "L1_ffn_Wr", "L1_ffn_br", "L1_ffn_W1", "L1_ffn_b1", "L1_ffn_g1", "L1_ffn_be1", "L1_ffn_m1", "L1_ffn_v1",
        "L1_ffn_W2", "L1_ffn_b2", "L1_ffn_g2", "L1_ffn_be2", "L1_ffn_m2", "L1_ffn_v2", "L1_ffn_Wo", "L1_ffn_bo"]


def kernel(**inputs):
    import numpy as np
    import concourse.bacc as bacc
    from concourse.bass_utils import run_bass_kernel_spmd

    nc = bacc.Bacc("TRN2", target_bir_lowering=False, num_devices=1)
    arrays, args = {}, {}
    for name in _INS:
        a = np.ascontiguousarray(inputs[name])
        arrays[f"in_{name}"] = a
        args[name] = nc.dram_tensor(f"in_{name}", a.shape, mybir.dt.from_np(a.dtype), kind="ExternalInput").ap()
    out = nc.dram_tensor("out", args["x"].shape, F32, kind="ExternalOutput").ap()
    gnn_experts(nc, args, out)
    r = run_bass_kernel_spmd(nc, [arrays], core_ids=[0])
    return r.results[0]["out"]
```

```python
from contextlib import ExitStack

import concourse.bass as bass
from concourse import mybir

F32 = mybir.dt.float32
BF16 = mybir.dt.bfloat16
I32 = mybir.dt.int32
ALU = mybir.AluOpType
ACT = mybir.ActivationFunctionType
AX = mybir.AxisListType
ds = bass.ds

P = 128
LN_EPS = 1e-5
BN_EPS = 0.001
NEG_SLOPE = 0.2
FAR = 1e30
SPREAD = 60.0


class Shapes:

    def __init__(self, x, src, w0, attn, pos, w1, w2, wr, v1):
        self.N, self.D = x.shape
        self.E = src.shape[0]
        self.C = w0.shape[0]
        self.H, self.HD = attn.shape[1:]
        self.PD = pos.shape[2]
        self.X, _, self.F = w1.shape
        self.X2, self.F2 = v1.shape
        self.T = -(-self.N // P)
        self.G = 7
        self.NG = self.T // self.G
        self.W = self.G * P
        self.HW = self.W // 2
        self.LAST = self.N - (self.T - 1) * P
        self.KC = self.D // P
        self.HC = self.F // P
        self.K = 8
        self.HK = self.K // 2
        self.B = P * self.K
        self.NB = 2 * -(-self.E // (2 * self.B))
        self.A = self.HD + 1
        assert self.T % self.G == 0 and self.D % P == 0 and self.H * self.HD == self.D
        assert self.C + self.PD == self.D and self.HW <= 512 and self.X == self.X2


class Chain:

    def __init__(self, eng, sem, per=0):
        self.eng, self.sem, self.per, self.base, self.n = eng, sem, per, 0, 0

    def begin(self, i):
        self.base, self.n = i * self.per, 0

    def link(self, ins):
        self.n += 1
        ins.then_inc(self.sem, 1)
        self.eng.wait_ge(self.sem, self.base + self.n)

    def end(self):
        assert self.n == self.per, (self.n, self.per)


class Core:

    def __init__(self, nc, z):
        self.nc, self.z, self.phase = nc, z, "all"

    def sb(self, ctx, name, shape, dt=F32):
        return ctx.enter_context(self.nc.sbuf_tensor(f"{self.phase}_{name}", shape, dt))

    def ps(self, ctx, name, shape, dt=F32):
        bank = ctx.enter_context(self.nc.psum_tensor(f"{self.phase}_{name}", [P, 2048 // (2 if dt == BF16 else 4)], dt))
        if len(shape) == 2:
            return bank[:, 0:shape[1]]
        size = 1
        for n in shape[1:]:
            size *= n
        names = "abcd"[:len(shape) - 1]
        sizes = dict(zip(names, shape[1:]))
        return bank[:, 0:size].rearrange(f"p ({' '.join(names)}) -> p {' '.join(names)}", **sizes)

    def sem(self, ctx, name):
        return ctx.enter_context(self.nc.semaphore(f"{self.phase}_{name}"))


def alone(c, eng):
    eng.sem_inc(c.pace, 1)


def spread(ap, shape):
    return ap.broadcast_to(shape)


def prepare(c, x, src, dst, w0, attn_src, attn_dst, pos_src, pos_dst, bn_in, bn_out):
    nc, z = c.nc, c.z
    T, K, NB, B, H, HD, KC, X = z.T, z.K, z.NB, z.B, z.H, z.HD, z.KC, z.X
    NT = -(-NB // P)
    full, rest = z.E // B, z.E % B
    c.phase = "prepare"
    with ExitStack() as ctx:
        s = lambda n: c.sem(ctx, n)
        posw = c.sb(ctx, "posw", [P, KC, 2 * H])
        ablk = c.sb(ctx, "ablk", [P, KC, 2 * H])
        wt = c.sb(ctx, "wt", [P, KC, KC * P])
        edge_i = c.sb(ctx, "edge_i", [P, 2, NT, B], I32)
        edge_f = c.sb(ctx, "edge_f", [P, 2, NT, B])
        span_i = c.sb(ctx, "span_i", [P, NT, 2], I32)
        iota_i = c.sb(ctx, "iota_i", [P, P], I32)
        base_i = c.sb(ctx, "base_i", [P, T], I32)
        bn = c.sb(ctx, "bn", [P, 2, 5, X, z.F2 // P])
        tmp = c.sb(ctx, "bn_tmp", [P, 2, X, z.F2 // P])
        tp = [c.ps(ctx, f"tp{i}", [P, 512]) for i in range(2)]
        wa = c.ps(ctx, "wa", [P, KC, 2 * H])
        x_in, w_in, e_in, bn_ld = s("x_in"), s("w_in"), s("e_in"), s("bn_ld")
        cleared, pool_step, consts, edges_f, dve_step = s("cleared"), s("pool_step"), s("consts"), s("edges_f"), s("dve_step")
        turned, copied, span_out, span_in, wa_ready, sd_ready, bn_ready, bn_st = (
            s("turned"), s("copied"), s("span_out"), s("span_in"), s("wa_ready"), s("sd_ready"), s("bn_ready"), s("bn_st"))
        tmp_out = [[bn[:, n, 1, :, :], bn[:, n, 2, :, :]] for n in range(2)]
        block = ctx.enter_context(nc.Block())

        @block.gpsimd
        def _(pool):
            pool.memset(c.wall[:, :, :], 0.0)
            pool.memset(posw[:, :, :], 0.0)
            pool.memset(ablk[:, :, :], 0.0)
            pool.memset(c.res[:, T - 1, :], 0.0)
            pool.memset(edge_i[:, 0, NT - 1, :], 0)
            pool.memset(edge_i[:, 1, NT - 1, :], T * P + 1).then_inc(cleared, 1)
            pool.memset(c.src_all[:, NB * K:(NB + 1) * K], 0)
            pool.memset(c.ident[:, :], 0.0)
            pool.memset(c.ones[:, :], 1.0)
            pool.memset(c.tri[:, :, :], 0.0)
            pool.memset(c.sel[:, :, :], 0.0)
            pool.memset(c.eps[:, 0:1], LN_EPS)
            pool.memset(c.eps[:, 1:2], BN_EPS)
            pool.iota(iota_i[:, :], pattern=[[1, P]], base=0, channel_multiplier=0)
            pool.iota(base_i[:, :], pattern=[[P, T]], base=0, channel_multiplier=0).then_inc(pool_step, 1)
            pool.wait_ge(pool_step, 1)
            pool.affine_select(out=c.ident[:, :], in_=c.ident[:, :], compare_op=ALU.not_equal, fill=1.0,
                               base=0, pattern=[[-1, P]], channel_multiplier=1)
            pool.affine_select(out=c.tri[:, :, :], in_=c.tri[:, :, :], compare_op=ALU.is_ge, fill=1.0,
                               base=0, pattern=[[-1, X], [1, X]], channel_multiplier=0)
            pool.affine_select(out=c.sel[:, :, :], in_=c.sel[:, :, :], compare_op=ALU.not_equal, fill=1.0,
                               base=0, pattern=[[-1, H], [0, P]], channel_multiplier=1).then_inc(consts, 1)

        @block.sync
        def _(sp):
            sp.wait_ge(cleared, 1)
            for n, e in enumerate((src, dst)):
                for t in range(NT):
                    rows = min(full - t * P, P)
                    sp.dma_start(edge_i[0:rows, n, t, :],
                                 e[t * P * B:(t * P + rows) * B].rearrange("(s e) -> s e", e=B)).then_inc(e_in, 16)
                    if rows < P and rest:
                        sp.dma_start(edge_i[rows:rows + 1, n, t, 0:rest],
                                     e[full * B:z.E].rearrange("(s e) -> s e", s=1)).then_inc(e_in, 16)
            sp.dma_start(c.wall[:, 0, 0:z.D], w0[0:P, :]).then_inc(w_in, 16)
            sp.dma_start(c.wall[0:z.C - P, 1, 0:z.D], w0[P:z.C, :]).then_inc(w_in, 16)
            for n, a in enumerate((attn_src, attn_dst)):
                for h in range(H):
                    at = h * HD
                    sp.dma_start(ablk[at % P:at % P + HD, at // P, n * H + h:n * H + h + 1],
                                 a[0, h, :].rearrange("(d o) -> d o", o=1)).then_inc(w_in, 16)
            for n, a in enumerate((pos_src, pos_dst)):
                sp.dma_start(posw[z.C - P:P, 1, n * H:(n + 1) * H],
                             a[0, :, :].rearrange("h p -> p h"), allow_slow_non_contiguous=True).then_inc(w_in, 16)
            for n, layer in enumerate(bn_in):
                for m, a in enumerate(layer):
                    for e in range(X):
                        sp.dma_start(bn[:, n, m, e, :], a[e, :].rearrange("(k p) -> p k", p=P),
                                     allow_slow_non_contiguous=True).then_inc(bn_ld, 16)
            sp.wait_ge(dve_step, 4)
            for t in range(NT):
                rows = min(NB - t * P, P)
                sp.dma_start(c.span_d[t * P:t * P + rows, :], span_i[0:rows, t, :]).then_inc(span_out, 16)
            sp.wait_ge(span_out, 16 * NT)
            sp.dma_start(c.spans[0:1, :], c.span_d.rearrange("(o s) c -> o (s c)", o=1)).then_inc(span_in, 16)
            sp.wait_ge(bn_ready, 1)
            for n in range(2):
                for m in range(2):
                    sp.dma_start(bn_out[n][m].rearrange("e p k -> p e k"), tmp_out[n][m]).then_inc(bn_st, 16)
            sp.wait_ge(bn_st, 16 * 4)
            sp.wait_ge(span_in, 16)
            sp.wait_ge(x_in, 32)

        @block.scalar
        def _(act):
            act.dma_start(c.res[:, 0:T - 1, :],
                          x[0:(T - 1) * P, :].rearrange("(t p) d -> p t d", p=P)).then_inc(x_in, 16)
            act.wait_ge(cleared, 1)
            act.dma_start(c.res[0:z.LAST, T - 1, :], x[(T - 1) * P:z.N, :]).then_inc(x_in, 16)
            act.wait_ge(consts, 1)
            q = 0
            for n, table in enumerate((c.src_all, c.dst_all)):
                for t in range(NT):
                    rows = min(NB - t * P, P)
                    for k in range(K):
                        act.wait_ge(turned, q + 1)
                        out = table[:, t * P * K:(t * P + rows) * K].rearrange("p (s k) -> p s k", k=K)[:, :, k]
                        act.activation(out, tp[q % 2][:, 0:rows], ACT.Copy).then_inc(copied, 1)
                        q += 1
            for j in range(KC * KC):
                act.wait_ge(turned, q + 1)
                act.activation(wt[:, j // KC, (j % KC) * P:(j % KC + 1) * P], tp[q % 2][:, 0:P], ACT.Copy).then_inc(copied, 1)
                q += 1
            act.wait_ge(bn_ld, 16 * 10 * X)
            for n in range(2):
                last = act.activation(tmp[:, n, :, :], bn[:, n, 4, :, :], ACT.Sqrt, bias=c.eps[:, 1:2])
            last.then_inc(sd_ready, 1)

        @block.tensor
        def _(pe):
            pe.wait_ge(consts, 1)
            pe.wait_ge(edges_f, 1)
            q = 0
            for n in range(2):
                for t in range(NT):
                    rows = min(NB - t * P, P)
                    for k in range(K):
                        if q >= 2:
                            pe.wait_ge(copied, q - 1)
                        pe.transpose(tp[q % 2][:, 0:rows],
                                     edge_f[0:rows, n, t, :].rearrange("s (p k) -> s p k", k=K)[:, :, k],
                                     c.ident[0:rows, 0:rows]).then_inc(turned, 1)
                        q += 1
            pe.wait_ge(w_in, 16 * (4 + 2 * H))
            for jc in range(KC):
                for kc in range(KC):
                    pe.wait_ge(copied, q - 1)
                    pe.transpose(tp[q % 2][:, 0:P], c.wall[:, kc, jc * P:(jc + 1) * P],
                                 c.ident[:, :]).then_inc(turned, 1)
                    q += 1
            pe.wait_ge(copied, q)
            for kc in range(KC):
                for jc in range(KC):
                    last = pe.matmul(wa[:, kc, :], wt[:, jc, kc * P:(kc + 1) * P], ablk[:, jc, :],
                                     start=(jc == 0), stop=(jc == KC - 1))
            last.then_inc(wa_ready, 1)

        @block.vector
        def _(dve):
            ch = Chain(dve, dve_step)
            dve.wait_ge(e_in, 16 * (2 * NT + 2))
            for n in range(2):
                last = dve.tensor_copy(edge_f[:, n, :, :], edge_i[:, n, :, :])
            last.then_inc(edges_f, 1)
            dve.wait_ge(edges_f, 1)
            last = dve.tensor_reduce(span_i[:, :, 0], edge_f[:, 1, :, :], AX.X, ALU.min)
            ch.link(dve.tensor_reduce(span_i[:, :, 1], edge_f[:, 1, :, :], AX.X, ALU.max))
            ch.link(dve.tensor_scalar(span_i[:, :, :], span_i[:, :, :], 7, None, ALU.arith_shift_right))
            ch.link(dve.tensor_scalar(span_i[:, :, 1], span_i[:, :, 1], 1.0, float(T), ALU.add, ALU.min))
            ch.link(dve.tensor_scalar(span_i[:, :, 0], span_i[:, :, 0], float(T - 1), None, ALU.min))
            dve.wait_ge(pool_step, 1)
            dve.tensor_copy(c.iota[:, :], iota_i[:, :])
            dve.tensor_copy(c.base[:, :], base_i[:, :])
            dve.wait_ge(consts, 1)
            dve.tensor_copy(c.ident_b[:, :], c.ident[:, :])
            dve.wait_ge(w_in, 16 * (4 + 2 * H))
            dve.wait_ge(wa_ready, 1)
            dve.tensor_tensor(c.wall[:, :, z.D:], wa[:, :, :], posw[:, :, :], ALU.add)
            dve.wait_ge(sd_ready, 1)
            ch.link(dve.reciprocal(tmp[:, :, :, :], tmp[:, :, :, :]))
            ch.link(dve.tensor_tensor(bn[:, :, 1, :, :], bn[:, :, 1, :, :], tmp[:, :, :, :], ALU.mult))
            ch.link(dve.tensor_tensor(bn[:, :, 0, :, :], bn[:, :, 0, :, :], bn[:, :, 3, :, :], ALU.subtract))
            ch.link(dve.tensor_tensor(bn[:, :, 0, :, :], bn[:, :, 0, :, :], bn[:, :, 1, :, :], ALU.mult))
            dve.tensor_tensor(bn[:, :, 2, :, :], bn[:, :, 0, :, :], bn[:, :, 2, :, :], ALU.add).then_inc(bn_ready, 1)


def normalise(c, dve, ch, g, stats, mv, sd, rstd, xn, var_ready, sd_ready, nth):
    z = c.z
    alone(c, dve)
    for j in range(z.G):
        last = dve.bn_stats(stats[:, j, :], c.res[:, ds(g * z.G + j, 1), :].rearrange("p a d -> p (a d)"))
    ch.link(last)
    alone(c, dve)
    for j in range(z.G):
        last = dve.bn_aggr(mv[:, j, :], stats[:, j, :])
    last.then_inc(var_ready, 1)
    dve.wait_ge(sd_ready, nth)
    ch.link(dve.reciprocal(rstd[:, :], sd[:, :]))
    dve.wait_ge(var_ready, nth)
    for j in range(z.G):
        last = dve.tensor_scalar(xn[:, j, :], c.res[:, ds(g * z.G + j, 1), :].rearrange("p a d -> p (a d)"),
                                 mv[:, j, 0:1], rstd[:, j:j + 1], ALU.subtract, ALU.mult)
    return last


def project(c, tab, scores):
    nc, z = c.nc, c.z
    G, KC, H = z.G, z.KC, z.H
    WC = z.D + 2 * H
    c.phase = "project"
    with ExitStack() as ctx:
        s = lambda n: c.sem(ctx, n)
        stats = c.sb(ctx, "stats", [P, G, 6])
        mv = c.sb(ctx, "mv", [P, G, 2])
        sd = c.sb(ctx, "sd", [P, G])
        rstd = c.sb(ctx, "rstd", [P, G])
        xn = c.sb(ctx, "xn", [P, G, z.D])
        xt = c.sb(ctx, "xt", [P, G, KC, P])
        rows = c.sb(ctx, "rows", [P, G, WC])
        tp = [c.ps(ctx, f"tp{i}", [P, KC, P]) for i in range(2)]
        ft = [c.ps(ctx, f"ft{i}", [P, 512]) for i in range(2)]
        dve_step, var_ready, sd_ready, xn_ready, turned, xt_ready, ft_ready, rows_ready, stored = (
            s(n) for n in ("dve_step", "var_ready", "sd_ready", "xn_ready", "turned", "xt_ready", "ft_ready", "rows_ready", "stored"))
        block = ctx.enter_context(nc.Block())

        @block.vector
        def _(dve):
            ch = Chain(dve, dve_step, 2)
            with dve.Fori(0, z.NG) as g:
                ch.begin(g)
                dve.wait_ge(turned, g * G)
                normalise(c, dve, ch, g, stats, mv, sd, rstd, xn, var_ready, sd_ready, g + 1).then_inc(xn_ready, 1)
                ch.end()
                dve.wait_ge(stored, g * 32)
                for j in range(G):
                    dve.wait_ge(ft_ready, g * G + j + 1)
                    dve.tensor_copy(rows[:, j, :], ft[j % 2][:, 0:WC]).then_inc(rows_ready, 1)

        @block.scalar
        def _(act):
            with act.Fori(0, z.NG) as g:
                act.wait_ge(var_ready, g + 1)
                act.activation(sd[:, :], mv[:, :, 1], ACT.Sqrt, bias=c.eps[:, 0:1]).then_inc(sd_ready, 1)
                for j in range(G):
                    act.wait_ge(turned, g * G + j + 1)
                    if j == 0:
                        act.wait_ge(ft_ready, g * G)
                    act.activation(xt[:, j, :, :], tp[j % 2][:, :, :], ACT.Copy).then_inc(xt_ready, 1)

        @block.tensor
        def _(pe):
            with pe.Fori(0, z.NG) as g:
                pe.wait_ge(xn_ready, g + 1)
                for j in range(G):
                    pe.wait_ge(xt_ready, g * G + max(j - 1, 0))
                    for k in range(KC):
                        last = pe.transpose(tp[j % 2][:, k, :], xn[:, j, k * P:(k + 1) * P], c.ident[:, :])
                    last.then_inc(turned, 1)
                for j in range(G):
                    pe.wait_ge(xt_ready, g * G + j + 1)
                    pe.wait_ge(rows_ready, g * G + max(j - 1, 0))
                    for k in range(KC):
                        last = pe.matmul(ft[j % 2][:, 0:WC], xt[:, j, k, :], c.wall[:, k, :],
                                         start=(k == 0), stop=(k == KC - 1))
                    last.then_inc(ft_ready, 1)

        @block.sync
        def _(sp):
            with sp.Fori(0, z.NG) as g:
                sp.wait_ge(rows_ready, g * G + G)
                sp.dma_start(tab[ds(g * z.W, z.W), :].rearrange("(t p) d -> p t d", p=P),
                             rows[:, :, 0:z.D + H]).then_inc(stored, 16)
                sp.dma_start(scores[ds(g * z.W, z.W), :].rearrange("(t p) d -> p t d", p=P),
                             rows[:, :, z.D:]).then_inc(stored, 16)
            sp.wait_ge(stored, z.NG * 32)


def width(c, eng):
    r = eng.alloc_register(f"{c.phase}_wide")
    eng.reg_load(r, c.wide[0:1, 0:1])
    return r


def unless_wide(c, eng):
    return eng.If_eq(width(c, eng), 0)


def if_wide(c, eng):
    return eng.If_ne(width(c, eng), 0)


def load_span(eng, c, sc):
    lo = eng.value_load(c.spans[0:1, ds(sc * 2, 1)], min_val=0, max_val=c.z.T - 1)
    hi = eng.value_load(c.spans[0:1, ds(sc * 2 + 1, 1)], min_val=1, max_val=c.z.T)
    return lo, hi


def gather_rows(c, pool, tab, idx, rows, idx_ready, rows_free, gathered):
    z = c.z
    with pool.Fori(0, z.NB // 2) as i:
        for u in range(2):
            pool.wait_ge(idx_ready, 2 * i + u + 1)
            pool.wait_ge(rows_free, 2 * i + u + 1)
            alone(c, pool)
            for k in range(z.K):
                pool.indirect_dma_start(rows[u][:, k, :], None, tab,
                                        bass.IndirectOffsetOnAxis(ap=idx[u][:, k:k + 1], axis=0)
                                        ).then_inc(gathered[u][k // z.HK], 16)


def copy_indices(c, act, sc, idx, u):
    return act.activation(idx[u][:, :], c.src_all[:, ds(sc * c.z.K, c.z.K)], ACT.Copy)


def bound_scores(c, scores):
    nc, z = c.nc, c.z
    c.phase = "bound_scores"
    T, H = z.T, z.H
    with ExitStack() as ctx:
        s = lambda n: c.sem(ctx, n)
        sc = c.sb(ctx, "scores", [P, T, 2 * H])
        neg = c.sb(ctx, "neg", [P, T, H])
        ends = c.sb(ctx, "ends", [P, 2])
        both = c.sb(ctx, "both", [2, 1])
        m = c.sb(ctx, "m", [P, T, H])
        pq = c.sb(ctx, "pq", [P, T, 2, H])
        part = c.sb(ctx, "part", [P, T, 2, H])
        wide_f = c.sb(ctx, "wide_f", [1, 1])
        tp = c.ps(ctx, "tp", [P, P])
        bp = c.ps(ctx, "bp", [P, 2])
        s_in, dve_step, ends_ready, turned, both_ready, spread_out, pq_z, pq_ready = (
            s(n) for n in ("s_in", "dve_step", "ends_ready", "turned", "both_ready", "spread_out", "pq_z", "pq_ready"))
        block = ctx.enter_context(nc.Block())

        @block.sync
        def _(sp):
            sp.dma_start(sc[:, :, :], scores.rearrange("(t p) c -> p t c", p=P)).then_inc(s_in, 16)
            sp.wait_ge(s_in, 16)

        @block.tensor
        def _(pe):
            pe.wait_ge(ends_ready, 1)
            pe.transpose(tp[0:2, :], ends[:, :], c.ident[:, :]).then_inc(turned, 1)
            pe.wait_ge(both_ready, 1)
            pe.matmul(bp[:, :], spread(both[:, :], [2, P]), c.ident[0:2, 0:2], start=True, stop=True).then_inc(spread_out, 1)

        @block.scalar
        def _(act):
            act.wait_ge(pq_z, 1)
            act.activation(pq[:, :, :, :], pq[:, :, :, :], ACT.Exp).then_inc(pq_ready, 1)

        @block.vector
        def _(dve):
            ch = Chain(dve, dve_step)
            dve.wait_ge(s_in, 16)
            ch.link(dve.tensor_scalar(neg[:, :, :], sc[:, :, 0:H], -1.0, None, ALU.mult))
            dve.tensor_reduce(ends[:, 0:1], sc[:, :, 0:H], AX.XY, ALU.max)
            dve.tensor_reduce(ends[:, 1:2], neg[:, :, :], AX.XY, ALU.max).then_inc(ends_ready, 1)
            dve.wait_ge(turned, 1)
            dve.tensor_reduce(both[:, :], tp[0:2, :], AX.X, ALU.max).then_inc(both_ready, 1)
            dve.wait_ge(spread_out, 1)
            ch.link(dve.tensor_copy(ends[:, :], bp[:, :]))
            ch.link(dve.tensor_tensor(wide_f[:, :], ends[0:1, 0:1], ends[0:1, 1:2], ALU.add))
            dve.tensor_scalar(c.wide[:, :], wide_f[:, :], SPREAD, None, ALU.is_gt)
            dve.tensor_scalar(c.less_top[:, 0:1], ends[:, 0:1], -1.0, None, ALU.mult)
            dve.tensor_scalar(c.less_top[:, 1:2], ends[:, 0:1], -NEG_SLOPE, None, ALU.mult)
            ch.link(dve.tensor_scalar(pq[:, :, 0, :], sc[:, :, H:], ends[:, 0:1], None, ALU.add))
            dve.tensor_scalar(pq[:, :, 1, :], pq[:, :, 0, :], NEG_SLOPE, None, ALU.mult)
            ch.link(dve.scalar_tensor_tensor(m[:, :, :], pq[:, :, 0, :], NEG_SLOPE, pq[:, :, 0, :], ALU.mult, ALU.max))
            for n in range(2):
                last = dve.tensor_tensor(pq[:, :, n, :], pq[:, :, n, :], m[:, :, :], ALU.subtract)
            last.then_inc(pq_z, 1)
            dve.wait_ge(pq_ready, 1)
            flat = pq[:, :, :, :].rearrange("p t n h -> p t (n h)")
            left = part[:, :, :, :].rearrange("p t n h -> p t (n h)")
            ch.link(dve.tensor_copy(c.factors[:, :, 0, :], flat))
            ch.link(dve.tensor_tensor(left, flat, c.factors[:, :, 0, :], ALU.subtract))
            ch.link(dve.tensor_copy(c.factors[:, :, 1, :], left))
            ch.link(dve.tensor_tensor(left, left, c.factors[:, :, 1, :], ALU.subtract))
            dve.tensor_copy(c.factors[:, :, 2, :], left)


def attend_bounded(c, tab):
    nc, z = c.nc, c.z
    c.phase = "attend_bounded"
    T, K, HK, H, HD, D, A = z.T, z.K, z.HK, z.H, z.HD, z.D, z.A
    MP = 2
    KP = HK // MP
    with ExitStack() as ctx:
        s = lambda n: c.sem(ctx, n)
        rows = [c.sb(ctx, f"rows{u}", [P, K, D + H]) for u in range(2)]
        idx = [c.sb(ctx, f"idx{u}", [P, K], I32) for u in range(2)]
        ab = [c.sb(ctx, f"ab{u}", [P, K, 2, H]) for u in range(2)]
        dl = [c.sb(ctx, f"dl{u}", [P, K]) for u in range(2)]
        oh = [[c.sb(ctx, f"oh{u}{h}", [P, HK, P]) for h in range(2)] for u in range(2)]
        oht = [c.sb(ctx, f"oht{h}", [P, HK * P], BF16) for h in range(2)]
        pair = [c.sb(ctx, f"pair{h}", [P, HK, 2, H]) for h in range(2)]
        msg = [c.sb(ctx, f"msg{h}", [P, HK, H, A]) for h in range(2)]
        tp = [c.ps(ctx, f"tp{h}", [P, HK * P], BF16) for h in range(2)]
        fe = [c.ps(ctx, f"fe{h}", [P, HK, 2 * H]) for h in range(2)]
        accp = c.ps(ctx, "accp", [P, 512])
        gathered = [[s(f"gathered{u}{h}") for h in range(2)] for u in range(2)]
        names = ("idx_ready", "rows_free", "ab_ready", "dve_step", "onehot_ready", "turned", "oht_ready", "fe_ready",
                 "w_ready", "msg_ready", "main_done", "acc_added", "final_step")
        (idx_ready, rows_free, ab_ready, dve_step, onehot_ready, turned, oht_ready, fe_ready,
         w_ready, msg_ready, main_done, acc_added, final_step) = (s(n) for n in names)
        block = ctx.enter_context(nc.Block())

        @block.gpsimd
        def _(pool):
            with unless_wide(c, pool):
                gather_rows(c, pool, tab, idx, rows, idx_ready, rows_free, gathered)

        @block.scalar
        def _(act):
            with unless_wide(c, act):
                copy_indices(c, act, 0, idx, 0).then_inc(idx_ready, 1)
                r = act.alloc_register(f"{c.phase}_pairs")
                act.reg_mov(r, 0)
                with act.Fori(0, z.NB // 2) as i:
                    for u in range(2):
                        sc = 2 * i + u
                        for h in range(2):
                            act.wait_ge(gathered[1 - u][h], (i + u) * 16 * HK)
                        alone(c, act)
                        copy_indices(c, act, sc + 1, idx, 1 - u).then_inc(idx_ready, 1)
                        lo, hi = load_span(act, c, sc)
                        for h in range(2):
                            act.wait_ge(gathered[u][h], (i + 1) * 16 * HK)
                        act.activation(ab[u][:, :, 0, :], rows[u][:, :, D:], ACT.Exp, bias=c.less_top[:, 0:1])
                        act.activation(ab[u][:, :, 1, :], rows[u][:, :, D:], ACT.Exp, bias=c.less_top[:, 1:2],
                                       scale=NEG_SLOPE).then_inc(ab_ready, 1)
                        with act.Fori(lo, hi) as b:
                            t = act.snap(r)
                            for h in range(2):
                                act.wait_ge(turned, 2 * t + h + 1)
                                act.activation(oht[h][:, :], tp[h][:, :], ACT.Copy).then_inc(oht_ready, 1)
                            act.reg_add(r, r, 1)

        @block.tensor
        def _(pe):
            with unless_wide(c, pe):
                pe.sem_inc(main_done, 2)
                r = pe.alloc_register(f"{c.phase}_pairs")
                pe.reg_mov(r, 0)
                with pe.Fori(0, z.NB // 2) as i:
                    for u in range(2):
                        lo, hi = load_span(pe, c, 2 * i + u)
                        with pe.Fori(lo, hi) as b:
                            t = pe.snap(r)
                            for h in range(2):
                                pe.wait_ge(onehot_ready, 2 * t + h + 1)
                                for k in range(HK):
                                    bits = oh[u][h][:, k, :].bitcast(BF16).rearrange("p (d w) -> p d w", w=2)[:, :, 1]
                                    last = pe.transpose(tp[h][:, k * P:(k + 1) * P], bits, c.ident_b[:, :])
                                last.then_inc(turned, 1)
                            for h in range(2):
                                pe.wait_ge(oht_ready, 2 * t + h + 1)
                                for k in range(HK):
                                    for n in range(3):
                                        last = pe.matmul(fe[h][:, k, :], oht[h][:, k * P:(k + 1) * P],
                                                         c.factors[:, ds(b, 1), n, :].rearrange("p a f -> p (a f)"),
                                                         start=(n == 0), stop=(n == 2))
                                last.then_inc(fe_ready, 1)
                            pe.wait_ge(acc_added, t)
                            for h in range(2):
                                for k in range(HK):
                                    if k % KP == 0:
                                        pe.wait_ge(msg_ready, 2 * MP * t + h * MP + k // KP + 1)
                                    last = pe.matmul(accp[:, 0:H * A], oh[u][h][:, k, :], msg[h][:, k, :, :].rearrange("p h a -> p (h a)"),
                                                     start=(h == 0 and k == 0), stop=(h == 1 and k == HK - 1))
                                last.then_inc(main_done, 1)
                            pe.reg_add(r, r, 1)

        @block.vector
        def _(dve):
            with unless_wide(c, dve):
                dve.memset(c.acc[:, :, :], 0.0).then_inc(final_step, 1)
                dve.sem_inc(rows_free, 2)
                dve.wait_ge(final_step, 1)
                r = dve.alloc_register(f"{c.phase}_pairs")
                dve.reg_mov(r, 0)
                last_b = dve.alloc_register(f"{c.phase}_last_block")
                dve.reg_mov(last_b, 0)
                used = [dve.alloc_register(f"{c.phase}_used{u}") for u in range(2)]
                for u in range(2):
                    dve.reg_mov(used[u], 0)

                def take(b):
                    a_b = c.acc[:, ds(b, 1), :].rearrange("p a d -> p (a d)")
                    return dve.tensor_tensor(a_b, a_b, accp[:, 0:H * A], ALU.add)

                with dve.Fori(0, z.NB // 2) as i:
                    for u in range(2):
                        sc = 2 * i + u
                        lo, hi = load_span(dve, c, sc)
                        with dve.Fori(lo, hi) as b:
                            t = dve.snap(r)
                            w = dve.snap(used[u])
                            dve.tensor_scalar(dl[u][:, :], c.dst_all[:, ds(sc * K, K)], c.base[:, ds(b, 1)], None,
                                              ALU.subtract).then_inc(dve_step, 1)
                            dve.wait_ge(dve_step, t + 1)
                            for h in range(2):
                                dve.wait_ge(main_done, 2 * w + h + 1)
                                dve.tensor_tensor(oh[u][h][:, :, :], spread(c.iota[:, :].unsqueeze(1), [P, HK, P]),
                                                  spread(dl[u][:, h * HK:(h + 1) * HK].unsqueeze(2), [P, HK, P]),
                                                  ALU.is_equal).then_inc(onehot_ready, 1)
                            with dve.If_ne(r, 0):
                                dve.wait_ge(main_done, 2 * t + 2)
                                take(dve.snap(last_b, min_val=0, max_val=T - 1)).then_inc(acc_added, 1)
                            dve.wait_ge(ab_ready, sc + 1)
                            for h in range(2):
                                dve.wait_ge(fe_ready, 2 * t + h + 1)
                                dve.tensor_tensor(pair[h][:, :, :, :].rearrange("p k n h -> p k (n h)"),
                                                  ab[u][:, h * HK:(h + 1) * HK, :, :].rearrange("p k n h -> p k (n h)"),
                                                  fe[h][:, :, :], ALU.mult).then_inc(w_ready, 1)
                                dve.wait_ge(w_ready, 4 * t + 2 * h + 1)
                                dve.tensor_tensor(msg[h][:, :, :, HD], pair[h][:, :, 0, :], pair[h][:, :, 1, :], ALU.max).then_inc(w_ready, 1)
                                dve.wait_ge(w_ready, 4 * t + 2 * h + 2)
                                for m in range(MP):
                                    at = slice(m * KP, (m + 1) * KP)
                                    dve.tensor_tensor(msg[h][:, at, :, 0:HD],
                                                      rows[u][:, h * HK + m * KP:h * HK + (m + 1) * KP, 0:D].rearrange("p k (h d) -> p k h d", h=H),
                                                      spread(msg[h][:, at, :, HD:], [P, KP, H, HD]), ALU.mult).then_inc(msg_ready, 1)
                            dve.reg_add(r, r, 1)
                            dve.reg_mov(used[u], r)
                            dve.reg_mov(last_b, b)
                        dve.wait_ge(msg_ready, dve.snap(r) * (2 * MP))
                        dve.sem_inc(rows_free, 1)
                dve.wait_ge(main_done, dve.snap(r) * 2 + 2)
                fin = Chain(dve, final_step)
                fin.n = 1
                fin.link(take(dve.snap(last_b, min_val=0, max_val=T - 1)))
                weigh(c, fin, dve)


def weigh(c, fin, dve):
    z = c.z
    parts = c.acc[:, :, :].rearrange("p t (h a) -> p (t h) a", a=z.A)
    fin.link(dve.tensor_scalar(parts[:, :, z.HD:], parts[:, :, z.HD:], 1e-30, None, ALU.max))
    fin.link(dve.reciprocal(parts[:, :, z.HD:], parts[:, :, z.HD:]))
    dve.tensor_tensor(parts[:, :, 0:z.HD], parts[:, :, 0:z.HD], spread(parts[:, :, z.HD:], [P, z.T * z.H, z.HD]), ALU.mult)


def attend(c, tab, scores):
    nc, z = c.nc, c.z
    T, K, HK, H, HD, D, A = z.T, z.K, z.HK, z.H, z.HD, z.D, z.A
    c.phase = "attend"
    with ExitStack() as ctx:
        s = lambda n: c.sem(ctx, n)
        rows = [c.sb(ctx, f"rows{u}", [P, K, D + H]) for u in range(2)]
        idx = [c.sb(ctx, f"idx{u}", [P, K], I32) for u in range(2)]
        ad = c.sb(ctx, "ad", [P, T, 2 * H])
        top = c.sb(ctx, "top", [P, T, H])
        dl = c.sb(ctx, "dl", [P, K])
        oh = [c.sb(ctx, f"oh{h}", [P, HK, P]) for h in range(2)]
        oht = [c.sb(ctx, f"oht{h}", [P, HK * P]) for h in range(2)]
        pen = [c.sb(ctx, f"pen{h}", [P, HK * P]) for h in range(2)]
        ast = [c.sb(ctx, f"ast{h}", [H, HK * P]) for h in range(2)]
        junk = c.sb(ctx, "junk", [P, HK * P])
        run = c.sb(ctx, "run", [P, 3, H])
        adm = c.sb(ctx, "adm", [P, 2, 2 * H])
        fade = c.sb(ctx, "fade", [P, 2, H])
        zz = [c.sb(ctx, f"zz{h}", [P, HK, H]) for h in range(2)]
        msg = [c.sb(ctx, f"msg{h}", [P, HK, H, A]) for h in range(2)]
        tp = [c.ps(ctx, f"tp{h}", [P, HK * P]) for h in range(2)]
        ade = [c.ps(ctx, f"ade{h}", [P, HK, 2 * H]) for h in range(2)]
        bc = [c.ps(ctx, f"bc{h}", [P, HK * P]) for h in range(2)]
        astp = c.ps(ctx, "astp", [P, HK * P])
        accp = c.ps(ctx, "accp", [P, 512])
        gathered = [[s(f"gathered{u}{h}") for h in range(2)] for u in range(2)]
        names = ("idx_ready", "rows_free", "ad_in", "cleared", "dve_step", "onehot_ready",
                 "turned", "oht_ready", "pen_ready", "ast_turned", "ast_ready", "bc_ready", "bc_used",
                 "top_ready", "fade_ready", "fade_z", "ade_ready", "z_ready", "w_ready", "msg_ready", "main_done", "acc_added", "final_step")
        (idx_ready, rows_free, ad_in, cleared, dve_step, onehot_ready,
         turned, oht_ready, pen_ready, ast_turned, ast_ready, bc_ready, bc_used,
         top_ready, fade_ready, fade_z, ade_ready, z_ready, w_ready, msg_ready, main_done, acc_added, final_step) = (s(n) for n in names)
        block = ctx.enter_context(nc.Block())

        @block.sync
        def _(sp):
            sp.dma_start(ad[:, :, :], scores.rearrange("(t p) c -> p t c", p=P)).then_inc(ad_in, 16)
            sp.wait_ge(ad_in, 16)

        @block.gpsimd
        def _(pool):
            with if_wide(c, pool):
                gather_rows(c, pool, tab, idx, rows, idx_ready, rows_free, gathered)

        @block.scalar
        def _(act):
            with if_wide(c, act):
                copy_indices(c, act, 0, idx, 0).then_inc(idx_ready, 1)
                r = act.alloc_register(f"{c.phase}_pairs")
                act.reg_mov(r, 0)
                with act.Fori(0, z.NB // 2) as i:
                    for u in range(2):
                        sc = 2 * i + u
                        for h in range(2):
                            act.wait_ge(gathered[1 - u][h], (i + u) * 16 * HK)
                        alone(c, act)
                        copy_indices(c, act, sc + 1, idx, 1 - u).then_inc(idx_ready, 1)
                        lo, hi = load_span(act, c, sc)
                        with act.Fori(lo, hi) as b:
                            t = act.snap(r)
                            for h in range(2):
                                act.wait_ge(turned, 2 * t + h + 1)
                                act.activation(oht[h][:, :], tp[h][:, :], ACT.Copy).then_inc(oht_ready, 1)
                                act.activation(pen[h][:, :], tp[h][:, :], ACT.Copy, scale=FAR, bias=-FAR).then_inc(pen_ready, 1)
                                act.wait_ge(ast_turned, 2 * t + h + 1)
                                act.activation(ast[h][:, :], astp[0:H, :], ACT.Copy).then_inc(ast_ready, 1)
                            act.wait_ge(fade_z, t + 1)
                            act.activation(fade[:, 1, :], fade[:, 0, :], ACT.Exp).then_inc(fade_ready, 1)
                            for h in range(2):
                                act.wait_ge(z_ready, 2 * t + h + 1)
                                act.activation(msg[h][:, :, :, HD], zz[h][:, :, :], ACT.Exp).then_inc(w_ready, 1)
                            act.reg_add(r, r, 1)

        @block.tensor
        def _(pe):
            with if_wide(c, pe):
                pe.sem_inc(main_done, 2)
                r = pe.alloc_register(f"{c.phase}_pairs")
                pe.reg_mov(r, 0)
                with pe.Fori(0, z.NB // 2) as i:
                    for u in range(2):
                        lo, hi = load_span(pe, c, 2 * i + u)
                        with pe.Fori(lo, hi) as b:
                            t = pe.snap(r)
                            for h in range(2):
                                pe.wait_ge(onehot_ready, 2 * t + h + 1)
                                for k in range(HK):
                                    last = pe.transpose(tp[h][:, k * P:(k + 1) * P], oh[h][:, k, :], c.ident[:, :])
                                last.then_inc(turned, 1)
                                pe.wait_ge(gathered[u][h], (i + 1) * 16 * HK)
                                pe.wait_ge(ast_ready, 2 * t + h)
                                for k in range(HK):
                                    last = pe.transpose(astp[0:H, k * P:(k + 1) * P], rows[u][:, h * HK + k, D:], c.ident[:, :])
                                last.then_inc(ast_turned, 1)
                                pe.wait_ge(ast_ready, 2 * t + h + 1)
                                for n in range(H):
                                    pe.wait_ge(bc_used, t * 2 * H + max(h * H + n - 1, 0))
                                    pe.matmul(bc[n % 2][:, :], c.sel[0:H, n, :], ast[h][:, :], start=True, stop=True).then_inc(bc_ready, 1)
                            pe.wait_ge(top_ready, t + 1)
                            for h in range(2):
                                pe.wait_ge(oht_ready, 2 * t + h + 1)
                                for k in range(HK):
                                    last = pe.matmul(ade[h][:, k, :], oht[h][:, k * P:(k + 1) * P], adm[:, 0, :], start=True, stop=True)
                                last.then_inc(ade_ready, 1)
                            pe.wait_ge(acc_added, t)
                            for h in range(2):
                                pe.wait_ge(msg_ready, 2 * t + h + 1)
                                for k in range(HK):
                                    last = pe.matmul(accp[:, 0:H * A], oh[h][:, k, :], msg[h][:, k, :, :].rearrange("p h a -> p (h a)"),
                                                     start=(h == 0 and k == 0), stop=(h == 1 and k == HK - 1))
                                last.then_inc(main_done, 1)
                            pe.reg_add(r, r, 1)

        @block.vector
        def _(dve):
            with if_wide(c, dve):
                dve.memset(c.acc[:, :, :], 0.0)
                dve.memset(top[:, :, :], -FAR).then_inc(cleared, 1)
                dve.sem_inc(rows_free, 2)
                dve.wait_ge(ad_in, 16)
                dve.wait_ge(cleared, 1)
                ch = Chain(dve, dve_step, 11)
                r = dve.alloc_register(f"{c.phase}_pairs")
                dve.reg_mov(r, 0)
                with dve.Fori(0, z.NB // 2) as i:
                    for u in range(2):
                        sc = 2 * i + u
                        lo, hi = load_span(dve, c, sc)
                        with dve.Fori(lo, hi) as b:
                            t = dve.snap(r)
                            ch.begin(t)
                            ch.link(dve.tensor_scalar(dl[:, :], c.dst_all[:, ds(sc * K, K)], c.base[:, ds(b, 1)], None, ALU.subtract))
                            for h in range(2):
                                dve.wait_ge(main_done, 2 * t + h + 1)
                                dve.tensor_tensor(oh[h][:, :, :], spread(c.iota[:, :].unsqueeze(1), [P, HK, P]),
                                                  spread(dl[:, h * HK:(h + 1) * HK].unsqueeze(2), [P, HK, P]),
                                                  ALU.is_equal).then_inc(onehot_ready, 1)
                            ch.link(dve.tensor_scalar(run[:, 0, :], top[:, ds(b, 1), :].rearrange("p a h -> p (a h)"), 1.0, None, ALU.mult))
                            for h in range(2):
                                dve.wait_ge(pen_ready, 2 * t + h + 1)
                                for n in range(H):
                                    dve.wait_ge(bc_ready, t * 2 * H + h * H + n + 1)
                                    alone(c, dve)
                                    dve.tensor_tensor_reduce(out=junk[:, :], in0=bc[n % 2][:, :], in1=pen[h][:, :], scale=1.0,
                                                             scalar=run[:, h, n:n + 1], op0=ALU.add, op1=ALU.max,
                                                             accum_out=run[:, h + 1, n:n + 1]).then_inc(bc_used, 1)
                                    dve.wait_ge(bc_used, t * 2 * H + h * H + n + 1)
                            ch.link(dve.tensor_scalar(top[:, ds(b, 1), :].rearrange("p a h -> p (a h)"), run[:, 2, :], 1.0, None, ALU.mult))
                            a_b = ad[:, ds(b, 1), H:2 * H].rearrange("p a h -> p (a h)")
                            dve.tensor_scalar(adm[:, 0, 0:H], a_b, 1.0, None, ALU.mult)
                            dve.tensor_tensor(adm[:, 0, H:], run[:, 2, :], a_b, ALU.add)
                            ch.link(dve.tensor_tensor(adm[:, 1, H:], run[:, 0, :], a_b, ALU.add))
                            dve.scalar_tensor_tensor(adm[:, 0, H:], adm[:, 0, H:], NEG_SLOPE, adm[:, 0, H:], ALU.mult, ALU.max).then_inc(top_ready, 1)
                            ch.link(dve.scalar_tensor_tensor(adm[:, 1, H:], adm[:, 1, H:], NEG_SLOPE, adm[:, 1, H:], ALU.mult, ALU.max))
                            dve.tensor_tensor(fade[:, 0, :], adm[:, 1, H:], adm[:, 0, H:], ALU.subtract).then_inc(fade_z, 1)
                            for h in range(2):
                                dve.wait_ge(ade_ready, 2 * t + h + 1)
                                dve.wait_ge(gathered[u][h], (i + 1) * 16 * HK)
                                ch.link(dve.tensor_tensor(zz[h][:, :, :], rows[u][:, h * HK:(h + 1) * HK, D:], ade[h][:, :, 0:H], ALU.add))
                                ch.link(dve.scalar_tensor_tensor(zz[h][:, :, :], zz[h][:, :, :], NEG_SLOPE, zz[h][:, :, :], ALU.mult, ALU.max))
                                ch.link(dve.tensor_tensor(zz[h][:, :, :], zz[h][:, :, :], ade[h][:, :, H:], ALU.subtract))
                                dve.tensor_scalar(zz[h][:, :, :], zz[h][:, :, :], 0.0, None, ALU.min).then_inc(z_ready, 1)
                            for h in range(2):
                                dve.wait_ge(w_ready, 2 * t + h + 1)
                                dve.tensor_tensor(msg[h][:, :, :, 0:HD],
                                                  rows[u][:, h * HK:(h + 1) * HK, 0:D].rearrange("p k (h d) -> p k h d", h=H),
                                                  spread(msg[h][:, :, :, HD:], [P, HK, H, HD]), ALU.mult).then_inc(msg_ready, 1)
                            dve.wait_ge(main_done, 2 * t + 4)
                            dve.wait_ge(fade_ready, t + 1)
                            for n in range(H):
                                a_n = c.acc[:, ds(b, 1), n * A:(n + 1) * A].rearrange("p a d -> p (a d)")
                                last = dve.scalar_tensor_tensor(a_n, a_n, fade[:, 1, n:n + 1], accp[:, n * A:(n + 1) * A], ALU.mult, ALU.add)
                            last.then_inc(acc_added, 1)
                            ch.end()
                            dve.reg_add(r, r, 1)
                        dve.wait_ge(msg_ready, dve.snap(r) * 2)
                        dve.sem_inc(rows_free, 1)
                dve.wait_ge(acc_added, dve.snap(r))
                alone(c, dve)
                weigh(c, Chain(dve, final_step), dve)



def aggregate(c, tab):
    nc, z = c.nc, c.z
    K, HK, D = z.K, z.HK, z.D
    c.phase = "aggregate"
    with ExitStack() as ctx:
        s = lambda n: c.sem(ctx, n)
        rows = [c.sb(ctx, f"rows{u}", [P, K, D]) for u in range(2)]
        idx = [c.sb(ctx, f"idx{u}", [P, K], I32) for u in range(2)]
        dl = c.sb(ctx, "dl", [P, K])
        oh = [c.sb(ctx, f"oh{h}", [P, HK, P]) for h in range(2)]
        accp = c.ps(ctx, "accp", [P, 512])
        gathered = [[s(f"gathered{u}{h}") for h in range(2)] for u in range(2)]
        names = ("idx_ready", "rows_free", "dve_step", "onehot_ready", "main_done", "acc_added", "cleared")
        idx_ready, rows_free, dve_step, onehot_ready, main_done, acc_added, cleared = (s(n) for n in names)
        block = ctx.enter_context(nc.Block())

        @block.gpsimd
        def _(pool):
            gather_rows(c, pool, tab, idx, rows, idx_ready, rows_free, gathered)

        @block.scalar
        def _(act):
            copy_indices(c, act, 0, idx, 0).then_inc(idx_ready, 1)
            with act.Fori(0, z.NB // 2) as i:
                for u in range(2):
                    for h in range(2):
                        act.wait_ge(gathered[1 - u][h], (i + u) * 16 * HK)
                    alone(c, act)
                    copy_indices(c, act, 2 * i + u + 1, idx, 1 - u).then_inc(idx_ready, 1)

        @block.tensor
        def _(pe):
            pe.sem_inc(main_done, 2)
            r = pe.alloc_register(f"{c.phase}_pairs")
            pe.reg_mov(r, 0)
            pe.sem_inc(rows_free, 2)
            with pe.Fori(0, z.NB // 2) as i:
                for u in range(2):
                    lo, hi = load_span(pe, c, 2 * i + u)
                    with pe.Fori(lo, hi) as b:
                        t = pe.snap(r)
                        pe.wait_ge(acc_added, t)
                        for h in range(2):
                            pe.wait_ge(onehot_ready, 2 * t + h + 1)
                            pe.wait_ge(gathered[u][h], (i + 1) * 16 * HK)
                            for k in range(HK):
                                last = pe.matmul(accp[:, 0:D], oh[h][:, k, :], rows[u][:, h * HK + k, :],
                                                 start=(h == 0 and k == 0), stop=(h == 1 and k == HK - 1))
                            last.then_inc(main_done, 1)
                        pe.reg_add(r, r, 1)
                    pe.wait_ge(main_done, pe.snap(r) * 2 + 2)
                    pe.sem_inc(rows_free, 1)

        @block.vector
        def _(dve):
            dve.memset(c.acc[:, :, :], 0.0).then_inc(cleared, 1)
            dve.wait_ge(cleared, 1)
            ch = Chain(dve, dve_step, 1)
            r = dve.alloc_register(f"{c.phase}_pairs")
            dve.reg_mov(r, 0)
            with dve.Fori(0, z.NB // 2) as i:
                for u in range(2):
                    sc = 2 * i + u
                    lo, hi = load_span(dve, c, sc)
                    with dve.Fori(lo, hi) as b:
                        t = dve.snap(r)
                        ch.begin(t)
                        ch.link(dve.tensor_scalar(dl[:, :], c.dst_all[:, ds(sc * K, K)], c.base[:, ds(b, 1)], None, ALU.subtract))
                        for h in range(2):
                            dve.wait_ge(main_done, 2 * t + h + 1)
                            dve.tensor_tensor(oh[h][:, :, :], spread(c.iota[:, :].unsqueeze(1), [P, HK, P]),
                                              spread(dl[:, h * HK:(h + 1) * HK].unsqueeze(2), [P, HK, P]),
                                              ALU.is_equal).then_inc(onehot_ready, 1)
                        ch.end()
                        dve.wait_ge(main_done, 2 * t + 4)
                        a_b = c.acc[:, ds(b, 1), 0:D].rearrange("p a d -> p (a d)")
                        dve.tensor_tensor(a_b, a_b, accp[:, 0:D], ALU.add).then_inc(acc_added, 1)
                        dve.reg_add(r, r, 1)


def combine(c, xt_all, gate, gate_b, conv=None):
    nc, z = c.nc, c.z
    G, KC, D, X, H, HD, A, W = z.G, z.KC, z.D, z.X, z.H, z.HD, z.A, z.W
    NTP = 3 if conv else 1
    c.phase = "combine_sums" if conv else "combine_attention"
    with ExitStack() as ctx:
        s = lambda n: c.sem(ctx, n)
        stats = c.sb(ctx, "stats", [P, G, 6])
        mv = c.sb(ctx, "mv", [P, G, 2])
        sd = c.sb(ctx, "sd", [P, G])
        rstd = c.sb(ctx, "rstd", [P, G])
        xn = c.sb(ctx, "xn", [P, G, D])
        xt = c.sb(ctx, "xt", [P, G, KC, P])
        lg = c.sb(ctx, "lg", [P, G, X])
        red = c.sb(ctx, "red", [P, G])
        gt = c.sb(ctx, "gt", [P, G, X, X])
        eq = c.sb(ctx, "eq", [P, G, X, X])
        gw = c.sb(ctx, "gw", [P, KC, X])
        gb = c.sb(ctx, "gb", [1, X])
        if conv:
            cw = c.sb(ctx, "conv_w", [P, 2, KC, D])
            sums = c.sb(ctx, "sums", [P, G, D])
            st = c.sb(ctx, "st", [P, G, KC, P])
        tp = [c.ps(ctx, f"tp{i}", [P, KC, P]) for i in range(2)]
        cv = [c.ps(ctx, f"cv{i}", [P, 512]) for i in range(2)]
        lgp = c.ps(ctx, "lgp", [P, G, X])
        names = ("dve_step", "var_ready", "sd_ready", "xn_ready", "sums_ready", "turned", "xt_ready", "cv_ready",
                 "res_ready", "lg_ready", "lg_used", "e_ready", "xt_out", "w_in")
        (dve_step, var_ready, sd_ready, xn_ready, sums_ready, turned, xt_ready, cv_ready,
         res_ready, lg_ready, lg_used, e_ready, xt_out, w_in) = (s(n) for n in names)
        block = ctx.enter_context(nc.Block())
        NW = 4 if conv else 2

        @block.sync
        def _(sp):
            sp.dma_start(gw[:, :, :], gate.rearrange("(k p) e -> p k e", p=P)).then_inc(w_in, 16)
            sp.dma_start(gb[:, :], gate_b.rearrange("(o e) -> o e", o=1)).then_inc(w_in, 16)
            for n, w in enumerate(conv or ()):
                sp.dma_start(cw[:, n, :, :], w.rearrange("(k p) d -> p k d", p=P)).then_inc(w_in, 16)
            sp.wait_ge(w_in, 16 * NW)

        rounds = [(xn, xt), (sums, st), (xn, xt)] if conv else [(xn, xt)]

        @block.tensor
        def _(pe):
            pe.wait_ge(w_in, 16 * NW)
            with pe.Fori(0, z.NG) as g:
                for n, (from_, _) in enumerate(rounds):
                    if n == NTP - 1:
                        pe.wait_ge(xn_ready, g * (2 if conv else 1) + (2 if conv else 1))
                    elif n == 0:
                        pe.wait_ge(xn_ready, g * 2 + 1)
                    else:
                        pe.wait_ge(sums_ready, g + 1)
                    for j in range(G):
                        q = n * G + j
                        pe.wait_ge(xt_ready, g * G * NTP + max(q - 1, 0))
                        for k in range(KC):
                            last = pe.transpose(tp[q % 2][:, k, :], from_[:, j, k * P:(k + 1) * P], c.ident[:, :])
                        last.then_inc(turned, 1)
                    if n == 1:
                        for j in range(G):
                            pe.wait_ge(xt_ready, g * G * NTP + G + j + 1)
                            pe.wait_ge(res_ready, g * G + max(j - 1, 0))
                            for m, a in enumerate((xt, st)):
                                for k in range(KC):
                                    last = pe.matmul(cv[j % 2][:, 0:D], a[:, j, k, :], cw[:, m, k, :],
                                                     start=(m == 0 and k == 0), stop=(m == 1 and k == KC - 1))
                            last.then_inc(cv_ready, 1)
                pe.wait_ge(xt_ready, (g + 1) * G * NTP)
                pe.wait_ge(lg_used, g)
                for j in range(G):
                    for k in range(KC):
                        pe.matmul(lgp[:, j, :], xt[:, j, k, :], gw[:, k, :], start=(k == 0), stop=False)
                    last = pe.matmul(lgp[:, j, :], c.ones[0:1, :], gb[:, :], start=False, stop=True)
                last.then_inc(lg_ready, 1)

        @block.scalar
        def _(act):
            with act.Fori(0, z.NG) as g:
                def root(n):
                    act.wait_ge(var_ready, g * 2 + n)
                    act.activation(sd[:, :], mv[:, :, 1], ACT.Sqrt, bias=c.eps[:, 0:1]).then_inc(sd_ready, 1)
                root(1)
                act.wait_ge(lg_ready, g)
                act.wait_ge(xt_out, g)
                for n, (_, to) in enumerate(rounds):
                    if n == NTP - 1:
                        root(2)
                        if conv:
                            act.wait_ge(cv_ready, (g + 1) * G)
                    for j in range(G):
                        q = n * G + j
                        act.wait_ge(turned, g * G * NTP + q + 1)
                        act.activation(to[:, j, :, :], tp[q % 2][:, :, :], ACT.Copy).then_inc(xt_ready, 1)
                act.wait_ge(lg_used, g + 1)
                act.activation(lg[:, :, :], lg[:, :, :], ACT.Exp).then_inc(e_ready, 1)

        @block.gpsimd
        def _(pool):
            with pool.Fori(0, z.NG) as g:
                pool.wait_ge(xt_ready, (g + 1) * G * NTP)
                alone(c, pool)
                for k in range(KC):
                    last = pool.tensor_copy(xt_all[:, k, ds(g * W, W)].rearrange("p (t n) -> p t n", n=P), xt[:, :, k, :])
                last.then_inc(xt_out, 1)

        @block.vector
        def _(dve):
            ch = Chain(dve, dve_step, 8 if conv else 15)
            with dve.Fori(0, z.NG) as g:
                ch.begin(g)
                group = c.res[:, ds(g * G, G), :]
                dve.wait_ge(turned, g * G * NTP)
                last = normalise(c, dve, ch, g, stats, mv, sd, rstd, xn, var_ready, sd_ready, g * 2 + 1)
                if conv:
                    last.then_inc(xn_ready, 1)
                    dve.tensor_scalar(sums[:, :, :], c.acc[:, ds(g * G, G), 0:D], 1.0, None, ALU.mult).then_inc(sums_ready, 1)
                    for j in range(G):
                        row = c.res[:, ds(g * G + j, 1), :].rearrange("p a d -> p (a d)")
                        dve.wait_ge(cv_ready, g * G + j + 1)
                        dve.scalar_tensor_tensor(row, cv[j % 2][:, 0:D], 0.0, row, ALU.max, ALU.add).then_inc(res_ready, 1)
                    dve.wait_ge(res_ready, (g + 1) * G)
                    dve.wait_ge(turned, g * G * NTP + G)
                else:
                    ch.link(last)
                    ch.link(dve.tensor_tensor(group, group, xn[:, :, :], ALU.add))
                    for j in range(G):
                        row = c.res[:, ds(g * G + j, 1), :].rearrange("p a (h d) -> p (a h) d", h=H)
                        att = c.acc[:, ds(g * G + j, 1), :].rearrange("p a (h d) -> p (a h) d", h=H)[:, :, 0:HD]
                        last = dve.tensor_tensor(row, row, att, ALU.add)
                    ch.link(last)
                normalise(c, dve, ch, g, stats, mv, sd, rstd, xn, var_ready, sd_ready, g * 2 + 2).then_inc(xn_ready, 1)
                dve.wait_ge(lg_ready, g + 1)
                ch.link(dve.tensor_reduce(red[:, :], lgp[:, :, :], AX.X, ALU.max))
                dve.tensor_tensor(lg[:, :, :], lgp[:, :, :], spread(red[:, :].unsqueeze(2), [P, G, X]), ALU.subtract).then_inc(lg_used, 1)
                dve.wait_ge(e_ready, g + 1)
                ch.link(dve.tensor_reduce(red[:, :], lg[:, :, :], AX.X, ALU.add))
                ch.link(dve.reciprocal(red[:, :], red[:, :]))
                gates = c.gates[:, ds(g * G, G), :]
                probs = gates if conv else lg[:, :, :]
                ch.link(dve.tensor_tensor(probs, lg[:, :, :], spread(red[:, :].unsqueeze(2), [P, G, X]), ALU.mult))
                if not conv:
                    mine = spread(lg[:, :, :].unsqueeze(3), [P, G, X, X])
                    other = spread(lg[:, :, :].unsqueeze(2), [P, G, X, X])
                    dve.tensor_tensor(gt[:, :, :, :], other, mine, ALU.is_gt)
                    ch.link(dve.tensor_tensor(eq[:, :, :, :], other, mine, ALU.is_equal))
                    tri = spread(c.tri[:, :, :].rearrange("p i j -> p (i j)").unsqueeze(1), [P, G, X * X])
                    ch.link(dve.tensor_tensor(eq[:, :, :, :].rearrange("p t i j -> p t (i j)"),
                                              eq[:, :, :, :].rearrange("p t i j -> p t (i j)"), tri, ALU.mult))
                    ch.link(dve.tensor_tensor(gt[:, :, :, :], gt[:, :, :, :], eq[:, :, :, :], ALU.add))
                    ch.link(dve.tensor_reduce(eq[:, :, :, 0], gt[:, :, :, :], AX.X, ALU.add))
                    dve.scalar_tensor_tensor(gates, eq[:, :, :, 0], 1.5, lg[:, :, :], ALU.is_lt, ALU.mult)
                ch.end()


def experts_gelu(c, xt_all, w1, b1, w2, b2):
    nc, z = c.nc, c.z
    G, KC, HC, D, F, X, W, HW, NG = z.G, z.KC, z.HC, z.D, z.F, z.X, z.W, z.HW, z.NG
    UP = 2 * HC
    c.phase = "experts_gelu"
    with ExitStack() as ctx:
        s = lambda n: c.sem(ctx, n)
        w1s = [c.sb(ctx, f"w1s{u}", [P, KC, F]) for u in range(2)]
        w2s = [c.sb(ctx, f"w2s{u}", [P, HC, D]) for u in range(2)]
        b1s = [c.sb(ctx, f"b1s{u}", [P, HC]) for u in range(2)]
        b2s = [c.sb(ctx, f"b2s{u}", [1, D]) for u in range(2)]
        ht = c.sb(ctx, "ht", [P, HC, W])
        up = [c.ps(ctx, f"up{i}", [P, 512]) for i in range(4)]
        yp = [c.ps(ctx, f"yp{i}", [P, 512]) for i in range(2)]
        w_in = [s(f"w_in{u}") for u in range(2)]
        up_ready, h_ready, y_ready, y_added = (s(n) for n in ("up_ready", "h_ready", "y_ready", "y_added"))
        block = ctx.enter_context(nc.Block())

        @block.sync
        def _(sp):
            def load(e, u):
                sp.dma_start(w1s[u][:, :, :], w1[ds(e, 1), :, :].rearrange("o (k p) f -> p (o k) f", p=P)).then_inc(w_in[u], 16)
                sp.dma_start(w2s[u][:, :, :], w2[ds(e, 1), :, :].rearrange("o (k p) d -> p (o k) d", p=P)).then_inc(w_in[u], 16)
                sp.dma_start(b1s[u][:, :], b1[ds(e, 1), :].rearrange("o (k p) -> p (o k)", p=P),
                             allow_slow_non_contiguous=True).then_inc(w_in[u], 16)
                sp.dma_start(b2s[u][:, :], b2[ds(e, 1), :]).then_inc(w_in[u], 16)

            load(0, 0)
            load(1, 1)
            with sp.Fori(1, X // 2) as o:
                for u in range(2):
                    sp.wait_ge(y_ready, (2 * o + u - 1) * NG * G)
                    load(2 * o + u, u)
            for u in range(2):
                sp.wait_ge(w_in[u], 64 * (X // 2))

        @block.tensor
        def _(pe):
            with pe.Fori(0, X // 2) as o:
                for u in range(2):
                    pe.wait_ge(w_in[u], (o + 1) * 64)
                    alone(c, pe)
                    with pe.Fori(0, NG) as g:
                        n = (2 * o + u) * NG + g
                        for hc in range(HC):
                            for v in range(2):
                                q = 2 * hc + v
                                pe.wait_ge(h_ready, n * UP + max(q - 3, 0))
                                for k in range(KC):
                                    last = pe.matmul(up[q % 4][:, 0:HW], w1s[u][:, k, hc * P:(hc + 1) * P],
                                                     xt_all[:, k, ds(g * W + v * HW, HW)], start=(k == 0), stop=(k == KC - 1))
                                last.then_inc(up_ready, 1)
                        pe.wait_ge(h_ready, (n + 1) * UP)
                        for j in range(G):
                            pe.wait_ge(y_added, n * G + max(j - 1, 0))
                            for hc in range(HC):
                                pe.matmul(yp[j % 2][:, 0:D], ht[:, hc, j * P:(j + 1) * P], w2s[u][:, hc, :], start=(hc == 0), stop=False)
                            pe.matmul(yp[j % 2][:, 0:D], c.ones[0:1, :], b2s[u][:, :], start=False, stop=True).then_inc(y_ready, 1)

        @block.scalar
        def _(act):
            with act.Fori(0, X // 2) as o:
                for u in range(2):
                    act.wait_ge(w_in[u], (o + 1) * 64)
                    with act.Fori(0, NG) as g:
                        n = (2 * o + u) * NG + g
                        act.wait_ge(y_ready, n * G)
                        for q in range(UP):
                            act.wait_ge(up_ready, n * UP + q + 1)
                            act.activation(ht[:, q // 2, (q % 2) * HW:(q % 2 + 1) * HW], up[q % 4][:, 0:HW], ACT.Gelu,
                                           bias=b1s[u][:, q // 2:q // 2 + 1]).then_inc(h_ready, 1)

        @block.vector
        def _(dve):
            with dve.Fori(0, X) as e:
                with dve.Fori(0, NG) as g:
                    n = e * NG + g
                    for j in range(G):
                        row = c.res[:, ds(g * G + j, 1), :].rearrange("p a d -> p (a d)")
                        gate = c.gates[:, ds(g * G + j, 1), ds(e, 1)].rearrange("p a e -> p (a e)")
                        dve.wait_ge(y_ready, n * G + j + 1)
                        if j == 0:
                            dve.wait_ge(y_added, n * G)
                        dve.scalar_tensor_tensor(row, yp[j % 2][:, 0:D], gate, row, ALU.mult, ALU.add).then_inc(y_added, 1)


def store_norms(c, tab):
    nc, z = c.nc, c.z
    G = z.G
    c.phase = "store_norms"
    with ExitStack() as ctx:
        s = lambda n: c.sem(ctx, n)
        stats = c.sb(ctx, "stats", [P, G, 6])
        mv = c.sb(ctx, "mv", [P, G, 2])
        sd = c.sb(ctx, "sd", [P, G])
        rstd = c.sb(ctx, "rstd", [P, G])
        xn = c.sb(ctx, "xn", [P, G, z.D])
        dve_step, var_ready, sd_ready, xn_ready, stored = (s(n) for n in ("dve_step", "var_ready", "sd_ready", "xn_ready", "stored"))
        block = ctx.enter_context(nc.Block())

        @block.vector
        def _(dve):
            ch = Chain(dve, dve_step, 2)
            with dve.Fori(0, z.NG) as g:
                ch.begin(g)
                dve.wait_ge(stored, g * 16)
                normalise(c, dve, ch, g, stats, mv, sd, rstd, xn, var_ready, sd_ready, g + 1).then_inc(xn_ready, 1)
                ch.end()

        @block.scalar
        def _(act):
            with act.Fori(0, z.NG) as g:
                act.wait_ge(var_ready, g + 1)
                act.activation(sd[:, :], mv[:, :, 1], ACT.Sqrt, bias=c.eps[:, 0:1]).then_inc(sd_ready, 1)

        @block.sync
        def _(sp):
            with sp.Fori(0, z.NG) as g:
                sp.wait_ge(xn_ready, g + 1)
                sp.dma_start(tab[ds(g * z.W, z.W), :].rearrange("(t p) d -> p t d", p=P), xn[:, :, :]).then_inc(stored, 16)
            sp.wait_ge(stored, z.NG * 16)


def experts_deep(c, xt_all, w1, w2, wo, bo, bn_out, out):
    nc, z = c.nc, c.z
    G, KC, D, X, W, HW, NG, F2 = z.G, z.KC, z.D, z.X, z.W, z.HW, z.NG, z.F2
    HC = F2 // P
    UP = 2 * HC
    c.phase = "experts_deep"
    with ExitStack() as ctx:
        s = lambda n: c.sem(ctx, n)
        w1s = [c.sb(ctx, f"w1s{u}", [P, KC, F2]) for u in range(2)]
        w2s = [c.sb(ctx, f"w2s{u}", [P, HC, F2]) for u in range(2)]
        wos = [c.sb(ctx, f"wos{u}", [P, HC, D]) for u in range(2)]
        aff = [c.sb(ctx, f"aff{u}", [P, 2, 2, HC]) for u in range(2)]
        bos = [c.sb(ctx, f"bos{u}", [1, D]) for u in range(2)]
        hid = [c.sb(ctx, f"hid{n}", [P, HC, W]) for n in range(2)]
        up = [c.ps(ctx, f"up{i}", [P, 512]) for i in range(4)]
        yp = [c.ps(ctx, f"yp{i}", [P, 512]) for i in range(2)]
        w_in = [s(f"w_in{u}") for u in range(2)]
        up_ready, h_ready, y_ready, y_added, stored = (s(n) for n in ("up_ready", "h_ready", "y_ready", "y_added", "stored"))
        block = ctx.enter_context(nc.Block())
        NL = 8

        @block.sync
        def _(sp):
            def load(e, u):
                for to, w in ((w1s, w1), (w2s, w2), (wos, wo)):
                    sp.dma_start(to[u][:, :, :], w[ds(e, 1), :, :].rearrange("o (k p) f -> p (o k) f", p=P)).then_inc(w_in[u], 16)
                for n in range(2):
                    for m in range(2):
                        sp.dma_start(aff[u][:, n, m, :], bn_out[n][m][ds(e, 1), :, :].rearrange("o p k -> p (o k)")).then_inc(w_in[u], 16)
                sp.dma_start(bos[u][:, :], bo[ds(e, 1), :]).then_inc(w_in[u], 16)

            load(0, 0)
            load(1, 1)
            with sp.Fori(1, X // 2) as o:
                for u in range(2):
                    sp.wait_ge(y_ready, (2 * o + u - 1) * NG * G)
                    load(2 * o + u, u)
            for u in range(2):
                sp.wait_ge(w_in[u], 16 * NL * (X // 2))
            sp.wait_ge(y_added, X * NG * G)
            sp.dma_start(out[0:(z.T - 1) * P, :].rearrange("(t p) d -> p t d", p=P), c.res[:, 0:z.T - 1, :]).then_inc(stored, 16)
            sp.dma_start(out[(z.T - 1) * P:z.N, :], c.res[0:z.LAST, z.T - 1, :]).then_inc(stored, 16)
            sp.wait_ge(stored, 32)

        @block.tensor
        def _(pe):
            with pe.Fori(0, X // 2) as o:
                for u in range(2):
                    pe.wait_ge(w_in[u], (o + 1) * 16 * NL)
                    alone(c, pe)
                    with pe.Fori(0, NG) as g:
                        n = (2 * o + u) * NG + g
                        for layer in range(2):
                            for hc in range(HC):
                                for v in range(2):
                                    q = layer * UP + 2 * hc + v
                                    pe.wait_ge(h_ready, n * 2 * UP + (max(q - 3, 0) if layer == 0 else UP))
                                    for k in range(KC):
                                        moving = xt_all[:, k, ds(g * W + v * HW, HW)] if layer == 0 else hid[0][:, k, v * HW:(v + 1) * HW]
                                        last = pe.matmul(up[q % 4][:, 0:HW], (w1s if layer == 0 else w2s)[u][:, k, hc * P:(hc + 1) * P],
                                                         moving, start=(k == 0), stop=(k == KC - 1))
                                    last.then_inc(up_ready, 1)
                        pe.wait_ge(h_ready, (n + 1) * 2 * UP)
                        for j in range(G):
                            pe.wait_ge(y_added, n * G + max(j - 1, 0))
                            for hc in range(HC):
                                pe.matmul(yp[j % 2][:, 0:D], hid[1][:, hc, j * P:(j + 1) * P], wos[u][:, hc, :], start=(hc == 0), stop=False)
                            pe.matmul(yp[j % 2][:, 0:D], c.ones[0:1, :], bos[u][:, :], start=False, stop=True).then_inc(y_ready, 1)

        @block.scalar
        def _(act):
            with act.Fori(0, X // 2) as o:
                for u in range(2):
                    act.wait_ge(w_in[u], (o + 1) * 16 * NL)
                    with act.Fori(0, NG) as g:
                        n = (2 * o + u) * NG + g
                        act.wait_ge(y_ready, n * G)
                        for q in range(2 * UP):
                            layer, hc, v = q // UP, q % UP // 2, q % 2
                            act.wait_ge(up_ready, n * 2 * UP + q + 1)
                            act.activation(hid[layer][:, hc, v * HW:(v + 1) * HW], up[q % 4][:, 0:HW], ACT.Relu,
                                           scale=aff[u][:, layer, 0, hc:hc + 1], bias=aff[u][:, layer, 1, hc:hc + 1]).then_inc(h_ready, 1)

        @block.vector
        def _(dve):
            with dve.Fori(0, X) as e:
                with dve.Fori(0, NG) as g:
                    n = e * NG + g
                    for j in range(G):
                        row = c.res[:, ds(g * G + j, 1), :].rearrange("p a d -> p (a d)")
                        gate = c.gates[:, ds(g * G + j, 1), ds(e, 1)].rearrange("p a e -> p (a e)")
                        dve.wait_ge(y_ready, n * G + j + 1)
                        if j == 0:
                            dve.wait_ge(y_added, n * G)
                        dve.scalar_tensor_tensor(row, yp[j % 2][:, 0:D], gate, row, ALU.mult, ALU.add).then_inc(y_added, 1)


def gnn_experts(nc, a, out, phases=99):
    z = Shapes(a["x"], a["src"], a["L0_gnn_W"], a["L0_gnn_attn_src"], a["L0_gnn_pos_attn_src"],
               a["L0_ffn_W1"], a["L0_ffn_W2"], a["L1_ffn_Wr"], a["L1_ffn_v1"])
    c = Core(nc, z)
    dram = lambda name, shape, dt=F32: nc.dram_tensor(name, shape, dt, kind="Internal").ap()
    tab0 = dram("rows_attention", (z.T * P, z.D + z.H))
    scores = dram("scores", (z.T * P, 2 * z.H))
    tab1 = dram("rows_sums", (z.T * P, z.D))
    c.span_d = dram("spans_dram", (z.NB, 2), I32)
    bn_out = [[dram(f"bn{n}{m}", (z.X, P, z.F2 // P)) for m in range(2)] for n in range(2)]
    with ExitStack() as ctx:
        c.pace = c.sem(ctx, "pace")
        c.res = c.sb(ctx, "res", [P, z.T, z.D])
        c.gates = c.sb(ctx, "gates", [P, z.T, z.X])
        c.ident = c.sb(ctx, "ident", [P, P])
        c.ident_b = c.sb(ctx, "ident_b", [P, P], BF16)
        c.wide = c.sb(ctx, "wide", [1, 1], I32)
        c.less_top = c.sb(ctx, "less_top", [P, 2])
        c.ones = c.sb(ctx, "ones", [1, P])
        c.eps = c.sb(ctx, "eps", [P, 2])
        c.tri = c.sb(ctx, "tri", [P, z.X, z.X])
        c.sel = c.sb(ctx, "sel", [P, z.H, P])
        c.iota = c.sb(ctx, "iota", [P, P])
        c.base = c.sb(ctx, "base", [P, z.T])
        c.spans = c.sb(ctx, "spans", [1, 2 * z.NB], I32)
        c.src_all = c.sb(ctx, "src_all", [P, (z.NB + 1) * z.K], I32)
        c.dst_all = c.sb(ctx, "dst_all", [P, z.NB * z.K])
        c.wall = c.sb(ctx, "wall", [P, z.KC, z.D + 2 * z.H])
        bn_in = [[a[f"L1_ffn_{n}{i}"] for n in ("b", "g", "be", "m", "v")] for i in (1, 2)]
        prepare(c, a["x"], a["src"], a["dst"], a["L0_gnn_W"], a["L0_gnn_attn_src"], a["L0_gnn_attn_dst"],
                a["L0_gnn_pos_attn_src"], a["L0_gnn_pos_attn_dst"], bn_in, bn_out)
        if phases > 1:
            project(c, tab0, scores)
        for layer in range(2):
            with ExitStack() as inner:
                c.phase = f"layer{layer}"
                c.acc = c.sb(inner, "acc", [P, z.T, z.H * z.A])
                if layer == 0:
                    if phases > 2:
                        c.factors = c.sb(inner, "factors", [P, z.T, 3, 2 * z.H], BF16)
                        bound_scores(c, scores)
                        attend_bounded(c, tab0)
                        attend(c, tab0, scores)
                elif phases > 6:
                    aggregate(c, tab1)
                c.phase = f"layer{layer}"
                c.xt_all = c.sb(inner, "xt_all", [P, z.KC, z.T * P])
                if layer == 0 and phases > 3:
                    combine(c, c.xt_all, a["L0_ffn_gate_w"], a["L0_ffn_gate_b"])
                if layer == 1 and phases > 7:
                    combine(c, c.xt_all, a["L1_ffn_Wr"], a["L1_ffn_br"], (a["L1_gnn_W"], a["L1_gnn_M"]))
                if layer == 0 and phases > 4:
                    experts_gelu(c, c.xt_all, a["L0_ffn_W1"], a["L0_ffn_b1"], a["L0_ffn_W2"], a["L0_ffn_b2"])
                if layer == 0 and phases > 5:
                    store_norms(c, tab1)
                if layer == 1 and phases > 8:
                    experts_deep(c, c.xt_all, a["L1_ffn_W1"], a["L1_ffn_W2"], a["L1_ffn_Wo"], a["L1_ffn_bo"], bn_out, out)


_INS = ["x", "src", "dst", "L0_gnn_W", "L0_gnn_attn_src", "L0_gnn_attn_dst", "L0_gnn_pos_attn_src", "L0_gnn_pos_attn_dst",
        "L0_ffn_gate_w", "L0_ffn_gate_b", "L0_ffn_W1", "L0_ffn_b1", "L0_ffn_W2", "L0_ffn_b2", "L1_gnn_W", "L1_gnn_M",
        "L1_ffn_Wr", "L1_ffn_br", "L1_ffn_W1", "L1_ffn_b1", "L1_ffn_g1", "L1_ffn_be1", "L1_ffn_m1", "L1_ffn_v1",
        "L1_ffn_W2", "L1_ffn_b2", "L1_ffn_g2", "L1_ffn_be2", "L1_ffn_m2", "L1_ffn_v2", "L1_ffn_Wo", "L1_ffn_bo"]


def kernel(**inputs):
    import numpy as np
    import concourse.bacc as bacc
    from concourse.bass_utils import run_bass_kernel_spmd

    nc = bacc.Bacc("TRN2", target_bir_lowering=False, num_devices=1)
    arrays, args = {}, {}
    for name in _INS:
        a = np.ascontiguousarray(inputs[name])
        arrays[f"in_{name}"] = a
        args[name] = nc.dram_tensor(f"in_{name}", a.shape, mybir.dt.from_np(a.dtype), kind="ExternalInput").ap()
    out = nc.dram_tensor("out", args["x"].shape, F32, kind="ExternalOutput").ap()
    gnn_experts(nc, args, out)
    r = run_bass_kernel_spmd(nc, [arrays], core_ids=[0])
    return r.results[0]["out"]
```

```python
from contextlib import ExitStack

import concourse.bass as bass
from concourse import mybir

F32 = mybir.dt.float32
BF16 = mybir.dt.bfloat16
I32 = mybir.dt.int32
ALU = mybir.AluOpType
ACT = mybir.ActivationFunctionType
AX = mybir.AxisListType
ds = bass.ds

P = 128
LN_EPS = 1e-5
BN_EPS = 0.001
NEG_SLOPE = 0.2
FAR = 1e30
SPREAD = 60.0


class Shapes:

    def __init__(self, x, src, w0, attn, pos, w1, w2, wr, v1):
        self.N, self.D = x.shape
        self.E = src.shape[0]
        self.C = w0.shape[0]
        self.H, self.HD = attn.shape[1:]
        self.PD = pos.shape[2]
        self.X, _, self.F = w1.shape
        self.X2, self.F2 = v1.shape
        self.T = -(-self.N // P)
        self.G = 7
        self.NG = self.T // self.G
        self.W = self.G * P
        self.HW = self.W // 2
        self.LAST = self.N - (self.T - 1) * P
        self.KC = self.D // P
        self.HC = self.F // P
        self.K = 8
        self.HK = self.K // 2
        self.B = P * self.K
        self.NR = 4
        self.NB = self.NR * -(-self.E // (self.NR * self.B))
        self.U = 4
        self.US = self.U * P
        self.NU = -(-self.T // self.U)
        self.S = (self.NU + 1) * self.US
        self.R = self.D + 2
        self.A = self.HD + 1
        assert self.T % self.G == 0 and self.D % P == 0 and self.H * self.HD == self.D
        assert self.C + self.PD == self.D and self.HW <= 512 and self.X == self.X2


def after(n):
    return n + 1


class Chain:

    def __init__(self, eng, sem, per=0):
        self.eng, self.sem, self.per, self.base, self.n = eng, sem, per, 0, 0

    def begin(self, i):
        self.base, self.n = i * self.per, 0

    def link(self, ins):
        self.n += 1
        ins.then_inc(self.sem, 1)
        self.eng.wait_ge(self.sem, after(self.base + self.n))

    def end(self):
        assert self.n == self.per, (self.n, self.per)


class Core:

    def __init__(self, nc, z):
        self.nc, self.z, self.phase = nc, z, "all"
        self.fresh = []

    def sb(self, ctx, name, shape, dt=F32):
        return ctx.enter_context(self.nc.sbuf_tensor(f"{self.phase}_{name}", shape, dt))

    def ps(self, ctx, name, shape, dt=F32):
        bank = ctx.enter_context(self.nc.psum_tensor(f"{self.phase}_{name}", [P, 2048 // (2 if dt == BF16 else 4)], dt))
        if len(shape) == 2:
            return bank[:, 0:shape[1]]
        size = 1
        for n in shape[1:]:
            size *= n
        names = "abcd"[:len(shape) - 1]
        sizes = dict(zip(names, shape[1:]))
        return bank[:, 0:size].rearrange(f"p ({' '.join(names)}) -> p {' '.join(names)}", **sizes)

    def sem(self, ctx, name):
        sem = ctx.enter_context(self.nc.semaphore(f"{self.phase}_{name}"))
        self.fresh.append(sem)
        return sem

    def pool_dma_sem(self, ctx, name):
        return ctx.enter_context(self.nc.semaphore(f"{self.phase}_{name}"))

    def block(self, ctx):
        with self.nc.Block() as first:
            @first.sync
            def _(sp):
                for sem in self.fresh:
                    sp.sem_inc(sem, 1)
        self.fresh = []
        return ctx.enter_context(self.nc.Block())


def alone(c, eng):
    eng.sem_inc(c.pace, 1)


def spread(ap, shape):
    return ap.broadcast_to(shape)


def prepare(c, x, src, dst, w0, attn_src, attn_dst, pos_src, pos_dst, bn_in, bn_out):
    nc, z = c.nc, c.z
    T, K, NB, B, H, HD, KC, X = z.T, z.K, z.NB, z.B, z.H, z.HD, z.KC, z.X
    NT = -(-NB // P)
    full, rest = z.E // B, z.E % B
    c.phase = "prepare"
    with ExitStack() as ctx:
        s = lambda n: c.sem(ctx, n)
        posw = c.sb(ctx, "posw", [P, KC, 2 * H])
        ablk = c.sb(ctx, "ablk", [P, KC, 2 * H])
        wt = c.sb(ctx, "wt", [P, KC, KC * P])
        edge_i = c.sb(ctx, "edge_i", [P, 2, NT, B], I32)
        edge_f = c.sb(ctx, "edge_f", [P, 2, NT, B])
        span_i = c.sb(ctx, "span_i", [P, NT, 2], I32)
        iota_i = c.sb(ctx, "iota_i", [P, P], I32)
        base_i = c.sb(ctx, "base_i", [P, T], I32)
        node_i = c.sb(ctx, "node_i", [P, T], I32)
        home_i = c.sb(ctx, "home_i", [P, X], I32)
        before_f = c.sb(ctx, "before_f", [P, P])
        ones_f = c.sb(ctx, "ones_f", [P, P])
        bn = c.sb(ctx, "bn", [P, 2, 5, X, z.F2 // P])
        tmp = c.sb(ctx, "bn_tmp", [P, 2, X, z.F2 // P])
        tp = [c.ps(ctx, f"tp{i}", [P, 512]) for i in range(2)]
        wa = c.ps(ctx, "wa", [P, KC, 2 * H])
        x_in, w_in, e_in, bn_ld = s("x_in"), s("w_in"), s("e_in"), s("bn_ld")
        pool_step, consts, edges_f, dve_step = s("pool_step"), s("consts"), s("edges_f"), s("dve_step")
        turned, copied, span_moved, wa_ready, sd_ready, bn_ready, bn_st = (
            s("turned"), s("copied"), s("span_moved"), s("wa_ready"), s("sd_ready"), s("bn_ready"), s("bn_st"))
        tmp_out = [[bn[:, n, 1, :, :], bn[:, n, 2, :, :]] for n in range(2)]
        block = c.block(ctx)

        @block.gpsimd
        def _(pool):
            pool.memset(c.wall[:, :, :], 0.0)
            pool.memset(posw[:, :, :], 0.0)
            pool.memset(ablk[:, :, :], 0.0)
            pool.memset(c.res[:, T - 1, :], 0.0)
            pool.memset(edge_i[:, 0, NT - 1, :], 0)
            pool.memset(edge_i[:, 1, NT - 1, :], T * P + 1).then_inc(pool_step, 1)
            pool.memset(c.src_all[:, NB * K:(NB + z.NR) * K], 0)
            pool.memset(c.ident[:, :], 0.0)
            pool.memset(c.tri[:, :, :], 0.0)
            pool.memset(before_f[:, :], 0.0)
            pool.memset(ones_f[:, :], 1.0)
            pool.memset(c.sel[:, :, :], 0.0)
            pool.memset(c.eps[:, 0:1], LN_EPS)
            pool.memset(c.eps[:, 1:2], BN_EPS)
            pool.iota(iota_i[:, :], pattern=[[1, P]], base=0, channel_multiplier=0)
            pool.iota(node_i[:, :], pattern=[[P, T]], base=0, channel_multiplier=1)
            pool.iota(home_i[:, :], pattern=[[z.S, X]], base=0, channel_multiplier=0)
            pool.iota(base_i[:, :], pattern=[[P, T]], base=0, channel_multiplier=0).then_inc(pool_step, 1)
            pool.wait_ge(pool_step, after(2))
            pool.affine_select(out=c.ident[:, :], in_=c.ident[:, :], compare_op=ALU.not_equal, fill=1.0,
                               base=0, pattern=[[-1, P]], channel_multiplier=1)
            pool.affine_select(out=c.tri[:, :, :], in_=c.tri[:, :, :], compare_op=ALU.is_ge, fill=1.0,
                               base=0, pattern=[[-1, X], [1, X]], channel_multiplier=0)
            pool.affine_select(out=before_f[:, :], in_=before_f[:, :], compare_op=ALU.is_ge, fill=1.0,
                               base=0, pattern=[[-1, P]], channel_multiplier=1)
            pool.affine_select(out=c.sel[:, :, :], in_=c.sel[:, :, :], compare_op=ALU.not_equal, fill=1.0,
                               base=0, pattern=[[-1, H], [0, P]], channel_multiplier=1).then_inc(consts, 1)

        @block.sync
        def _(sp):
            sp.wait_ge(pool_step, after(1))
            for n, e in enumerate((src, dst)):
                for t in range(NT):
                    rows = min(full - t * P, P)
                    sp.dma_start(edge_i[0:rows, n, t, :],
                                 e[t * P * B:(t * P + rows) * B].rearrange("(s e) -> s e", e=B)).then_inc(e_in, 16)
                    if rows < P and rest:
                        sp.dma_start(edge_i[rows:rows + 1, n, t, 0:rest],
                                     e[full * B:z.E].rearrange("(s e) -> s e", s=1)).then_inc(e_in, 16)
            sp.dma_start(c.wall[:, 0, 0:z.D], w0[0:P, :]).then_inc(w_in, 16)
            sp.dma_start(c.wall[0:z.C - P, 1, 0:z.D], w0[P:z.C, :]).then_inc(w_in, 16)
            for n, a in enumerate((attn_src, attn_dst)):
                for h in range(H):
                    at = h * HD
                    sp.dma_start(ablk[at % P:at % P + HD, at // P, n * H + h:n * H + h + 1],
                                 a[0, h, :].rearrange("(d o) -> d o", o=1)).then_inc(w_in, 16)
            for n, a in enumerate((pos_src, pos_dst)):
                sp.dma_start(posw[z.C - P:P, 1, n * H:(n + 1) * H],
                             a[0, :, :].rearrange("h p -> p h"), allow_slow_non_contiguous=True).then_inc(w_in, 16)
            for n, layer in enumerate(bn_in):
                for m, a in enumerate(layer):
                    for e in range(X):
                        sp.dma_start(bn[:, n, m, e, :], a[e, :].rearrange("(k p) -> p k", p=P),
                                     allow_slow_non_contiguous=True).then_inc(bn_ld, 16)
            sp.wait_ge(dve_step, after(4))
            for t in range(NT):
                rows = min(NB - t * P, P)
                sp.dma_start(c.span_d[t * P:t * P + rows, :], span_i[0:rows, t, :]).then_inc(span_moved, 16)
            sp.wait_ge(span_moved, after(16 * NT))
            sp.dma_start(c.spans[0:1, :], c.span_d.rearrange("(o s) c -> o (s c)", o=1)).then_inc(span_moved, 16)
            sp.wait_ge(bn_ready, after(1))
            for n in range(2):
                for m in range(2):
                    sp.dma_start(bn_out[n][m].rearrange("e p k -> p e k"), tmp_out[n][m]).then_inc(bn_st, 16)
            sp.wait_ge(bn_st, after(16 * 4))
            sp.wait_ge(span_moved, after(16 * (NT + 1)))
            sp.wait_ge(x_in, after(32))

        @block.scalar
        def _(act):
            act.dma_start(c.res[:, 0:T - 1, :],
                          x[0:(T - 1) * P, :].rearrange("(t p) d -> p t d", p=P)).then_inc(x_in, 16)
            act.wait_ge(pool_step, after(1))
            act.dma_start(c.res[0:z.LAST, T - 1, :], x[(T - 1) * P:z.N, :]).then_inc(x_in, 16)
            act.wait_ge(consts, after(1))
            q = 0
            for n, table in enumerate((c.src_all, c.dst_all)):
                for t in range(NT):
                    rows = min(NB - t * P, P)
                    for k in range(K):
                        act.wait_ge(turned, after(q + 1))
                        out = table[:, t * P * K:(t * P + rows) * K].rearrange("p (s k) -> p s k", k=K)[:, :, k]
                        act.activation(out, tp[q % 2][:, 0:rows], ACT.Copy).then_inc(copied, 1)
                        q += 1
            for j in range(KC * KC):
                act.wait_ge(turned, after(q + 1))
                act.activation(wt[:, j // KC, (j % KC) * P:(j % KC + 1) * P], tp[q % 2][:, 0:P], ACT.Copy).then_inc(copied, 1)
                q += 1
            act.wait_ge(bn_ld, after(16 * 10 * X))
            for n in range(2):
                last = act.activation(tmp[:, n, :, :], bn[:, n, 4, :, :], ACT.Sqrt, bias=c.eps[:, 1:2])
            last.then_inc(sd_ready, 1)

        @block.tensor
        def _(pe):
            pe.wait_ge(consts, after(1))
            pe.wait_ge(edges_f, after(1))
            q = 0
            for n in range(2):
                for t in range(NT):
                    rows = min(NB - t * P, P)
                    for k in range(K):
                        if q >= 2:
                            pe.wait_ge(copied, after(q - 1))
                        pe.transpose(tp[q % 2][:, 0:rows],
                                     edge_f[0:rows, n, t, :].rearrange("s (p k) -> s p k", k=K)[:, :, k],
                                     c.ident[0:rows, 0:rows]).then_inc(turned, 1)
                        q += 1
            pe.wait_ge(w_in, after(16 * (4 + 2 * H)))
            for jc in range(KC):
                for kc in range(KC):
                    pe.wait_ge(copied, after(q - 1))
                    pe.transpose(tp[q % 2][:, 0:P], c.wall[:, kc, jc * P:(jc + 1) * P],
                                 c.ident[:, :]).then_inc(turned, 1)
                    q += 1
            pe.wait_ge(copied, after(q))
            for kc in range(KC):
                for jc in range(KC):
                    last = pe.matmul(wa[:, kc, :], wt[:, jc, kc * P:(kc + 1) * P], ablk[:, jc, :],
                                     start=(jc == 0), stop=(jc == KC - 1))
            last.then_inc(wa_ready, 1)

        @block.vector
        def _(dve):
            ch = Chain(dve, dve_step)
            dve.wait_ge(e_in, after(16 * (2 * NT + 2)))
            for n in range(2):
                last = dve.tensor_copy(edge_f[:, n, :, :], edge_i[:, n, :, :])
            last.then_inc(edges_f, 1)
            dve.wait_ge(edges_f, after(1))
            last = dve.tensor_reduce(span_i[:, :, 0], edge_f[:, 1, :, :], AX.X, ALU.min)
            ch.link(dve.tensor_reduce(span_i[:, :, 1], edge_f[:, 1, :, :], AX.X, ALU.max))
            ch.link(dve.tensor_scalar(span_i[:, :, :], span_i[:, :, :], 7, None, ALU.arith_shift_right))
            ch.link(dve.tensor_scalar(span_i[:, :, 1], span_i[:, :, 1], 1.0, float(T), ALU.add, ALU.min))
            ch.link(dve.tensor_scalar(span_i[:, :, 0], span_i[:, :, 0], float(T - 1), None, ALU.min))
            dve.wait_ge(pool_step, after(2))
            dve.tensor_copy(c.iota[:, :], iota_i[:, :])
            dve.tensor_copy(c.base[:, :], base_i[:, :])
            dve.tensor_copy(c.node[:, :], node_i[:, :])
            dve.tensor_copy(c.home[:, :], home_i[:, :])
            dve.wait_ge(consts, after(1))
            dve.tensor_copy(c.ident_b[:, :], c.ident[:, :])
            dve.tensor_copy(c.before[:, :], before_f[:, :])
            dve.tensor_copy(c.ones_b[:, :], ones_f[:, :])
            dve.wait_ge(w_in, after(16 * (4 + 2 * H)))
            dve.wait_ge(wa_ready, after(1))
            dve.tensor_tensor(c.wall[:, :, z.D:], wa[:, :, :], posw[:, :, :], ALU.add)
            dve.wait_ge(sd_ready, after(1))
            ch.link(dve.reciprocal(tmp[:, :, :, :], tmp[:, :, :, :]))
            ch.link(dve.tensor_tensor(bn[:, :, 1, :, :], bn[:, :, 1, :, :], tmp[:, :, :, :], ALU.mult))
            ch.link(dve.tensor_tensor(bn[:, :, 0, :, :], bn[:, :, 0, :, :], bn[:, :, 3, :, :], ALU.subtract))
            ch.link(dve.tensor_tensor(bn[:, :, 0, :, :], bn[:, :, 0, :, :], bn[:, :, 1, :, :], ALU.mult))
            dve.tensor_tensor(bn[:, :, 2, :, :], bn[:, :, 0, :, :], bn[:, :, 2, :, :], ALU.add).then_inc(bn_ready, 1)


def normalise(c, dve, ch, g, stats, mv, sd, rstd, xn, var_ready, sd_ready, nth):
    z = c.z
    alone(c, dve)
    for j in range(z.G):
        last = dve.bn_stats(stats[:, j, :], c.res[:, ds(g * z.G + j, 1), :].rearrange("p a d -> p (a d)"))
    ch.link(last)
    alone(c, dve)
    for j in range(z.G):
        last = dve.bn_aggr(mv[:, j, :], stats[:, j, :])
    last.then_inc(var_ready, 1)
    dve.wait_ge(sd_ready, after(nth))
    ch.link(dve.reciprocal(rstd[:, :], sd[:, :]))
    dve.wait_ge(var_ready, after(nth))
    for j in range(z.G):
        last = dve.tensor_scalar(xn[:, j, 0:z.D], c.res[:, ds(g * z.G + j, 1), :].rearrange("p a d -> p (a d)"),
                                 mv[:, j, 0:1], rstd[:, j:j + 1], ALU.subtract, ALU.mult)
    return last


def project(c, tab, scores):
    nc, z = c.nc, c.z
    G, KC, H = z.G, z.KC, z.H
    WC = z.D + 2 * H
    c.phase = "project"
    with ExitStack() as ctx:
        s = lambda n: c.sem(ctx, n)
        stats = c.sb(ctx, "stats", [P, G, 6])
        mv = c.sb(ctx, "mv", [P, G, 2])
        sd = c.sb(ctx, "sd", [P, G])
        rstd = c.sb(ctx, "rstd", [P, G])
        xn = c.sb(ctx, "xn", [P, G, z.D])
        xt = c.sb(ctx, "xt", [P, G, KC, P])
        rows = c.sb(ctx, "rows", [P, G, WC])
        tp = [c.ps(ctx, f"tp{i}", [P, KC, P]) for i in range(2)]
        ft = [c.ps(ctx, f"ft{i}", [P, 512]) for i in range(2)]
        dve_step, var_ready, sd_ready, xn_ready, turned, xt_ready, ft_ready, rows_ready, stored = (
            s(n) for n in ("dve_step", "var_ready", "sd_ready", "xn_ready", "turned", "xt_ready", "ft_ready", "rows_ready", "stored"))
        block = c.block(ctx)

        @block.vector
        def _(dve):
            ch = Chain(dve, dve_step, 2)
            with dve.Fori(0, z.NG) as g:
                ch.begin(g)
                dve.wait_ge(turned, after(g * G))
                normalise(c, dve, ch, g, stats, mv, sd, rstd, xn, var_ready, sd_ready, g + 1).then_inc(xn_ready, 1)
                ch.end()
                dve.wait_ge(stored, after(g * 32))
                for j in range(G):
                    dve.wait_ge(ft_ready, after(g * G + j + 1))
                    dve.tensor_copy(rows[:, j, :], ft[j % 2][:, 0:WC]).then_inc(rows_ready, 1)

        @block.scalar
        def _(act):
            with act.Fori(0, z.NG) as g:
                act.wait_ge(var_ready, after(g + 1))
                act.activation(sd[:, :], mv[:, :, 1], ACT.Sqrt, bias=c.eps[:, 0:1]).then_inc(sd_ready, 1)
                for j in range(G):
                    act.wait_ge(turned, after(g * G + j + 1))
                    if j == 0:
                        act.wait_ge(ft_ready, after(g * G))
                    act.activation(xt[:, j, :, :], tp[j % 2][:, :, :], ACT.Copy).then_inc(xt_ready, 1)

        @block.tensor
        def _(pe):
            with pe.Fori(0, z.NG) as g:
                pe.wait_ge(xn_ready, after(g + 1))
                for j in range(G):
                    pe.wait_ge(xt_ready, after(g * G + max(j - 1, 0)))
                    for k in range(KC):
                        last = pe.transpose(tp[j % 2][:, k, :], xn[:, j, k * P:(k + 1) * P], c.ident[:, :])
                    last.then_inc(turned, 1)
                for j in range(G):
                    pe.wait_ge(xt_ready, after(g * G + j + 1))
                    pe.wait_ge(rows_ready, after(g * G + max(j - 1, 0)))
                    for k in range(KC):
                        last = pe.matmul(ft[j % 2][:, 0:WC], xt[:, j, k, :], c.wall[:, k, :],
                                         start=(k == 0), stop=(k == KC - 1))
                    last.then_inc(ft_ready, 1)

        @block.sync
        def _(sp):
            with sp.Fori(0, z.NG) as g:
                sp.wait_ge(rows_ready, after(g * G + G))
                sp.dma_start(tab[ds(g * z.W, z.W), :].rearrange("(t p) d -> p t d", p=P),
                             rows[:, :, 0:z.D + H]).then_inc(stored, 16)
                sp.dma_start(scores[ds(g * z.W, z.W), :].rearrange("(t p) d -> p t d", p=P),
                             rows[:, :, z.D:]).then_inc(stored, 16)
            sp.wait_ge(stored, after(z.NG * 32))


def width(c, eng):
    r = eng.alloc_register(f"{c.phase}_wide")
    eng.reg_load(r, c.wide[0:1, 0:1])
    return r


def unless_wide(c, eng):
    return eng.If_eq(width(c, eng), 0)


def if_wide(c, eng):
    return eng.If_ne(width(c, eng), 0)


def load_span(eng, c, sc):
    lo = eng.value_load(c.spans[0:1, ds(sc * 2, 1)], min_val=0, max_val=c.z.T - 1)
    hi = eng.value_load(c.spans[0:1, ds(sc * 2 + 1, 1)], min_val=1, max_val=c.z.T)
    return lo, hi


def gather_rows(c, pool, tab, idx, rows, idx_ready, rows_free, gathered):
    z = c.z
    depth, parts = len(rows), len(gathered[0])
    with pool.Fori(0, z.NB // depth) as i:
        for u in range(depth):
            pool.wait_ge(idx_ready, after(depth * i + u + 1))
            pool.wait_ge(rows_free, after(depth * i + u + 1))
            alone(c, pool)
            for k in range(z.K):
                pool.indirect_dma_start(rows[u][:, k, :], None, tab,
                                        bass.IndirectOffsetOnAxis(ap=idx[u][:, k:k + 1], axis=0)
                                        ).then_inc(gathered[u][k * parts // z.K], 16)


def copy_indices(c, act, sc, idx, u):
    return act.activation(idx[u][:, :], c.src_all[:, ds(sc * c.z.K, c.z.K)], ACT.Copy)


def bound_scores(c, scores):
    nc, z = c.nc, c.z
    c.phase = "bound_scores"
    T, H = z.T, z.H
    with ExitStack() as ctx:
        s = lambda n: c.sem(ctx, n)
        sc = c.sb(ctx, "scores", [P, T, 2 * H])
        neg = c.sb(ctx, "neg", [P, T, H])
        ends = c.sb(ctx, "ends", [P, 2])
        both = c.sb(ctx, "both", [2, 1])
        m = c.sb(ctx, "m", [P, T, H])
        pq = c.sb(ctx, "pq", [P, T, 2, H])
        part = c.sb(ctx, "part", [P, T, 2, H])
        wide_f = c.sb(ctx, "wide_f", [1, 1])
        tp = c.ps(ctx, "tp", [P, P])
        bp = c.ps(ctx, "bp", [P, 2])
        s_in, dve_step, ends_ready, ends_moved, both_ready, pq_z, pq_ready = (
            s(n) for n in ("s_in", "dve_step", "ends_ready", "ends_moved", "both_ready", "pq_z", "pq_ready"))
        block = c.block(ctx)

        @block.sync
        def _(sp):
            sp.dma_start(sc[:, :, :], scores.rearrange("(t p) c -> p t c", p=P)).then_inc(s_in, 16)
            sp.wait_ge(s_in, after(16))

        @block.tensor
        def _(pe):
            pe.wait_ge(ends_ready, after(1))
            pe.transpose(tp[0:2, :], ends[:, :], c.ident[:, :]).then_inc(ends_moved, 1)
            pe.wait_ge(both_ready, after(1))
            pe.matmul(bp[:, :], spread(both[:, :], [2, P]), c.ident[0:2, 0:2], start=True, stop=True).then_inc(ends_moved, 1)

        @block.scalar
        def _(act):
            act.wait_ge(pq_z, after(1))
            act.activation(pq[:, :, :, :], pq[:, :, :, :], ACT.Exp).then_inc(pq_ready, 1)

        @block.vector
        def _(dve):
            ch = Chain(dve, dve_step)
            dve.wait_ge(s_in, after(16))
            ch.link(dve.tensor_scalar(neg[:, :, :], sc[:, :, 0:H], -1.0, None, ALU.mult))
            dve.tensor_reduce(ends[:, 0:1], sc[:, :, 0:H], AX.XY, ALU.max)
            dve.tensor_reduce(ends[:, 1:2], neg[:, :, :], AX.XY, ALU.max).then_inc(ends_ready, 1)
            dve.wait_ge(ends_moved, after(1))
            dve.tensor_reduce(both[:, :], tp[0:2, :], AX.X, ALU.max).then_inc(both_ready, 1)
            dve.wait_ge(ends_moved, after(2))
            ch.link(dve.tensor_copy(ends[:, :], bp[:, :]))
            ch.link(dve.tensor_tensor(wide_f[:, :], ends[0:1, 0:1], ends[0:1, 1:2], ALU.add))
            dve.tensor_scalar(c.wide[:, :], wide_f[:, :], SPREAD, None, ALU.is_gt)
            dve.tensor_scalar(c.less_top[:, 0:1], ends[:, 0:1], -1.0, None, ALU.mult)
            dve.tensor_scalar(c.less_top[:, 1:2], ends[:, 0:1], -NEG_SLOPE, None, ALU.mult)
            ch.link(dve.tensor_scalar(pq[:, :, 0, :], sc[:, :, H:], ends[:, 0:1], None, ALU.add))
            dve.tensor_scalar(pq[:, :, 1, :], pq[:, :, 0, :], NEG_SLOPE, None, ALU.mult)
            ch.link(dve.scalar_tensor_tensor(m[:, :, :], pq[:, :, 0, :], NEG_SLOPE, pq[:, :, 0, :], ALU.mult, ALU.max))
            for n in range(2):
                last = dve.tensor_tensor(pq[:, :, n, :], pq[:, :, n, :], m[:, :, :], ALU.subtract)
            last.then_inc(pq_z, 1)
            dve.wait_ge(pq_ready, after(1))
            flat = pq[:, :, :, :].rearrange("p t n h -> p t (n h)")
            left = part[:, :, :, :].rearrange("p t n h -> p t (n h)")
            ch.link(dve.tensor_copy(c.factors[:, :, 0, :], flat))
            ch.link(dve.tensor_tensor(left, flat, c.factors[:, :, 0, :], ALU.subtract))
            ch.link(dve.tensor_copy(c.factors[:, :, 1, :], left))
            ch.link(dve.tensor_tensor(left, left, c.factors[:, :, 1, :], ALU.subtract))
            dve.tensor_copy(c.factors[:, :, 2, :], left)


def attend_bounded(c, tab):
    nc, z = c.nc, c.z
    c.phase = "attend_bounded"
    T, K, HK, NR, H, HD, D, A = z.T, z.K, z.HK, z.NR, z.H, z.HD, z.D, z.A
    KV = HK - 1
    with ExitStack() as ctx:
        s = lambda n: c.sem(ctx, n)
        rows = [c.sb(ctx, f"rows{u}", [P, K, D + H]) for u in range(NR)]
        idx = [c.sb(ctx, f"idx{u}", [P, K], I32) for u in range(NR)]
        ab = [c.sb(ctx, f"ab{u}", [P, K, 2, H]) for u in range(NR)]
        dl = [c.sb(ctx, f"dl{u}", [P, K]) for u in range(2)]
        oh = [[c.sb(ctx, f"oh{u}{h}", [P, HK, P]) for h in range(2)] for u in range(2)]
        oht = [c.sb(ctx, f"oht{h}", [P, HK * P], BF16) for h in range(2)]
        pair = [c.sb(ctx, f"pair{h}", [P, HK, 2, H]) for h in range(2)]
        msg = [c.sb(ctx, f"msg{h}", [P, HK, H, A]) for h in range(2)]
        tp = [c.ps(ctx, f"tp{h}", [P, HK * P], BF16) for h in range(2)]
        fe = [c.ps(ctx, f"fe{h}", [P, HK, 3, 2 * H]) for h in range(2)]
        factor = [c.sb(ctx, f"factor{h}", [P, HK, 2 * H]) for h in range(2)]
        accp = c.ps(ctx, "accp", [P, 512])
        gathered = [[g] for g in c.gathered]
        names = ("idx_ready", "rows_free", "ab_ready", "dve_step", "onehot_ready", "turned", "oht_ready", "fe_ready",
                 "w_ready", "msg_ready", "last_msg_ready", "main_done", "acc_added", "final_step")
        (idx_ready, rows_free, ab_ready, dve_step, onehot_ready, turned, oht_ready, fe_ready,
         w_ready, msg_ready, last_msg_ready, main_done, acc_added, final_step) = (s(n) for n in names)
        block = c.block(ctx)

        @block.gpsimd
        def _(pool):
            with unless_wide(c, pool):
                gather_rows(c, pool, tab, idx, rows, idx_ready, rows_free, gathered)

        @block.scalar
        def _(act):
            with unless_wide(c, act):
                for u in range(NR):
                    copy_indices(c, act, u, idx, u).then_inc(idx_ready, 1)
                r = act.alloc_register(f"{c.phase}_pairs")
                act.reg_mov(r, 0)
                with act.Fori(0, z.NB // NR) as i:
                    for u in range(NR):
                        sc = NR * i + u
                        act.wait_ge(gathered[u][0], (i + 1) * 16 * K)
                        alone(c, act)
                        copy_indices(c, act, sc + NR, idx, u).then_inc(idx_ready, 1)
                        lo, hi = load_span(act, c, sc)
                        act.activation(ab[u][:, :, 0, :], rows[u][:, :, D:], ACT.Exp, bias=c.less_top[:, 0:1])
                        act.activation(ab[u][:, :, 1, :], rows[u][:, :, D:], ACT.Exp, bias=c.less_top[:, 1:2],
                                       scale=NEG_SLOPE).then_inc(ab_ready, 1)
                        with act.Fori(lo, hi) as b:
                            t = act.snap(r)
                            for h in range(2):
                                act.wait_ge(turned, after(2 * t + h + 1))
                                act.activation(oht[h][:, :], tp[h][:, :], ACT.Copy).then_inc(oht_ready, 1)
                            for h in range(2):
                                act.wait_ge(w_ready, after(6 * t + 3 * h + 3))
                                for n in range(H):
                                    last = act.activation(msg[h][:, KV, n, 0:HD], rows[u][:, h * HK + KV, n * HD:(n + 1) * HD],
                                                          ACT.Copy, scale=msg[h][:, KV, n, HD:])
                                last.then_inc(last_msg_ready, 1)
                            act.reg_add(r, r, 1)

        @block.tensor
        def _(pe):
            with unless_wide(c, pe):
                pe.sem_inc(main_done, 2)
                r = pe.alloc_register(f"{c.phase}_pairs")
                pe.reg_mov(r, 0)
                with pe.Fori(0, z.NB // NR) as i:
                    for u in range(NR):
                        lo, hi = load_span(pe, c, NR * i + u)
                        with pe.Fori(lo, hi) as b:
                            t = pe.snap(r)
                            for h in range(2):
                                pe.wait_ge(onehot_ready, after(2 * t + h + 1))
                                for k in range(HK):
                                    bits = oh[u % 2][h][:, k, :].bitcast(BF16).rearrange("p (d w) -> p d w", w=2)[:, :, 1]
                                    last = pe.transpose(tp[h][:, k * P:(k + 1) * P], bits, c.ident_b[:, :])
                                last.then_inc(turned, 1)
                            for h in range(2):
                                pe.wait_ge(oht_ready, after(2 * t + h + 1))
                                for k in range(HK):
                                    last = pe.matmul(fe[h][:, k, :, :].rearrange("p n f -> p (n f)"), oht[h][:, k * P:(k + 1) * P],
                                                     c.factors[:, ds(b, 1), :, :].rearrange("p a n f -> p (a n f)"),
                                                     start=True, stop=True)
                                last.then_inc(fe_ready, 1)
                            pe.wait_ge(acc_added, after(t))
                            for h in range(2):
                                for k in range(HK):
                                    if k == 0:
                                        pe.wait_ge(msg_ready, after(2 * t + h + 1))
                                    if k == KV:
                                        pe.wait_ge(last_msg_ready, after(2 * t + h + 1))
                                    last = pe.matmul(accp[:, 0:H * A], oh[u % 2][h][:, k, :], msg[h][:, k, :, :].rearrange("p h a -> p (h a)"),
                                                     start=(h == 0 and k == 0), stop=(h == 1 and k == HK - 1))
                                last.then_inc(main_done, 1)
                            pe.reg_add(r, r, 1)

        @block.vector
        def _(dve):
            with unless_wide(c, dve):
                dve.memset(c.acc[:, :, :], 0.0).then_inc(final_step, 1)
                dve.sem_inc(rows_free, NR)
                dve.wait_ge(final_step, after(1))
                r = dve.alloc_register(f"{c.phase}_pairs")
                dve.reg_mov(r, 0)
                last_b = dve.alloc_register(f"{c.phase}_last_block")
                dve.reg_mov(last_b, 0)
                used = [dve.alloc_register(f"{c.phase}_used{u}") for u in range(2)]
                for u in range(2):
                    dve.reg_mov(used[u], 0)

                def take(b):
                    a_b = c.acc[:, ds(b, 1), :].rearrange("p a d -> p (a d)")
                    return dve.tensor_tensor(a_b, a_b, accp[:, 0:H * A], ALU.add)

                with dve.Fori(0, z.NB // NR) as i:
                    for u in range(NR):
                        sc = NR * i + u
                        lo, hi = load_span(dve, c, sc)
                        with dve.Fori(lo, hi) as b:
                            t = dve.snap(r)
                            w = dve.snap(used[u % 2])
                            dve.tensor_scalar(dl[u % 2][:, :], c.dst_all[:, ds(sc * K, K)], c.base[:, ds(b, 1)], None,
                                              ALU.subtract).then_inc(dve_step, 1)
                            dve.wait_ge(dve_step, after(t + 1))
                            for h in range(2):
                                dve.wait_ge(main_done, after(2 * w + h + 1))
                                dve.tensor_tensor(oh[u % 2][h][:, :, :], spread(c.iota[:, :].unsqueeze(1), [P, HK, P]),
                                                  spread(dl[u % 2][:, h * HK:(h + 1) * HK].unsqueeze(2), [P, HK, P]),
                                                  ALU.is_equal).then_inc(onehot_ready, 1)
                            with dve.If_ne(r, 0):
                                dve.wait_ge(main_done, after(2 * t + 2))
                                take(dve.snap(last_b, min_val=0, max_val=T - 1)).then_inc(acc_added, 1)
                            dve.wait_ge(ab_ready, after(sc + 1))
                            for h in range(2):
                                dve.wait_ge(fe_ready, after(2 * t + h + 1))
                                dve.tensor_reduce(factor[h][:, :, :], fe[h][:, :, :, :].rearrange("p k n f -> p k f n"),
                                                  AX.X, ALU.add).then_inc(w_ready, 1)
                                dve.wait_ge(w_ready, after(6 * t + 3 * h + 1))
                                dve.tensor_tensor(pair[h][:, :, :, :].rearrange("p k n h -> p k (n h)"),
                                                  ab[u][:, h * HK:(h + 1) * HK, :, :].rearrange("p k n h -> p k (n h)"),
                                                  factor[h][:, :, :], ALU.mult).then_inc(w_ready, 1)
                                dve.wait_ge(w_ready, after(6 * t + 3 * h + 2))
                                dve.tensor_tensor(msg[h][:, :, :, HD], pair[h][:, :, 0, :], pair[h][:, :, 1, :], ALU.max).then_inc(w_ready, 1)
                                dve.wait_ge(w_ready, after(6 * t + 3 * h + 3))
                                dve.tensor_tensor(msg[h][:, 0:KV, :, 0:HD],
                                                  rows[u][:, h * HK:h * HK + KV, 0:D].rearrange("p k (h d) -> p k h d", h=H),
                                                  spread(msg[h][:, 0:KV, :, HD:], [P, KV, H, HD]), ALU.mult).then_inc(msg_ready, 1)
                            dve.reg_add(r, r, 1)
                            dve.reg_mov(used[u % 2], r)
                            dve.reg_mov(last_b, b)
                        dve.wait_ge(msg_ready, after(dve.snap(r) * 2))
                        alone(c, dve)
                        dve.wait_ge(last_msg_ready, after(dve.snap(r) * 2))
                        dve.sem_inc(rows_free, 1)
                dve.wait_ge(main_done, after(dve.snap(r) * 2 + 2))
                fin = Chain(dve, final_step)
                fin.n = 1
                fin.link(take(dve.snap(last_b, min_val=0, max_val=T - 1)))
                weigh(c, fin, dve)


def weigh(c, fin, dve):
    z = c.z
    parts = c.acc[:, :, :].rearrange("p t (h a) -> p (t h) a", a=z.A)
    fin.link(dve.tensor_scalar(parts[:, :, z.HD:], parts[:, :, z.HD:], 1e-30, None, ALU.max))
    fin.link(dve.reciprocal(parts[:, :, z.HD:], parts[:, :, z.HD:]))
    dve.tensor_tensor(parts[:, :, 0:z.HD], parts[:, :, 0:z.HD], spread(parts[:, :, z.HD:], [P, z.T * z.H, z.HD]), ALU.mult)


def attend(c, tab, scores):
    nc, z = c.nc, c.z
    T, K, HK, H, HD, D, A = z.T, z.K, z.HK, z.H, z.HD, z.D, z.A
    c.phase = "attend"
    with ExitStack() as ctx:
        s = lambda n: c.sem(ctx, n)
        rows = [c.sb(ctx, f"rows{u}", [P, K, D + H]) for u in range(2)]
        idx = [c.sb(ctx, f"idx{u}", [P, K], I32) for u in range(2)]
        ad = c.sb(ctx, "ad", [P, T, 2 * H])
        top = c.sb(ctx, "top", [P, T, H])
        dl = c.sb(ctx, "dl", [P, K])
        oh = [c.sb(ctx, f"oh{h}", [P, HK, P]) for h in range(2)]
        oht = [c.sb(ctx, f"oht{h}", [P, HK * P]) for h in range(2)]
        pen = [c.sb(ctx, f"pen{h}", [P, HK * P]) for h in range(2)]
        ast = [c.sb(ctx, f"ast{h}", [H, HK * P]) for h in range(2)]
        junk = c.sb(ctx, "junk", [P, HK * P])
        run = c.sb(ctx, "run", [P, 3, H])
        adm = c.sb(ctx, "adm", [P, 2, 2 * H])
        fade = c.sb(ctx, "fade", [P, 2, H])
        zz = [c.sb(ctx, f"zz{h}", [P, HK, H]) for h in range(2)]
        msg = [c.sb(ctx, f"msg{h}", [P, HK, H, A]) for h in range(2)]
        tp = [c.ps(ctx, f"tp{h}", [P, HK * P]) for h in range(2)]
        ade = [c.ps(ctx, f"ade{h}", [P, HK, 2 * H]) for h in range(2)]
        bc = [c.ps(ctx, f"bc{h}", [P, HK * P]) for h in range(2)]
        astp = c.ps(ctx, "astp", [P, HK * P])
        accp = c.ps(ctx, "accp", [P, 512])
        gathered = [c.gathered[2 * u:2 * u + 2] for u in range(2)]
        names = ("idx_ready", "rows_free", "ad_in", "cleared", "dve_step", "onehot_ready",
                 "turned", "oht_ready", "pen_ready", "ast_turned", "ast_ready", "bc_ready", "bc_used",
                 "top_ready", "fade_ready", "fade_z", "ade_ready", "z_ready", "w_ready", "msg_ready", "main_done", "acc_added")
        (idx_ready, rows_free, ad_in, cleared, dve_step, onehot_ready,
         turned, oht_ready, pen_ready, ast_turned, ast_ready, bc_ready, bc_used,
         top_ready, fade_ready, fade_z, ade_ready, z_ready, w_ready, msg_ready, main_done, acc_added) = (s(n) for n in names)
        block = c.block(ctx)

        @block.sync
        def _(sp):
            sp.dma_start(ad[:, :, :], scores.rearrange("(t p) c -> p t c", p=P)).then_inc(ad_in, 16)
            sp.wait_ge(ad_in, after(16))

        @block.gpsimd
        def _(pool):
            with if_wide(c, pool):
                gather_rows(c, pool, tab, idx, rows, idx_ready, rows_free, gathered)

        @block.scalar
        def _(act):
            with if_wide(c, act):
                for u in range(2):
                    copy_indices(c, act, u, idx, u).then_inc(idx_ready, 1)
                r = act.alloc_register(f"{c.phase}_pairs")
                act.reg_mov(r, 0)
                with act.Fori(0, z.NB // 2) as i:
                    for u in range(2):
                        sc = 2 * i + u
                        lo, hi = load_span(act, c, sc)
                        with act.Fori(lo, hi) as b:
                            t = act.snap(r)
                            for h in range(2):
                                act.wait_ge(turned, after(2 * t + h + 1))
                                act.activation(oht[h][:, :], tp[h][:, :], ACT.Copy).then_inc(oht_ready, 1)
                                act.activation(pen[h][:, :], tp[h][:, :], ACT.Copy, scale=FAR, bias=-FAR).then_inc(pen_ready, 1)
                                act.wait_ge(ast_turned, after(2 * t + h + 1))
                                act.activation(ast[h][:, :], astp[0:H, :], ACT.Copy).then_inc(ast_ready, 1)
                            act.wait_ge(fade_z, after(t + 1))
                            act.activation(fade[:, 1, :], fade[:, 0, :], ACT.Exp).then_inc(fade_ready, 1)
                            for h in range(2):
                                act.wait_ge(z_ready, after(2 * t + h + 1))
                                act.activation(msg[h][:, :, :, HD], zz[h][:, :, :], ACT.Exp).then_inc(w_ready, 1)
                            act.reg_add(r, r, 1)
                        for h in range(2):
                            act.wait_ge(gathered[u][h], (i + 1) * 16 * HK)
                        alone(c, act)
                        copy_indices(c, act, sc + 2, idx, u).then_inc(idx_ready, 1)

        @block.tensor
        def _(pe):
            with if_wide(c, pe):
                pe.sem_inc(main_done, 2)
                r = pe.alloc_register(f"{c.phase}_pairs")
                pe.reg_mov(r, 0)
                with pe.Fori(0, z.NB // 2) as i:
                    for u in range(2):
                        lo, hi = load_span(pe, c, 2 * i + u)
                        with pe.Fori(lo, hi) as b:
                            t = pe.snap(r)
                            for h in range(2):
                                pe.wait_ge(onehot_ready, after(2 * t + h + 1))
                                for k in range(HK):
                                    last = pe.transpose(tp[h][:, k * P:(k + 1) * P], oh[h][:, k, :], c.ident[:, :])
                                last.then_inc(turned, 1)
                                pe.wait_ge(gathered[u][h], (i + 1) * 16 * HK)
                                pe.wait_ge(ast_ready, after(2 * t + h))
                                for k in range(HK):
                                    last = pe.transpose(astp[0:H, k * P:(k + 1) * P], rows[u][:, h * HK + k, D:], c.ident[:, :])
                                last.then_inc(ast_turned, 1)
                                pe.wait_ge(ast_ready, after(2 * t + h + 1))
                                for n in range(H):
                                    pe.wait_ge(bc_used, after(t * 2 * H + max(h * H + n - 1, 0)))
                                    pe.matmul(bc[n % 2][:, :], c.sel[0:H, n, :], ast[h][:, :], start=True, stop=True).then_inc(bc_ready, 1)
                            pe.wait_ge(top_ready, after(t + 1))
                            for h in range(2):
                                pe.wait_ge(oht_ready, after(2 * t + h + 1))
                                for k in range(HK):
                                    last = pe.matmul(ade[h][:, k, :], oht[h][:, k * P:(k + 1) * P], adm[:, 0, :], start=True, stop=True)
                                last.then_inc(ade_ready, 1)
                            pe.wait_ge(acc_added, after(t))
                            for h in range(2):
                                pe.wait_ge(msg_ready, after(2 * t + h + 1))
                                for k in range(HK):
                                    last = pe.matmul(accp[:, 0:H * A], oh[h][:, k, :], msg[h][:, k, :, :].rearrange("p h a -> p (h a)"),
                                                     start=(h == 0 and k == 0), stop=(h == 1 and k == HK - 1))
                                last.then_inc(main_done, 1)
                            pe.reg_add(r, r, 1)

        @block.vector
        def _(dve):
            with if_wide(c, dve):
                dve.memset(c.acc[:, :, :], 0.0)
                dve.memset(top[:, :, :], -FAR).then_inc(cleared, 1)
                dve.sem_inc(rows_free, 2)
                dve.wait_ge(ad_in, after(16))
                dve.wait_ge(cleared, after(1))
                ch = Chain(dve, dve_step, 11)
                r = dve.alloc_register(f"{c.phase}_pairs")
                dve.reg_mov(r, 0)
                with dve.Fori(0, z.NB // 2) as i:
                    for u in range(2):
                        sc = 2 * i + u
                        lo, hi = load_span(dve, c, sc)
                        with dve.Fori(lo, hi) as b:
                            t = dve.snap(r)
                            ch.begin(t)
                            ch.link(dve.tensor_scalar(dl[:, :], c.dst_all[:, ds(sc * K, K)], c.base[:, ds(b, 1)], None, ALU.subtract))
                            for h in range(2):
                                dve.wait_ge(main_done, after(2 * t + h + 1))
                                dve.tensor_tensor(oh[h][:, :, :], spread(c.iota[:, :].unsqueeze(1), [P, HK, P]),
                                                  spread(dl[:, h * HK:(h + 1) * HK].unsqueeze(2), [P, HK, P]),
                                                  ALU.is_equal).then_inc(onehot_ready, 1)
                            ch.link(dve.tensor_scalar(run[:, 0, :], top[:, ds(b, 1), :].rearrange("p a h -> p (a h)"), 1.0, None, ALU.mult))
                            for h in range(2):
                                dve.wait_ge(pen_ready, after(2 * t + h + 1))
                                for n in range(H):
                                    dve.wait_ge(bc_ready, after(t * 2 * H + h * H + n + 1))
                                    alone(c, dve)
                                    dve.tensor_tensor_reduce(out=junk[:, :], in0=bc[n % 2][:, :], in1=pen[h][:, :], scale=1.0,
                                                             scalar=run[:, h, n:n + 1], op0=ALU.add, op1=ALU.max,
                                                             accum_out=run[:, h + 1, n:n + 1]).then_inc(bc_used, 1)
                                    dve.wait_ge(bc_used, after(t * 2 * H + h * H + n + 1))
                            ch.link(dve.tensor_scalar(top[:, ds(b, 1), :].rearrange("p a h -> p (a h)"), run[:, 2, :], 1.0, None, ALU.mult))
                            a_b = ad[:, ds(b, 1), H:2 * H].rearrange("p a h -> p (a h)")
                            dve.tensor_scalar(adm[:, 0, 0:H], a_b, 1.0, None, ALU.mult)
                            dve.tensor_tensor(adm[:, 0, H:], run[:, 2, :], a_b, ALU.add)
                            ch.link(dve.tensor_tensor(adm[:, 1, H:], run[:, 0, :], a_b, ALU.add))
                            dve.scalar_tensor_tensor(adm[:, 0, H:], adm[:, 0, H:], NEG_SLOPE, adm[:, 0, H:], ALU.mult, ALU.max).then_inc(top_ready, 1)
                            ch.link(dve.scalar_tensor_tensor(adm[:, 1, H:], adm[:, 1, H:], NEG_SLOPE, adm[:, 1, H:], ALU.mult, ALU.max))
                            dve.tensor_tensor(fade[:, 0, :], adm[:, 1, H:], adm[:, 0, H:], ALU.subtract).then_inc(fade_z, 1)
                            for h in range(2):
                                dve.wait_ge(ade_ready, after(2 * t + h + 1))
                                dve.wait_ge(gathered[u][h], (i + 1) * 16 * HK)
                                ch.link(dve.tensor_tensor(zz[h][:, :, :], rows[u][:, h * HK:(h + 1) * HK, D:], ade[h][:, :, 0:H], ALU.add))
                                ch.link(dve.scalar_tensor_tensor(zz[h][:, :, :], zz[h][:, :, :], NEG_SLOPE, zz[h][:, :, :], ALU.mult, ALU.max))
                                ch.link(dve.tensor_tensor(zz[h][:, :, :], zz[h][:, :, :], ade[h][:, :, H:], ALU.subtract))
                                dve.tensor_scalar(zz[h][:, :, :], zz[h][:, :, :], 0.0, None, ALU.min).then_inc(z_ready, 1)
                            for h in range(2):
                                dve.wait_ge(w_ready, after(2 * t + h + 1))
                                dve.tensor_tensor(msg[h][:, :, :, 0:HD],
                                                  rows[u][:, h * HK:(h + 1) * HK, 0:D].rearrange("p k (h d) -> p k h d", h=H),
                                                  spread(msg[h][:, :, :, HD:], [P, HK, H, HD]), ALU.mult).then_inc(msg_ready, 1)
                            dve.wait_ge(main_done, after(2 * t + 4))
                            dve.wait_ge(fade_ready, after(t + 1))
                            for n in range(H):
                                a_n = c.acc[:, ds(b, 1), n * A:(n + 1) * A].rearrange("p a d -> p (a d)")
                                last = dve.scalar_tensor_tensor(a_n, a_n, fade[:, 1, n:n + 1], accp[:, n * A:(n + 1) * A], ALU.mult, ALU.add)
                            last.then_inc(acc_added, 1)
                            ch.end()
                            dve.reg_add(r, r, 1)
                        dve.wait_ge(msg_ready, after(dve.snap(r) * 2))
                        dve.sem_inc(rows_free, 1)
                dve.wait_ge(acc_added, after(dve.snap(r)))
                alone(c, dve)
                fin = Chain(dve, cleared)
                fin.n = 1
                weigh(c, fin, dve)


def aggregate(c, tab):
    nc, z = c.nc, c.z
    K, HK, NR, D, T = z.K, z.HK, z.NR, z.D, z.T
    c.phase = "aggregate"
    with ExitStack() as ctx:
        s = lambda n: c.sem(ctx, n)
        rows = [c.sb(ctx, f"rows{u}", [P, K, D]) for u in range(NR)]
        idx = [c.sb(ctx, f"idx{u}", [P, K], I32) for u in range(NR)]
        dl = [c.sb(ctx, f"dl{u}", [P, K]) for u in range(2)]
        oh = [[c.sb(ctx, f"oh{u}{h}", [P, HK, P]) for h in range(2)] for u in range(2)]
        accp = c.ps(ctx, "accp", [P, 512])
        gathered = [[c.pool_dma_sem(ctx, f"gathered{u}")] for u in range(NR)]
        names = ("idx_ready", "rows_free", "dve_step", "onehot_ready", "main_done", "acc_added")
        idx_ready, rows_free, dve_step, onehot_ready, main_done, acc_added = (s(n) for n in names)
        block = c.block(ctx)

        @block.gpsimd
        def _(pool):
            gather_rows(c, pool, tab, idx, rows, idx_ready, rows_free, gathered)

        @block.scalar
        def _(act):
            for u in range(NR):
                copy_indices(c, act, u, idx, u).then_inc(idx_ready, 1)
            with act.Fori(0, z.NB // NR) as i:
                for u in range(NR):
                    act.wait_ge(gathered[u][0], (i + 1) * 16 * K)
                    alone(c, act)
                    copy_indices(c, act, NR * (i + 1) + u, idx, u).then_inc(idx_ready, 1)

        @block.tensor
        def _(pe):
            pe.sem_inc(main_done, 2)
            r = pe.alloc_register(f"{c.phase}_pairs")
            pe.reg_mov(r, 0)
            pe.sem_inc(rows_free, NR)
            with pe.Fori(0, z.NB // NR) as i:
                for u in range(NR):
                    lo, hi = load_span(pe, c, NR * i + u)
                    with pe.Fori(lo, hi) as b:
                        t = pe.snap(r)
                        pe.wait_ge(acc_added, after(t))
                        for h in range(2):
                            pe.wait_ge(onehot_ready, after(2 * t + h + 1))
                            pe.wait_ge(gathered[u][0], (i + 1) * 16 * K)
                            for k in range(HK):
                                last = pe.matmul(accp[:, 0:D], oh[u % 2][h][:, k, :], rows[u][:, h * HK + k, :],
                                                 start=(h == 0 and k == 0), stop=(h == 1 and k == HK - 1))
                            last.then_inc(main_done, 1)
                        pe.reg_add(r, r, 1)
                    pe.wait_ge(main_done, after(pe.snap(r) * 2 + 2))
                    pe.sem_inc(rows_free, 1)

        @block.vector
        def _(dve):
            r = dve.alloc_register(f"{c.phase}_pairs")
            dve.reg_mov(r, 0)
            last_b = dve.alloc_register(f"{c.phase}_last_block")
            dve.reg_mov(last_b, 0)
            used = [dve.alloc_register(f"{c.phase}_used{u}") for u in range(2)]
            for u in range(2):
                dve.reg_mov(used[u], 0)

            def take(b):
                a_b = c.acc[:, ds(b, 1), 0:D].rearrange("p a d -> p (a d)")
                return dve.tensor_tensor(a_b, a_b, accp[:, 0:D], ALU.add)

            with dve.Fori(0, z.NB // NR) as i:
                for u in range(NR):
                    sc = NR * i + u
                    lo, hi = load_span(dve, c, sc)
                    with dve.Fori(lo, hi) as b:
                        t = dve.snap(r)
                        w = dve.snap(used[u % 2])
                        dve.wait_ge(onehot_ready, after(2 * t))
                        alone(c, dve)
                        dve.tensor_scalar(dl[u % 2][:, :], c.dst_all[:, ds(sc * K, K)], c.base[:, ds(b, 1)], None,
                                          ALU.subtract).then_inc(dve_step, 1)
                        dve.wait_ge(dve_step, after(t + 1))
                        for h in range(2):
                            dve.wait_ge(main_done, after(2 * w + h + 1))
                            dve.tensor_tensor(oh[u % 2][h][:, :, :], spread(c.iota[:, :].unsqueeze(1), [P, HK, P]),
                                              spread(dl[u % 2][:, h * HK:(h + 1) * HK].unsqueeze(2), [P, HK, P]),
                                              ALU.is_equal).then_inc(onehot_ready, 1)
                        with dve.If_ne(r, 0):
                            dve.wait_ge(main_done, after(2 * t + 2))
                            take(dve.snap(last_b, min_val=0, max_val=T - 1)).then_inc(acc_added, 1)
                        dve.reg_add(r, r, 1)
                        dve.reg_mov(used[u % 2], r)
                        dve.reg_mov(last_b, b)
            dve.wait_ge(main_done, after(dve.snap(r) * 2 + 2))
            take(dve.snap(last_b, min_val=0, max_val=T - 1))


def combine(c, gate, gate_b, xt_all=None, slot_rows=None):
    conv = xt_all is not None
    nc, z = c.nc, c.z
    G, KC, D, X, H, HD, A, W = z.G, z.KC, z.D, z.X, z.H, z.HD, z.A, z.W
    NN = 1 if conv else 2
    c.phase = "combine_sums" if conv else "combine_attention"
    with ExitStack() as ctx:
        s = lambda n: c.sem(ctx, n)
        stats = c.sb(ctx, "stats", [P, G, 6])
        mv = c.sb(ctx, "mv", [P, G, 2])
        sd = c.sb(ctx, "sd", [P, G])
        rstd = c.sb(ctx, "rstd", [P, G])
        xn = c.sb(ctx, "xn", [P, G, D])
        xt = c.sb(ctx, "xt", [P, G, KC, P])
        lg = c.sb(ctx, "lg", [P, G, X])
        red = c.sb(ctx, "red", [P, G])
        gt = c.sb(ctx, "gt", [P, G, X, X])
        eq = c.sb(ctx, "eq", [P, G, X, X])
        gw = c.sb(ctx, "gw", [P, KC, X])
        gb = c.sb(ctx, "gb", [P, X])
        if not conv:
            slotted = [c.sb(ctx, f"slotted{m}", [P, G, z.R]) for m in range(2)]
            xm = slotted[0]
            pad = c.sb(ctx, "pad", [P, z.U, z.R])
            chosen = c.sb(ctx, "chosen", [P, G, 2, X])
            part = c.sb(ctx, "part", [P, G, 2, X])
            either = c.sb(ctx, "either", [P, G, X], BF16)
            slot = c.sb(ctx, "slot", [P, G, X])
            to = c.sb(ctx, "to", [P, G, 2], I32)
            to_f = c.sb(ctx, "to_f", [P, G, 2])
            filled = c.sb(ctx, "filled_to", [P, X])
            count = c.sb(ctx, "count", [P, X])
            pos = c.ps(ctx, "pos", [P, G + 1, X])
        else:
            xm = xn
        tp = [c.ps(ctx, f"tp{i}", [P, KC, P]) for i in range(2)]
        lgp = c.ps(ctx, "lgp", [P, G, X])
        names = ("dve_step", "var_ready", "sd_ready", "xn_ready", "turned", "xt_ready", "lg_ready", "lg_used", "e_ready", "w_in")
        dve_step, var_ready, sd_ready, xn_ready, turned, xt_ready, lg_ready, lg_used, e_ready, w_in = (s(n) for n in names)
        if conv:
            xt_out = s("xt_out")
        else:
            names = ("either_ready", "pos_ready", "pos_used", "to_ready", "copied", "slotted_free", "pad_zero", "pad_ready", "counted", "padded")
            either_ready, pos_ready, pos_used, to_ready, copied, slotted_free, pad_zero, pad_ready, counted, padded = (s(n) for n in names)
            scattered = c.pool_dma_sem(ctx, "scattered")
        block = c.block(ctx)
        NW = 2

        @block.sync
        def _(sp):
            sp.dma_start(gw[:, :, :], gate.rearrange("(k p) e -> p k e", p=P)).then_inc(w_in, 16)
            sp.dma_start(gb[:, :], gate_b.rearrange("(o e) -> o e", o=1).broadcast_to([P, X])).then_inc(w_in, 16)
            sp.wait_ge(w_in, after(16 * NW))
            if not conv:
                sp.wait_ge(pad_ready, after(1))
                sp.wait_ge(counted, after(1))
                with sp.Fori(0, X) as e:
                    count = sp.value_load(c.counts[0:1, ds(e, 1)], min_val=0, max_val=z.T * P)
                    sp.dma_start(slot_rows[ds(e * z.S + count, z.US), :].rearrange("(t p) d -> p t d", p=P), pad[:, :, :]).then_inc(padded, 16)
                sp.wait_ge(padded, after(16 * X))

        @block.tensor
        def _(pe):
            pe.wait_ge(w_in, after(16 * NW))
            with pe.Fori(0, z.NG) as g:
                pe.wait_ge(xn_ready, after(g + 1))
                for j in range(G):
                    pe.wait_ge(xt_ready, after(g * G + max(j - 1, 0)))
                    for k in range(KC):
                        last = pe.transpose(tp[j % 2][:, k, :], xm[:, j, k * P:(k + 1) * P], c.ident[:, :])
                    last.then_inc(turned, 1)
                pe.wait_ge(lg_used, after(g))
                for j in range(G):
                    pe.wait_ge(xt_ready, after(g * G + j + 1))
                    for k in range(KC):
                        last = pe.matmul(lgp[:, j, :], xt[:, j, k, :], gw[:, k, :], start=(k == 0), stop=(k == KC - 1))
                last.then_inc(lg_ready, 1)
                if not conv:
                    pe.wait_ge(either_ready, after(g + 2))
                    pe.wait_ge(pos_used, after(g))
                    for j in range(G + 1):
                        for i in range(min(j, G)):
                            last = pe.matmul(pos[:, j, :], c.ones_b[:, :], either[:, i, :], start=(i == 0), stop=(i == G - 1))
                        if j < G:
                            last = pe.matmul(pos[:, j, :], c.before[:, :], either[:, j, :], start=(j == 0), stop=True)
                    last.then_inc(pos_ready, 1)

        @block.scalar
        def _(act):
            with act.Fori(0, z.NG) as g:
                for n in range(NN):
                    act.wait_ge(var_ready, after(g * NN + n + 1))
                    act.activation(sd[:, :], mv[:, :, 1], ACT.Sqrt, bias=c.eps[:, 0:1]).then_inc(sd_ready, 1)
                act.wait_ge(lg_ready, after(g))
                if conv:
                    act.wait_ge(xt_out, after(g))
                for j in range(G):
                    act.wait_ge(turned, after(g * G + j + 1))
                    act.activation(xt[:, j, :, :], tp[j % 2][:, :, :], ACT.Copy).then_inc(xt_ready, 1)
                act.wait_ge(lg_used, after(g + 1))
                act.activation(lg[:, :, :], lg[:, :, :], ACT.Exp).then_inc(e_ready, 1)
                if not conv:
                    act.activation(slotted[1][:, :, 0:D], xm[:, :, 0:D], ACT.Copy).then_inc(copied, 1)

        @block.gpsimd
        def _(pool):
            if not conv:
                pool.memset(pad[:, :, :], 0.0).then_inc(pad_zero, 1)
            with pool.Fori(0, z.NG) as g:
                if conv:
                    pool.wait_ge(xt_ready, after((g + 1) * G))
                    alone(c, pool)
                    for k in range(KC):
                        last = pool.tensor_copy(xt_all[:, k, ds(g * W, W)].rearrange("p (t n) -> p t n", n=P), xt[:, :, k, :])
                    last.then_inc(xt_out, 1)
                else:
                    pool.wait_ge(to_ready, after(g + 1))
                    pool.wait_ge(copied, after(g + 1))
                    alone(c, pool)
                    for j in range(G):
                        for m in range(2):
                            pool.indirect_dma_start(slot_rows, bass.IndirectOffsetOnAxis(ap=to[:, j, m:m + 1], axis=0),
                                                    slotted[m][:, j, :], None).then_inc(scattered, 16)
                    pool.wait_ge(scattered, (g + 1) * (G * 2 * 16))
                    pool.sem_inc(slotted_free, 1)

        @block.vector
        def _(dve):
            if not conv:
                dve.tensor_copy(filled[:, :], c.home[:, :]).then_inc(either_ready, 1)
                dve.wait_ge(pad_zero, after(1))
                for t in range(z.U):
                    last = dve.tensor_scalar(pad[:, t, D:D + 1], c.node[:, t:t + 1], float(2 * z.T * P), None, ALU.add)
                last.then_inc(pad_ready, 1)
            dve.wait_ge(w_in, after(16 * NW))
            ch = Chain(dve, dve_step, 8 if conv else 22)
            with dve.Fori(0, z.NG) as g:
                ch.begin(g)
                group = c.res[:, ds(g * G, G), :]
                dve.wait_ge(turned, after(g * G))
                if conv:
                    alone(c, dve)
                    ch.link(dve.scalar_tensor_tensor(group, c.acc[:, ds(g * G, G), 0:D], 0.0, group, ALU.max, ALU.add))
                else:
                    ch.link(normalise(c, dve, ch, g, stats, mv, sd, rstd, xn, var_ready, sd_ready, g * NN + 1))
                    ch.link(dve.tensor_tensor(group, group, xn[:, :, :], ALU.add))
                    for j in range(G):
                        row = c.res[:, ds(g * G + j, 1), :].rearrange("p a (h d) -> p (a h) d", h=H)
                        att = c.acc[:, ds(g * G + j, 1), :].rearrange("p a (h d) -> p (a h) d", h=H)[:, :, 0:HD]
                        last = dve.tensor_tensor(row, row, att, ALU.add)
                    ch.link(last)
                    dve.wait_ge(slotted_free, after(g))
                normalise(c, dve, ch, g, stats, mv, sd, rstd, xm, var_ready, sd_ready, g * NN + NN).then_inc(xn_ready, 1)
                dve.wait_ge(lg_ready, after(g + 1))
                ch.link(dve.tensor_tensor(lg[:, :, :], lgp[:, :, :], spread(gb[:, :].unsqueeze(1), [P, G, X]), ALU.add))
                ch.link(dve.tensor_reduce(red[:, :], lg[:, :, :], AX.X, ALU.max))
                dve.tensor_tensor(lg[:, :, :], lg[:, :, :], spread(red[:, :].unsqueeze(2), [P, G, X]), ALU.subtract).then_inc(lg_used, 1)
                dve.wait_ge(e_ready, after(g + 1))
                ch.link(dve.tensor_reduce(red[:, :], lg[:, :, :], AX.X, ALU.add))
                ch.link(dve.reciprocal(red[:, :], red[:, :]))
                gates = c.gates[:, ds(g * G, G), :]
                probs = gates if conv else lg[:, :, :]
                ch.link(dve.tensor_tensor(probs, lg[:, :, :], spread(red[:, :].unsqueeze(2), [P, G, X]), ALU.mult))
                if not conv:
                    mine = spread(lg[:, :, :].unsqueeze(3), [P, G, X, X])
                    other = spread(lg[:, :, :].unsqueeze(2), [P, G, X, X])
                    dve.tensor_tensor(gt[:, :, :, :], other, mine, ALU.is_gt)
                    ch.link(dve.tensor_tensor(eq[:, :, :, :], other, mine, ALU.is_equal))
                    tri = spread(c.tri[:, :, :].rearrange("p i j -> p (i j)").unsqueeze(1), [P, G, X * X])
                    ch.link(dve.tensor_tensor(eq[:, :, :, :].rearrange("p t i j -> p t (i j)"),
                                              eq[:, :, :, :].rearrange("p t i j -> p t (i j)"), tri, ALU.mult))
                    ch.link(dve.tensor_tensor(gt[:, :, :, :], gt[:, :, :, :], eq[:, :, :, :], ALU.add))
                    ch.link(dve.tensor_reduce(eq[:, :, :, 0], gt[:, :, :, :], AX.X, ALU.add))
                    rank = eq[:, :, :, 0]
                    dve.tensor_scalar(either[:, :, :], rank, 1.5, None, ALU.is_lt).then_inc(either_ready, 1)
                    dve.tensor_scalar(chosen[:, :, 0, :], rank, 0.5, None, ALU.is_lt)
                    ch.link(dve.tensor_scalar(chosen[:, :, 1, :], rank, 1.0, None, ALU.is_equal))
                    dve.scalar_tensor_tensor(gates, rank, 1.5, lg[:, :, :], ALU.is_lt, ALU.mult)
                    ch.link(dve.tensor_tensor(part[:, :, :, :], chosen[:, :, :, :], spread(lg[:, :, :].unsqueeze(2), [P, G, 2, X]), ALU.mult))
                    for m in range(2):
                        last = dve.tensor_reduce(slotted[m][:, :, D + 1], part[:, :, m, :], AX.X, ALU.add)
                        dve.tensor_scalar(slotted[m][:, :, D], c.node[:, ds(g * G, G)], float(m * z.T * P), None, ALU.add)
                    ch.link(last)
                    dve.wait_ge(pos_ready, after(g + 1))
                    ch.link(dve.tensor_tensor(slot[:, :, :], pos[:, 0:G, :], spread(filled[:, :].unsqueeze(1), [P, G, X]), ALU.add))
                    dve.tensor_tensor(filled[:, :], filled[:, :], pos[:, G, :], ALU.add).then_inc(pos_used, 1)
                    ch.link(dve.tensor_tensor(part[:, :, :, :], chosen[:, :, :, :], spread(slot[:, :, :].unsqueeze(2), [P, G, 2, X]), ALU.mult))
                    ch.link(dve.tensor_reduce(to_f[:, :, :], part[:, :, :, :], AX.X, ALU.add))
                    dve.tensor_copy(to[:, :, :], to_f[:, :, :]).then_inc(to_ready, 1)
                    dve.wait_ge(pos_used, after(g + 1))
                    dve.wait_ge(to_ready, after(g + 1))
                ch.end()
            if not conv:
                fin = Chain(dve, dve_step)
                fin.n = ch.per * z.NG
                fin.link(dve.tensor_tensor(count[:, :], filled[:, :], c.home[:, :], ALU.subtract))
                fin.link(dve.tensor_scalar(c.units[:, :], count[0:1, :], float(z.US - 1), float(z.US), ALU.add, ALU.max))
                dve.tensor_scalar(c.units[:, :], c.units[:, :], z.US.bit_length() - 1, None, ALU.arith_shift_right)
                dve.tensor_copy(c.counts[:, :], count[0:1, :]).then_inc(counted, 1)


def units_of(eng, c, e):
    return eng.value_load(c.units[0:1, ds(e, 1)], min_val=0, max_val=c.z.NU)


def experts_gelu(c, slot_rows, results, w1, b1, w2):
    nc, z = c.nc, c.z
    KC, HC, D, F, X, U, US, S = z.KC, z.HC, z.D, z.F, z.X, z.U, z.US, z.S
    c.phase = "experts_gelu"
    with ExitStack() as ctx:
        s = lambda n: c.sem(ctx, n)
        w1s = [c.sb(ctx, f"w1s{u}", [P, KC, F]) for u in range(2)]
        w2s = [c.sb(ctx, f"w2s{u}", [P, HC, D]) for u in range(2)]
        b1s = [c.sb(ctx, f"b1s{u}", [P, HC]) for u in range(2)]
        rows = c.sb(ctx, "rows", [P, U, z.R])
        to = c.sb(ctx, "to", [P, U], I32)
        gate = c.sb(ctx, "gate", [P, U])
        xt = c.sb(ctx, "xt", [P, KC, US])
        ht = c.sb(ctx, "ht", [P, HC, US])
        y = c.sb(ctx, "y", [P, U, D])
        tp = [c.ps(ctx, f"tp{i}", [P, KC, P]) for i in range(2)]
        up = [c.ps(ctx, f"up{i}", [P, US]) for i in range(HC)]
        yp = [c.ps(ctx, f"yp{i}", [P, D]) for i in range(2)]
        w_in = [s(f"w_in{u}") for u in range(2)]
        names = ("rows_in", "info_ready", "turned", "xt_ready", "up_ready", "h_ready", "y_ready", "y_scaled", "to_free")
        rows_in, info_ready, turned, xt_ready, up_ready, h_ready, y_ready, y_scaled, to_free = (s(n) for n in names)
        scattered = c.pool_dma_sem(ctx, "scattered")
        block = c.block(ctx)

        def counter(eng):
            r = eng.alloc_register(f"{c.phase}_units")
            eng.reg_mov(r, 0)
            return r

        def load(eng, e, u):
            eng.dma_start(w1s[u][:, :, :], w1[ds(e, 1), :, :].rearrange("o (k p) f -> p (o k) f", p=P)).then_inc(w_in[u], 16)
            eng.dma_start(w2s[u][:, :, :], w2[ds(e, 1), :, :].rearrange("o (k p) d -> p (o k) d", p=P)).then_inc(w_in[u], 16)
            eng.dma_start(b1s[u][:, :], b1[ds(e, 1), :].rearrange("o (k p) -> p (o k)", p=P),
                          allow_slow_non_contiguous=True).then_inc(w_in[u], 16)

        @block.sync
        def _(sp):
            load(sp, 0, 0)
            load(sp, 1, 1)
            r = counter(sp)
            with sp.Fori(0, X) as e:
                units = units_of(sp, c, e)
                with sp.Fori(0, units) as m:
                    t = sp.snap(r)
                    sp.wait_ge(turned, after(t * U))
                    alone(c, sp)
                    sp.wait_ge(info_ready, after(t))
                    sp.dma_start(rows[:, :, :], slot_rows[ds(e * S + m * US, US), :].rearrange("(t p) d -> p t d", p=P)).then_inc(rows_in, 16)
                    sp.reg_add(r, r, 1)
            sp.wait_ge(rows_in, after(sp.snap(r) * 16))
            alone(c, sp)

        @block.gpsimd
        def _(pool):
            r = counter(pool)
            with pool.Fori(0, X) as e:
                units = units_of(pool, c, e)
                with pool.Fori(0, units) as m:
                    t = pool.snap(r)
                    for j in range(U):
                        pool.wait_ge(y_scaled, after(t * U + j + 1))
                        alone(c, pool)
                        pool.indirect_dma_start(results, bass.IndirectOffsetOnAxis(ap=to[:, j:j + 1], axis=0),
                                                y[:, j, :], None).then_inc(scattered, 16)
                    pool.wait_ge(scattered, (t + 1) * (16 * U))
                    pool.sem_inc(to_free, 1)
                    pool.reg_add(r, r, 1)

        @block.tensor
        def _(pe):
            r = counter(pe)
            with pe.Fori(0, X // 2) as o:
                for u in range(2):
                    units = units_of(pe, c, 2 * o + u)
                    pe.wait_ge(w_in[u], after((o + 1) * 48))
                    alone(c, pe)
                    with pe.Fori(0, units) as m:
                        t = pe.snap(r)
                        pe.wait_ge(rows_in, after((t + 1) * 16))
                        for j in range(U):
                            pe.wait_ge(xt_ready, after(t * U + max(j - 1, 0)))
                            for k in range(KC):
                                last = pe.transpose(tp[j % 2][:, k, :], rows[:, j, k * P:(k + 1) * P], c.ident[:, :])
                            last.then_inc(turned, 1)
                        pe.wait_ge(xt_ready, after((t + 1) * U))
                        pe.wait_ge(h_ready, after(t * HC))
                        for hc in range(HC):
                            for k in range(KC):
                                last = pe.matmul(up[hc][:, :], w1s[u][:, k, hc * P:(hc + 1) * P], xt[:, k, :],
                                                 start=(k == 0), stop=(k == KC - 1))
                            last.then_inc(up_ready, 1)
                        for j in range(U):
                            pe.wait_ge(y_scaled, after(t * U + max(j - 1, 0)))
                            for hc in range(HC):
                                if j == 0:
                                    pe.wait_ge(h_ready, after(t * HC + hc + 1))
                                last = pe.matmul(yp[j % 2][:, :], ht[:, hc, j * P:(j + 1) * P], w2s[u][:, hc, :],
                                                 start=(hc == 0), stop=(hc == HC - 1))
                            last.then_inc(y_ready, 1)
                        pe.reg_add(r, r, 1)

        @block.scalar
        def _(act):
            r = counter(act)

            def expert(e, o, u):
                units = units_of(act, c, e)
                act.wait_ge(w_in[u], after((o + 1) * 48))
                alone(c, act)
                with act.Fori(0, units) as m:
                    t = act.snap(r)
                    act.wait_ge(up_ready, after(t * HC))
                    for j in range(U):
                        act.wait_ge(turned, after(t * U + j + 1))
                        act.activation(xt[:, :, j * P:(j + 1) * P], tp[j % 2][:, :, :], ACT.Copy).then_inc(xt_ready, 1)
                    act.wait_ge(y_ready, after(t * U))
                    for hc in range(HC):
                        act.wait_ge(up_ready, after(t * HC + hc + 1))
                        act.activation(ht[:, hc, :], up[hc][:, :], ACT.Gelu, bias=b1s[u][:, hc:hc + 1]).then_inc(h_ready, 1)
                    act.reg_add(r, r, 1)

            with act.Fori(0, X // 2 - 1) as o:
                for u in range(2):
                    expert(2 * o + u, o, u)
                    act.wait_ge(y_ready, after(act.snap(r) * U))
                    alone(c, act)
                    load(act, 2 * o + 2 + u, u)
            for u in range(2):
                expert(X - 2 + u, X // 2 - 1, u)

        @block.vector
        def _(dve):
            r = counter(dve)
            with dve.Fori(0, X) as e:
                units = units_of(dve, c, e)
                with dve.Fori(0, units) as m:
                    t = dve.snap(r)
                    dve.wait_ge(rows_in, after((t + 1) * 16))
                    dve.wait_ge(to_free, after(t))
                    dve.tensor_copy(to[:, :], rows[:, :, D])
                    dve.tensor_copy(gate[:, :], rows[:, :, D + 1]).then_inc(info_ready, 1)
                    dve.wait_ge(info_ready, after(t + 1))
                    for j in range(U):
                        dve.wait_ge(y_ready, after(t * U + j + 1))
                        dve.tensor_scalar(y[:, j, :], yp[j % 2][:, :], gate[:, j:j + 1], None, ALU.mult).then_inc(y_scaled, 1)
                    dve.reg_add(r, r, 1)


class Biases:

    def __init__(self, c, ctx, bp):
        s = lambda n: c.sem(ctx, n)
        self.c, self.bp = c, bp
        self.gates = c.sb(ctx, "group_gates", [P, c.z.G, c.z.X])
        self.turned_gates = c.sb(ctx, "turned_gates", [c.z.X, c.z.G * P])
        self.biases = c.sb(ctx, "biases", [c.z.X, c.z.D])
        self.tp = [c.ps(ctx, f"gates_tp{h}", [P, 4 * P]) for h in range(2)]
        self.b_in, self.gates_ready, self.turned, self.gt_ready, self.mixed, self.taken = (
            s(n) for n in ("b_in", "gates_ready", "gates_turned", "gt_ready", "mixed", "taken"))
        self.halves = [range(0, 4), range(4, c.z.G)]

    def sync(self, sp, b, before=0):
        sp.dma_start(self.biases[:, :], b).then_inc(self.b_in, 16)
        sp.wait_ge(self.b_in, after(16 * (before + 1)))

    def scalar(self, act, g):
        c, G = self.c, self.c.z.G
        act.wait_ge(self.turned, after(g * 2))
        alone(c, act)
        act.activation(self.gates[:, :, :], c.gates[:, ds(g * G, G), :], ACT.Copy).then_inc(self.gates_ready, 1)
        act.wait_ge(self.mixed, after(g * G))
        for h, tiles in enumerate(self.halves):
            n = len(tiles) * P
            act.wait_ge(self.turned, after(g * 2 + h + 1))
            act.activation(self.turned_gates[:, tiles[0] * P:tiles[0] * P + n], self.tp[h][0:c.z.X, 0:n],
                           ACT.Copy).then_inc(self.gt_ready, 1)

    def tensor(self, pe, g):
        c, G = self.c, self.c.z.G
        pe.wait_ge(self.gates_ready, after(g + 1))
        pe.wait_ge(self.gt_ready, after(g * 2))
        for h, tiles in enumerate(self.halves):
            for j in tiles:
                at = (j - tiles[0]) * P
                last = pe.transpose(self.tp[h][0:c.z.X, at:at + P], self.gates[:, j, :], c.ident[:, :])
            last.then_inc(self.turned, 1)
        for h, tiles in enumerate(self.halves):
            pe.wait_ge(self.gt_ready, after(g * 2 + h + 1))
            for j in tiles:
                pe.wait_ge(self.taken, after(g * G + max(j - 1, 0)))
                pe.matmul(self.bp[j % 2][:, 0:c.z.D], self.turned_gates[:, j * P:(j + 1) * P], self.biases[:, :],
                          start=True, stop=True).then_inc(self.mixed, 1)

    def vector(self, dve, g):
        c, G = self.c, self.c.z.G
        for j in range(G):
            row = c.res[:, ds(g * G + j, 1), :].rearrange("p a d -> p (a d)")
            dve.wait_ge(self.mixed, after(g * G + j + 1))
            dve.tensor_tensor(row, row, self.bp[j % 2][:, 0:c.z.D], ALU.add).then_inc(self.taken, 1)


def collect(c, results, b2, w, m, tab):
    nc, z = c.nc, c.z
    G, D, KC = z.G, z.D, z.KC
    c.phase = "collect"
    with ExitStack() as ctx:
        s = lambda n: c.sem(ctx, n)
        both = c.sb(ctx, "both", [P, KC, 2 * D])
        y = [c.sb(ctx, f"y{n}", [P, G, D]) for n in range(2)]
        stats = c.sb(ctx, "stats", [P, G, 6])
        mv = c.sb(ctx, "mv", [P, G, 2])
        sd = c.sb(ctx, "sd", [P, G])
        rstd = c.sb(ctx, "rstd", [P, G])
        xn = c.sb(ctx, "xn", [P, G, D])
        xt = c.sb(ctx, "xt", [P, G, KC, P])
        sent = c.sb(ctx, "sent", [P, G, D])
        tp = [c.ps(ctx, f"tp{i}", [P, KC, P]) for i in range(2)]
        made = [c.ps(ctx, f"made{i}", [P, 2 * D]) for i in range(2)]
        bias = Biases(c, ctx, [c.ps(ctx, f"bp{i}", [P, D]) for i in range(2)])
        y_in = [c.pool_dma_sem(ctx, f"y_in{n}") for n in range(2)]
        names = ("y_used", "dve_step", "var_ready", "sd_ready", "xn_ready", "turned", "xt_ready", "made_ready", "copied", "stored")
        y_used, dve_step, var_ready, sd_ready, xn_ready, turned, xt_ready, made_ready, copied, stored = (s(n) for n in names)
        block = c.block(ctx)

        @block.gpsimd
        def _(pool):
            with pool.Fori(0, z.NG) as g:
                for n in range(2):
                    pool.wait_ge(y_used, after(g * 2 + n + 1))
                    alone(c, pool)
                    pool.dma_start(y[n][:, :, :], results[ds(g * z.W + n * z.T * P, z.W), :].rearrange("(t p) d -> p t d", p=P)
                                   ).then_inc(y_in[n], 16)

        @block.sync
        def _(sp):
            for n, a in enumerate((w, m)):
                sp.dma_start(both[:, :, n * D:(n + 1) * D], a.rearrange("(k p) d -> p k d", p=P)).then_inc(bias.b_in, 16)
            bias.sync(sp, b2, 2)
            with sp.Fori(0, z.NG) as g:
                sp.wait_ge(copied, after((g + 1) * G))
                sp.dma_start(tab[ds(g * z.W, z.W), :].rearrange("(t p) d -> p t d", p=P), sent[:, :, :]).then_inc(stored, 16)
            sp.wait_ge(stored, after(z.NG * 16))

        @block.tensor
        def _(pe):
            def group(g, more):
                pe.wait_ge(xn_ready, after(g + 1))
                for j in range(G):
                    pe.wait_ge(xt_ready, after(g * G + max(j - 1, 0)))
                    for k in range(KC):
                        last = pe.transpose(tp[j % 2][:, k, :], xn[:, j, k * P:(k + 1) * P], c.ident[:, :])
                    last.then_inc(turned, 1)
                if more:
                    bias.tensor(pe, g + 1)
                for j in range(G):
                    pe.wait_ge(xt_ready, after(g * G + j + 1))
                    pe.wait_ge(copied, after(g * G + max(j - 1, 0)))
                    for k in range(KC):
                        last = pe.matmul(made[j % 2][:, :], xt[:, j, k, :], both[:, k, :], start=(k == 0), stop=(k == KC - 1))
                    last.then_inc(made_ready, 1)

            pe.wait_ge(bias.b_in, after(48))
            bias.tensor(pe, 0)
            with pe.Fori(0, z.NG - 1) as g:
                group(g, True)
            group(z.NG - 1, False)

        @block.scalar
        def _(act):
            def group(g, more):
                act.wait_ge(var_ready, after(g + 1))
                act.activation(sd[:, :], mv[:, :, 1], ACT.Sqrt, bias=c.eps[:, 0:1]).then_inc(sd_ready, 1)
                act.wait_ge(made_ready, after(g * G))
                for j in range(G):
                    act.wait_ge(turned, after(g * G + j + 1))
                    act.activation(xt[:, j, :, :], tp[j % 2][:, :, :], ACT.Copy).then_inc(xt_ready, 1)
                if more:
                    bias.scalar(act, g + 1)
                act.wait_ge(stored, after(g * 16))
                alone(c, act)
                for j in range(G):
                    act.wait_ge(made_ready, after(g * G + j + 1))
                    alone(c, act)
                    act.activation(c.acc[:, ds(g * G + j, 1), 0:D].rearrange("p a d -> p (a d)"), made[j % 2][:, 0:D], ACT.Copy)
                    act.activation(sent[:, j, :], made[j % 2][:, D:], ACT.Copy).then_inc(copied, 1)

            bias.scalar(act, 0)
            with act.Fori(0, z.NG - 1) as g:
                group(g, True)
            group(z.NG - 1, False)

        @block.vector
        def _(dve):
            dve.sem_inc(y_used, 2)
            ch = Chain(dve, dve_step, 2)
            with dve.Fori(0, z.NG) as g:
                ch.begin(g)
                rows = c.res[:, ds(g * G, G), :]
                bias.vector(dve, g)
                dve.wait_ge(bias.taken, after((g + 1) * G))
                for n in range(2):
                    dve.wait_ge(y_in[n], (g + 1) * 16)
                    dve.tensor_tensor(rows, rows, y[n][:, :, :], ALU.add).then_inc(y_used, 1)
                    dve.wait_ge(y_used, after(g * 2 + n + 3))
                dve.wait_ge(turned, after(g * G))
                normalise(c, dve, ch, g, stats, mv, sd, rstd, xn, var_ready, sd_ready, g + 1).then_inc(xn_ready, 1)
                ch.end()


def experts_deep(c, xt_all, w1, w2, wo, bo, bn_out, out):
    nc, z = c.nc, c.z
    G, KC, D, X, W, HW, NG, F2 = z.G, z.KC, z.D, z.X, z.W, z.HW, z.NG, z.F2
    HC = F2 // P
    UP = 2 * HC
    c.phase = "experts_deep"
    with ExitStack() as ctx:
        s = lambda n: c.sem(ctx, n)
        w1s = [c.sb(ctx, f"w1s{u}", [P, KC, F2]) for u in range(2)]
        w2s = [c.sb(ctx, f"w2s{u}", [P, HC, F2]) for u in range(2)]
        wos = [c.sb(ctx, f"wos{u}", [P, HC, D]) for u in range(2)]
        aff = [c.sb(ctx, f"aff{u}", [P, 2, 2, HC]) for u in range(2)]
        hid = [c.sb(ctx, f"hid{n}", [P, HC, W]) for n in range(2)]
        up = [c.ps(ctx, f"up{i}", [P, 512]) for i in range(4)]
        yp = [c.ps(ctx, f"yp{i}", [P, 512]) for i in range(2)]
        bias = Biases(c, ctx, yp)
        w_in = [s(f"w_in{u}") for u in range(2)]
        up_ready, h_ready, y_ready, y_added, stored = (s(n) for n in ("up_ready", "h_ready", "y_ready", "y_added", "stored"))
        block = c.block(ctx)
        NL = 7

        @block.sync
        def _(sp):
            def load(e, u):
                for to, w in ((w1s, w1), (w2s, w2), (wos, wo)):
                    sp.dma_start(to[u][:, :, :], w[ds(e, 1), :, :].rearrange("o (k p) f -> p (o k) f", p=P)).then_inc(w_in[u], 16)
                for n in range(2):
                    for m in range(2):
                        sp.dma_start(aff[u][:, n, m, :], bn_out[n][m][ds(e, 1), :, :].rearrange("o p k -> p (o k)")).then_inc(w_in[u], 16)

            bias.sync(sp, bo)
            load(0, 0)
            load(1, 1)
            with sp.Fori(1, X // 2) as o:
                for u in range(2):
                    sp.wait_ge(y_ready, after((2 * o + u - 1) * NG * G))
                    load(2 * o + u, u)
            for u in range(2):
                sp.wait_ge(w_in[u], after(16 * NL * (X // 2)))
            sp.wait_ge(y_added, after(X * NG * G))
            sp.dma_start(out[0:(z.T - 1) * P, :].rearrange("(t p) d -> p t d", p=P), c.res[:, 0:z.T - 1, :]).then_inc(stored, 16)
            sp.dma_start(out[(z.T - 1) * P:z.N, :], c.res[0:z.LAST, z.T - 1, :]).then_inc(stored, 16)
            sp.wait_ge(stored, after(32))

        @block.tensor
        def _(pe):
            pe.wait_ge(bias.b_in, after(16))
            with pe.Fori(0, NG) as g:
                bias.tensor(pe, g)
            pe.wait_ge(bias.taken, after(z.T))
            with pe.Fori(0, X // 2) as o:
                for u in range(2):
                    pe.wait_ge(w_in[u], after((o + 1) * 16 * NL))
                    alone(c, pe)
                    with pe.Fori(0, NG) as g:
                        n = (2 * o + u) * NG + g
                        for layer in range(2):
                            for hc in range(HC):
                                for v in range(2):
                                    q = layer * UP + 2 * hc + v
                                    pe.wait_ge(h_ready, after(n * 2 * UP + (max(q - 3, 0) if layer == 0 else UP)))
                                    for k in range(KC):
                                        moving = xt_all[:, k, ds(g * W + v * HW, HW)] if layer == 0 else hid[0][:, k, v * HW:(v + 1) * HW]
                                        last = pe.matmul(up[q % 4][:, 0:HW], (w1s if layer == 0 else w2s)[u][:, k, hc * P:(hc + 1) * P],
                                                         moving, start=(k == 0), stop=(k == KC - 1))
                                    last.then_inc(up_ready, 1)
                        pe.wait_ge(h_ready, after((n + 1) * 2 * UP))
                        for j in range(G):
                            pe.wait_ge(y_added, after(n * G + max(j - 1, 0)))
                            for hc in range(HC):
                                last = pe.matmul(yp[j % 2][:, 0:D], hid[1][:, hc, j * P:(j + 1) * P], wos[u][:, hc, :],
                                                 start=(hc == 0), stop=(hc == HC - 1))
                            last.then_inc(y_ready, 1)

        @block.scalar
        def _(act):
            with act.Fori(0, NG) as g:
                bias.scalar(act, g)
            with act.Fori(0, X // 2) as o:
                for u in range(2):
                    act.wait_ge(w_in[u], after((o + 1) * 16 * NL))
                    with act.Fori(0, NG) as g:
                        n = (2 * o + u) * NG + g
                        act.wait_ge(y_ready, after(n * G))
                        for q in range(2 * UP):
                            layer, hc, v = q // UP, q % UP // 2, q % 2
                            act.wait_ge(up_ready, after(n * 2 * UP + q + 1))
                            act.activation(hid[layer][:, hc, v * HW:(v + 1) * HW], up[q % 4][:, 0:HW], ACT.Relu,
                                           scale=aff[u][:, layer, 0, hc:hc + 1], bias=aff[u][:, layer, 1, hc:hc + 1]).then_inc(h_ready, 1)

        @block.vector
        def _(dve):
            with dve.Fori(0, NG) as g:
                bias.vector(dve, g)
            dve.wait_ge(bias.taken, after(z.T))
            with dve.Fori(0, X) as e:
                with dve.Fori(0, NG) as g:
                    n = e * NG + g
                    for j in range(G):
                        row = c.res[:, ds(g * G + j, 1), :].rearrange("p a d -> p (a d)")
                        gate = c.gates[:, ds(g * G + j, 1), ds(e, 1)].rearrange("p a e -> p (a e)")
                        dve.wait_ge(y_ready, after(n * G + j + 1))
                        if j == 0:
                            dve.wait_ge(y_added, after(n * G))
                        dve.scalar_tensor_tensor(row, yp[j % 2][:, 0:D], gate, row, ALU.mult, ALU.add).then_inc(y_added, 1)


def gnn_experts(nc, a, out, phases=99):
    z = Shapes(a["x"], a["src"], a["L0_gnn_W"], a["L0_gnn_attn_src"], a["L0_gnn_pos_attn_src"],
               a["L0_ffn_W1"], a["L0_ffn_W2"], a["L1_ffn_Wr"], a["L1_ffn_v1"])
    c = Core(nc, z)
    dram = lambda name, shape, dt=F32: nc.dram_tensor(name, shape, dt, kind="Internal").ap()
    tab0 = dram("rows_attention", (z.T * P, z.D + z.H))
    scores = dram("scores", (z.T * P, 2 * z.H))
    slot_rows = dram("slot_rows", (z.X * z.S, z.R))
    results = dram("results", (2 * z.T * P + z.US, z.D))
    tab1 = dram("rows_sums", (z.T * P, z.D))
    c.span_d = dram("spans_dram", (z.NB, 2), I32)
    bn_out = [[dram(f"bn{n}{m}", (z.X, P, z.F2 // P)) for m in range(2)] for n in range(2)]
    with ExitStack() as ctx:
        c.pace = ctx.enter_context(nc.semaphore("pace"))
        c.res = c.sb(ctx, "res", [P, z.T, z.D])
        c.gates = c.sb(ctx, "gates", [P, z.T, z.X])
        c.ident = c.sb(ctx, "ident", [P, P])
        c.ident_b = c.sb(ctx, "ident_b", [P, P], BF16)
        c.wide = c.sb(ctx, "wide", [1, 1], I32)
        c.less_top = c.sb(ctx, "less_top", [P, 2])
        c.ones_b = c.sb(ctx, "ones_b", [P, P], BF16)
        c.before = c.sb(ctx, "before", [P, P], BF16)
        c.node = c.sb(ctx, "node", [P, z.T])
        c.home = c.sb(ctx, "home", [P, z.X])
        c.counts = c.sb(ctx, "counts", [1, z.X], I32)
        c.units = c.sb(ctx, "units", [1, z.X], I32)
        c.eps = c.sb(ctx, "eps", [P, 2])
        c.tri = c.sb(ctx, "tri", [P, z.X, z.X])
        c.sel = c.sb(ctx, "sel", [P, z.H, P])
        c.iota = c.sb(ctx, "iota", [P, P])
        c.base = c.sb(ctx, "base", [P, z.T])
        c.spans = c.sb(ctx, "spans", [1, 2 * z.NB], I32)
        c.src_all = c.sb(ctx, "src_all", [P, (z.NB + z.NR) * z.K], I32)
        c.dst_all = c.sb(ctx, "dst_all", [P, z.NB * z.K])
        c.wall = c.sb(ctx, "wall", [P, z.KC, z.D + 2 * z.H])
        bn_in = [[a[f"L1_ffn_{n}{i}"] for n in ("b", "g", "be", "m", "v")] for i in (1, 2)]
        prepare(c, a["x"], a["src"], a["dst"], a["L0_gnn_W"], a["L0_gnn_attn_src"], a["L0_gnn_attn_dst"],
                a["L0_gnn_pos_attn_src"], a["L0_gnn_pos_attn_dst"], bn_in, bn_out)
        if phases > 1:
            project(c, tab0, scores)
        with ExitStack() as inner:
            c.phase = "layer0"
            if phases > 2:
                c.factors = c.sb(inner, "factors", [P, z.T, 3, 2 * z.H], BF16)
                c.acc = c.sb(inner, "acc", [P, z.T, z.H * z.A])
                c.gathered = [c.pool_dma_sem(inner, f"gathered{u}") for u in range(z.NR)]
                bound_scores(c, scores)
                attend_bounded(c, tab0)
                attend(c, tab0, scores)
            if phases > 3:
                combine(c, a["L0_ffn_gate_w"], a["L0_ffn_gate_b"], slot_rows=slot_rows)
        if phases > 4:
            experts_gelu(c, slot_rows, results, a["L0_ffn_W1"], a["L0_ffn_b1"], a["L0_ffn_W2"])
        with ExitStack() as inner:
            c.phase = "layer1"
            if phases > 5:
                c.acc = c.sb(inner, "acc", [P, z.T, z.D])
                collect(c, results, a["L0_ffn_b2"], a["L1_gnn_W"], a["L1_gnn_M"], tab1)
            if phases > 6:
                aggregate(c, tab1)
            c.phase = "layer1"
            if phases > 7:
                xt_all = c.sb(inner, "xt_all", [P, z.KC, z.T * P])
                combine(c, a["L1_ffn_Wr"], a["L1_ffn_br"], xt_all=xt_all)
            if phases > 8:
                experts_deep(c, xt_all, a["L1_ffn_W1"], a["L1_ffn_W2"], a["L1_ffn_Wo"], a["L1_ffn_bo"], bn_out, out)


_INS = ["x", "src", "dst", "L0_gnn_W", "L0_gnn_attn_src", "L0_gnn_attn_dst", "L0_gnn_pos_attn_src", "L0_gnn_pos_attn_dst",
        "L0_ffn_gate_w", "L0_ffn_gate_b", "L0_ffn_W1", "L0_ffn_b1", "L0_ffn_W2", "L0_ffn_b2", "L1_gnn_W", "L1_gnn_M",
        "L1_ffn_Wr", "L1_ffn_br", "L1_ffn_W1", "L1_ffn_b1", "L1_ffn_g1", "L1_ffn_be1", "L1_ffn_m1", "L1_ffn_v1",
        "L1_ffn_W2", "L1_ffn_b2", "L1_ffn_g2", "L1_ffn_be2", "L1_ffn_m2", "L1_ffn_v2", "L1_ffn_Wo", "L1_ffn_bo"]


def kernel(**inputs):
    import numpy as np
    import concourse.bacc as bacc
    from concourse.bass_utils import run_bass_kernel_spmd

    nc = bacc.Bacc("TRN2", target_bir_lowering=False, num_devices=1)
    arrays, args = {}, {}
    for name in _INS:
        a = np.ascontiguousarray(inputs[name])
        arrays[f"in_{name}"] = a
        args[name] = nc.dram_tensor(f"in_{name}", a.shape, mybir.dt.from_np(a.dtype), kind="ExternalInput").ap()
    out = nc.dram_tensor("out", args["x"].shape, F32, kind="ExternalOutput").ap()
    gnn_experts(nc, args, out)
    r = run_bass_kernel_spmd(nc, [arrays], core_ids=[0])
    return r.results[0]["out"]
```
